# Optimizing a Trainium2 kernel written in Bass

```python
import numpy as np
import jax
import jax.numpy as jnp

def _softmax(x, axis=-1):
    return jax.nn.softmax(x, axis=axis)

def _gelu(x):
    return jax.nn.gelu(x, approximate=True)

def _silu(x):
    return jax.nn.silu(x)

def _sigmoid(x):
    return jax.nn.sigmoid(x)

def _layernorm(x, axis=-1, eps=1e-05):
    m = jnp.mean(x, axis=axis, keepdims=True)
    v = jnp.var(x, axis=axis, keepdims=True)
    return (x - m) / jnp.sqrt(v + eps)

def _scatter_add(tgt, idx, src, axis=0):
    return tgt.at[idx].add(src)

def _segment_sum(src, seg, n):
    return jax.ops.segment_sum(src, seg, n)
kernel_name = 'mk_seq_preln_d4_jaxref_r8_618250'

def setup_inputs(seed: int=0):
    np.random.seed(seed)
    _w = jnp.asarray

    def _L0_attn_setup():
        import jax, jax.numpy as jnp
        import numpy as np
        N_HEADS = 16
        N_KV_HEADS = 4
        HEAD_DIM = 128
        ROPE_THETA = 10000.0
        WINDOW = 128
        SOFTCAP = 50.0
        B, T, C = (2, 256, 256)
        G = N_HEADS // N_KV_HEADS

        def _sine_table(features, length, max_timescale):
            fraction = jnp.arange(0, features, 2, dtype=jnp.float32) / features
            inv_timescale = 1.0 / max_timescale ** fraction
            sinusoid = jnp.einsum('i,j->ij', jnp.arange(length), inv_timescale, precision=jax.lax.Precision.HIGHEST)
            sinusoid = jnp.concatenate([sinusoid, sinusoid], axis=-1)
            return (jnp.sin(sinusoid), jnp.cos(sinusoid))

        def _rotate_half(x):
            x1, x2 = jnp.split(x, 2, axis=-1)
            return jnp.concatenate([-x2, x1], axis=-1)

        def _attention(x, q_kernel, k_kernel, v_kernel, out_kernel):
            Bs, Ts, Cs = x.shape
            K, H, Gn = (N_KV_HEADS, HEAD_DIM, G)
            q = jnp.dot(x, q_kernel).reshape(Bs, Ts, K, Gn, H)
            k = jnp.dot(x, k_kernel).reshape(Bs, Ts, K, H)
            v = jnp.dot(x, v_kernel).reshape(Bs, Ts, K, H)
            sin, cos = _sine_table(H, Ts, ROPE_THETA)
            qcos = cos[None, :, None, None, :]
            qsin = sin[None, :, None, None, :]
            kcos = cos[None, :, None, :]
            ksin = sin[None, :, None, :]
            q = (q * qcos + _rotate_half(q) * qsin).astype(q.dtype)
            k = (k * kcos + _rotate_half(k) * ksin).astype(k.dtype)
            pos = jnp.arange(Ts)
            mask = (pos[:, None] >= pos[None, :]) & (pos[:, None] <= pos[None, :] + WINDOW)
            mask = mask[None, None, :, :]
            neg = jnp.asarray(-0.7 * jnp.finfo(jnp.float32).max, dtype=jnp.float32)
            scale = jnp.asarray(H ** (-0.5), dtype=q.dtype)
            encoded = []
            for i in range(Gn):
                qi = q[:, :, :, i] * scale
                logits = jnp.einsum('BTKH,BSKH->BKTS', qi, k)
                logits = jnp.tanh(logits / SOFTCAP) * SOFTCAP
                logits = jnp.where(mask, logits, neg)
                probs = jax.nn.softmax(logits.astype(jnp.float32), axis=-1).astype(logits.dtype)
                encoded.append(jnp.einsum('BKTS,BSKH->BTKH', probs, v))
            encoded = jnp.stack(encoded, axis=3)
            encoded = encoded.reshape(Bs, Ts, N_HEADS * H)
            return jnp.dot(encoded, out_kernel)
        key = jax.random.key(seed)
        kx, kq, kk, kv, ko = jax.random.split(key, 5)
        x = jax.random.normal(kx, (B, T, C), dtype=jnp.float32)
        init = lambda k, shape: 0.02 * jax.random.normal(k, shape, dtype=jnp.float32)
        q_kernel = init(kq, (C, N_HEADS * HEAD_DIM))
        k_kernel = init(kk, (C, N_KV_HEADS * HEAD_DIM))
        v_kernel = init(kv, (C, N_KV_HEADS * HEAD_DIM))
        out_kernel = init(ko, (N_HEADS * HEAD_DIM, C))
        return {'x': x, 'q_kernel': q_kernel, 'k_kernel': k_kernel, 'v_kernel': v_kernel, 'out_kernel': out_kernel}
    _L0_attn_in = _L0_attn_setup()

    def _L0_ffn_setup():
        import jax, jax.numpy as jnp
        import numpy as np

        def binarize_weight(w):
            alpha = jnp.mean(jnp.abs(w), axis=tuple(range(1, w.ndim)), keepdims=True)
            bw = jnp.where(w >= 0, 1.0, -1.0) * alpha
            return jax.lax.stop_gradient(bw - w) + w
        key = jax.random.key(seed)
        k1, k2, k3 = jax.random.split(key, 3)
        in_features, out_features = (256, 256)
        x = jax.random.normal(k1, (8, 256, in_features), dtype=jnp.float32)
        std = np.sqrt(2.0 / out_features).astype(np.float32)
        weight = jax.random.normal(k2, (out_features, in_features), dtype=jnp.float32) * std
        bias = jax.random.normal(k3, (out_features,), dtype=jnp.float32) * 0.01
        return {'x': x, 'weight': weight, 'bias': bias}
    _L0_ffn_in = _L0_ffn_setup()

    def _L1_attn_setup():
        import jax, jax.numpy as jnp
        import numpy as np
        B, S, H = (2, 256, 256)
        NH = 16
        Q_LORA, KV_LORA = (192, 64)
        D_K, D_R, D_V = (128, 64, 128)
        IH, ID, TOPK = (8, 128, 8)

        def _rope_tables(dim, end, base=10000.0):
            inv = 1.0 / base ** (np.arange(0, dim, 2)[:dim // 2].astype(np.float32) / dim)
            freqs = np.outer(np.arange(end, dtype=np.float32), inv)
            return (jnp.asarray(np.cos(freqs)), jnp.asarray(np.sin(freqs)))

        def _apply_rope(x, cos, sin):
            xr, xi = (x[..., 0::2], x[..., 1::2])
            c, s_ = (cos[None, None], sin[None, None])
            out_r = xr * c - xi * s_
            out_i = xr * s_ + xi * c
            return jnp.stack([out_r, out_i], axis=-1).reshape(x.shape)
        key = jax.random.key(seed)
        ks = jax.random.split(key, 16)
        std = 0.02

        def w(k, shape):
            return jax.random.normal(k, shape, dtype=jnp.float32) * std
        return {'x': jax.random.normal(ks[0], (B, S, H), dtype=jnp.float32), 'W_c': w(ks[1], (H, KV_LORA)), 'W_cp': w(ks[2], (H, Q_LORA)), 'W_qc': w(ks[3], (Q_LORA, NH * D_K)), 'W_qr': w(ks[4], (Q_LORA, NH * D_R)), 'W_kc': w(ks[5], (KV_LORA, NH * D_K)), 'W_kr': w(ks[6], (H, D_R)), 'W_v': w(ks[7], (KV_LORA, NH * D_V)), 'W_o': w(ks[8], (NH * D_V, H)), 'W_idx': w(ks[9], (H, IH * ID)), 'W_gate': w(ks[10], (H, IH)), 'W_sq': w(ks[11], (ID, ID)), 'W_sk': w(ks[12], (ID, ID)), 'W_sv': w(ks[13], (ID, ID)), 'W_iout': w(ks[14], (ID, H))}
    _L1_attn_in = _L1_attn_setup()

    def _L1_ffn_setup():
        import jax, jax.numpy as jnp
        import numpy as np
        E, R, K = (8, 8, 2)
        D, F = (256, 1024)
        B, S = (2, 256)
        SCALING = 16.0 / 8.0

        def act(x):
            return jax.nn.gelu(x, approximate=True)
        key = jax.random.key(seed)
        ks = jax.random.split(key, 12)
        return {'hidden_states': jax.random.normal(ks[0], (B, S, D), jnp.float32), 'W_r': jax.random.normal(ks[1], (E, D), jnp.float32) * 0.02, 'b_r': jnp.zeros((E,), jnp.float32), 'W1': jax.random.normal(ks[2], (F, D), jnp.float32) * 0.02, 'b1': jnp.zeros((F,), jnp.float32), 'W2': jax.random.normal(ks[3], (D, F), jnp.float32) * 0.02, 'b2': jnp.zeros((D,), jnp.float32), 'A1': jax.random.normal(ks[4], (E, R, D), jnp.float32) * 0.02, 'B1': jax.random.normal(ks[5], (F, R) * 1 + ()).reshape(1, F, R).repeat(1, 0) * 0.0 + jax.random.normal(ks[5], (E, F, R), jnp.float32) * 0.02, 'A2': jax.random.normal(ks[6], (E, R, F), jnp.float32) * 0.02, 'B2': jax.random.normal(ks[7], (E, D, R), jnp.float32) * 0.02}
    _L1_ffn_in = _L1_ffn_setup()

    def _L2_attn_setup():
        import jax, jax.numpy as jnp
        import numpy as np
        D_MODEL = 256
        NUM_HEADS = 16
        D_K = D_MODEL // NUM_HEADS

        def _heads(t, B, S):
            return t.reshape(B, S, NUM_HEADS, D_K).transpose(0, 2, 1, 3)
        key = jax.random.key(seed)
        ks = jax.random.split(key, 9)
        s = 1.0 / np.sqrt(D_MODEL)
        x = jax.random.normal(ks[0], (4, 512, D_MODEL), dtype=jnp.float32)
        wq = jax.random.uniform(ks[1], (D_MODEL, D_MODEL), jnp.float32, -s, s)
        bq = jax.random.uniform(ks[2], (D_MODEL,), jnp.float32, -s, s)
        wk = jax.random.uniform(ks[3], (D_MODEL, D_MODEL), jnp.float32, -s, s)
        bk = jax.random.uniform(ks[4], (D_MODEL,), jnp.float32, -s, s)
        wv = jax.random.uniform(ks[5], (D_MODEL, D_MODEL), jnp.float32, -s, s)
        bv = jax.random.uniform(ks[6], (D_MODEL,), jnp.float32, -s, s)
        wo = jax.random.uniform(ks[7], (D_MODEL, D_MODEL), jnp.float32, -s, s)
        bo = jax.random.uniform(ks[8], (D_MODEL,), jnp.float32, -s, s)
        return {'x': x, 'wq': wq, 'bq': bq, 'wk': wk, 'bk': bk, 'wv': wv, 'bv': bv, 'wo': wo, 'bo': bo}
    _L2_attn_in = _L2_attn_setup()

    def _L2_ffn_setup():
        import jax, jax.numpy as jnp
        import numpy as np
        K = 2

        def gelu(v):
            return jax.nn.gelu(v, approximate=False)
        key = jax.random.key(seed)
        ks = jax.random.split(key, 10)
        B, S, D, H, E = (4, 256, 256, 128, 8)
        SH = 2 * H
        u = lambda k_, shape, b: jax.random.uniform(k_, shape, jnp.float32, -b, b)
        return {'x': jax.random.normal(ks[0], (B, S, D), jnp.float32), 'gate_w': u(ks[1], (D, E), 1.0 / D), 'w1': u(ks[2], (E, D, H), 1.0 / D), 'b1': u(ks[3], (E, H), 1.0 / np.sqrt(D)), 'w2': u(ks[4], (E, H, D), 1.0 / H), 'b2': u(ks[5], (E, D), 1.0 / np.sqrt(H)), 'shared_w1': u(ks[6], (D, SH), 1.0 / D), 'shared_b1': u(ks[7], (SH,), 1.0 / np.sqrt(D)), 'shared_w2': u(ks[8], (SH, D), 1.0 / SH), 'shared_b2': u(ks[9], (D,), 1.0 / np.sqrt(SH))}
    _L2_ffn_in = _L2_ffn_setup()

    def _L3_attn_setup():
        import jax, jax.numpy as jnp
        import numpy as np
        B, N, E = (4, 512, 256)
        H_DIM = 256
        HEADS = 16
        DH = H_DIM // HEADS
        LN_EPS = 1e-05

        def _heads(t):
            b, n, _ = t.shape
            return t.reshape(b, n, HEADS, DH).transpose(0, 2, 1, 3)

        def _layernorm(x, g, b):
            mu = jnp.mean(x, axis=-1, keepdims=True)
            var = jnp.mean(jnp.square(x - mu), axis=-1, keepdims=True)
            return (x - mu) * jax.lax.rsqrt(var + LN_EPS) * g + b
        key = jax.random.key(seed)
        ks = jax.random.split(key, 10)
        s = 1.0 / np.sqrt(E)
        so = 1.0 / np.sqrt(H_DIM)
        return {'x': jax.random.normal(ks[0], (B, N, E), jnp.float32), 'Wqk': jax.random.normal(ks[1], (E, H_DIM), jnp.float32) * s, 'bqk': jnp.zeros((H_DIM,), jnp.float32), 'Wv': jax.random.normal(ks[2], (E, H_DIM), jnp.float32) * s, 'bv': jnp.zeros((H_DIM,), jnp.float32), 'Wu': jax.random.normal(ks[3], (E, H_DIM), jnp.float32) * s, 'bu': jnp.zeros((H_DIM,), jnp.float32), 'Wo': jax.random.normal(ks[4], (H_DIM, E), jnp.float32) * so, 'bo': jnp.zeros((E,), jnp.float32), 'ln_g': jnp.ones((H_DIM,), jnp.float32), 'ln_b': jnp.zeros((H_DIM,), jnp.float32)}
    _L3_attn_in = _L3_attn_setup()

    def _L3_ffn_setup():
        import jax, jax.numpy as jnp
        import numpy as np

        def ternary_quantize(t, threshold, scale):
            return jnp.where(t > threshold, scale, jnp.where(t < -threshold, -scale, 0.0)).astype(t.dtype)
        key = jax.random.key(seed)
        k1, k2, k3 = jax.random.split(key, 3)
        B, S, D = (4, 512, 256)
        x = jax.random.normal(k1, (B, S, D), dtype=jnp.float32)
        weight = jax.random.normal(k2, (D, D), dtype=jnp.float32) * 0.02
        rram_variation = jax.random.normal(k3, (D, D), dtype=jnp.float32) * 0.05
        return {'x': x, 'weight': weight, 'rram_variation': rram_variation}
    _L3_ffn_in = _L3_ffn_setup()
    _d = {'L0_attn_x': _L0_attn_in['x'], 'L0_attn_q_kernel': _L0_attn_in['q_kernel'], 'L0_attn_k_kernel': _L0_attn_in['k_kernel'], 'L0_attn_v_kernel': _L0_attn_in['v_kernel'], 'L0_attn_out_kernel': _L0_attn_in['out_kernel'], 'L0_ffn_weight': _L0_ffn_in['weight'], 'L0_ffn_bias': _L0_ffn_in['bias'], 'L1_attn_W_c': _L1_attn_in['W_c'], 'L1_attn_W_cp': _L1_attn_in['W_cp'], 'L1_attn_W_qc': _L1_attn_in['W_qc'], 'L1_attn_W_qr': _L1_attn_in['W_qr'], 'L1_attn_W_kc': _L1_attn_in['W_kc'], 'L1_attn_W_kr': _L1_attn_in['W_kr'], 'L1_attn_W_v': _L1_attn_in['W_v'], 'L1_attn_W_o': _L1_attn_in['W_o'], 'L1_attn_W_idx': _L1_attn_in['W_idx'], 'L1_attn_W_gate': _L1_attn_in['W_gate'], 'L1_attn_W_sq': _L1_attn_in['W_sq'], 'L1_attn_W_sk': _L1_attn_in['W_sk'], 'L1_attn_W_sv': _L1_attn_in['W_sv'], 'L1_attn_W_iout': _L1_attn_in['W_iout'], 'L1_ffn_W_r': _L1_ffn_in['W_r'], 'L1_ffn_b_r': _L1_ffn_in['b_r'], 'L1_ffn_W1': _L1_ffn_in['W1'], 'L1_ffn_b1': _L1_ffn_in['b1'], 'L1_ffn_W2': _L1_ffn_in['W2'], 'L1_ffn_b2': _L1_ffn_in['b2'], 'L1_ffn_A1': _L1_ffn_in['A1'], 'L1_ffn_B1': _L1_ffn_in['B1'], 'L1_ffn_A2': _L1_ffn_in['A2'], 'L1_ffn_B2': _L1_ffn_in['B2'], 'L2_attn_wq': _L2_attn_in['wq'], 'L2_attn_bq': _L2_attn_in['bq'], 'L2_attn_wk': _L2_attn_in['wk'], 'L2_attn_bk': _L2_attn_in['bk'], 'L2_attn_wv': _L2_attn_in['wv'], 'L2_attn_bv': _L2_attn_in['bv'], 'L2_attn_wo': _L2_attn_in['wo'], 'L2_attn_bo': _L2_attn_in['bo'], 'L2_ffn_gate_w': _L2_ffn_in['gate_w'], 'L2_ffn_w1': _L2_ffn_in['w1'], 'L2_ffn_b1': _L2_ffn_in['b1'], 'L2_ffn_w2': _L2_ffn_in['w2'], 'L2_ffn_b2': _L2_ffn_in['b2'], 'L2_ffn_shared_w1': _L2_ffn_in['shared_w1'], 'L2_ffn_shared_b1': _L2_ffn_in['shared_b1'], 'L2_ffn_shared_w2': _L2_ffn_in['shared_w2'], 'L2_ffn_shared_b2': _L2_ffn_in['shared_b2'], 'L3_attn_Wqk': _L3_attn_in['Wqk'], 'L3_attn_bqk': _L3_attn_in['bqk'], 'L3_attn_Wv': _L3_attn_in['Wv'], 'L3_attn_bv': _L3_attn_in['bv'], 'L3_attn_Wu': _L3_attn_in['Wu'], 'L3_attn_bu': _L3_attn_in['bu'], 'L3_attn_Wo': _L3_attn_in['Wo'], 'L3_attn_bo': _L3_attn_in['bo'], 'L3_attn_ln_g': _L3_attn_in['ln_g'], 'L3_attn_ln_b': _L3_attn_in['ln_b'], 'L3_ffn_weight': _L3_ffn_in['weight'], 'L3_ffn_rram_variation': _L3_ffn_in['rram_variation']}
    _x0 = _d['L0_attn_x']
    _d['L0_attn_x'] = jax.random.normal(jax.random.fold_in(jax.random.key(seed), 1), (2, 1024, 256), dtype=_x0.dtype)
    del _x0
    return _d

def reference(L0_attn_x, L0_attn_q_kernel, L0_attn_k_kernel, L0_attn_v_kernel, L0_attn_out_kernel, L0_ffn_weight, L0_ffn_bias, L1_attn_W_c, L1_attn_W_cp, L1_attn_W_qc, L1_attn_W_qr, L1_attn_W_kc, L1_attn_W_kr, L1_attn_W_v, L1_attn_W_o, L1_attn_W_idx, L1_attn_W_gate, L1_attn_W_sq, L1_attn_W_sk, L1_attn_W_sv, L1_attn_W_iout, L1_ffn_W_r, L1_ffn_b_r, L1_ffn_W1, L1_ffn_b1, L1_ffn_W2, L1_ffn_b2, L1_ffn_A1, L1_ffn_B1, L1_ffn_A2, L1_ffn_B2, L2_attn_wq, L2_attn_bq, L2_attn_wk, L2_attn_bk, L2_attn_wv, L2_attn_bv, L2_attn_wo, L2_attn_bo, L2_ffn_gate_w, L2_ffn_w1, L2_ffn_b1, L2_ffn_w2, L2_ffn_b2, L2_ffn_shared_w1, L2_ffn_shared_b1, L2_ffn_shared_w2, L2_ffn_shared_b2, L3_attn_Wqk, L3_attn_bqk, L3_attn_Wv, L3_attn_bv, L3_attn_Wu, L3_attn_bu, L3_attn_Wo, L3_attn_bo, L3_attn_ln_g, L3_attn_ln_b, L3_ffn_weight, L3_ffn_rram_variation):

    def _L0_attn_ref(x, q_kernel, k_kernel, v_kernel, out_kernel):
        import jax, jax.numpy as jnp
        import numpy as np
        N_HEADS = 16
        N_KV_HEADS = 4
        HEAD_DIM = 128
        ROPE_THETA = 10000.0
        WINDOW = 128
        SOFTCAP = 50.0
        B, T, C = (2, 256, 256)
        G = N_HEADS // N_KV_HEADS

        def _sine_table(features, length, max_timescale):
            fraction = jnp.arange(0, features, 2, dtype=jnp.float32) / features
            inv_timescale = 1.0 / max_timescale ** fraction
            sinusoid = jnp.einsum('i,j->ij', jnp.arange(length), inv_timescale, precision=jax.lax.Precision.HIGHEST)
            sinusoid = jnp.concatenate([sinusoid, sinusoid], axis=-1)
            return (jnp.sin(sinusoid), jnp.cos(sinusoid))

        def _rotate_half(x):
            x1, x2 = jnp.split(x, 2, axis=-1)
            return jnp.concatenate([-x2, x1], axis=-1)

        def _attention(x, q_kernel, k_kernel, v_kernel, out_kernel):
            Bs, Ts, Cs = x.shape
            K, H, Gn = (N_KV_HEADS, HEAD_DIM, G)
            q = jnp.dot(x, q_kernel).reshape(Bs, Ts, K, Gn, H)
            k = jnp.dot(x, k_kernel).reshape(Bs, Ts, K, H)
            v = jnp.dot(x, v_kernel).reshape(Bs, Ts, K, H)
            sin, cos = _sine_table(H, Ts, ROPE_THETA)
            qcos = cos[None, :, None, None, :]
            qsin = sin[None, :, None, None, :]
            kcos = cos[None, :, None, :]
            ksin = sin[None, :, None, :]
            q = (q * qcos + _rotate_half(q) * qsin).astype(q.dtype)
            k = (k * kcos + _rotate_half(k) * ksin).astype(k.dtype)
            pos = jnp.arange(Ts)
            mask = (pos[:, None] >= pos[None, :]) & (pos[:, None] <= pos[None, :] + WINDOW)
            mask = mask[None, None, :, :]
            neg = jnp.asarray(-0.7 * jnp.finfo(jnp.float32).max, dtype=jnp.float32)
            scale = jnp.asarray(H ** (-0.5), dtype=q.dtype)
            encoded = []
            for i in range(Gn):
                qi = q[:, :, :, i] * scale
                logits = jnp.einsum('BTKH,BSKH->BKTS', qi, k)
                logits = jnp.tanh(logits / SOFTCAP) * SOFTCAP
                logits = jnp.where(mask, logits, neg)
                probs = jax.nn.softmax(logits.astype(jnp.float32), axis=-1).astype(logits.dtype)
                encoded.append(jnp.einsum('BKTS,BSKH->BTKH', probs, v))
            encoded = jnp.stack(encoded, axis=3)
            encoded = encoded.reshape(Bs, Ts, N_HEADS * H)
            return jnp.dot(encoded, out_kernel)
        return _attention(x, q_kernel, k_kernel, v_kernel, out_kernel)

    def _L0_ffn_ref(x, weight, bias):
        import jax, jax.numpy as jnp
        import numpy as np

        def binarize_weight(w):
            alpha = jnp.mean(jnp.abs(w), axis=tuple(range(1, w.ndim)), keepdims=True)
            bw = jnp.where(w >= 0, 1.0, -1.0) * alpha
            return jax.lax.stop_gradient(bw - w) + w
        bw = binarize_weight(weight)
        return jnp.einsum('bsi,oi->bso', x, bw) + bias

    def _L1_attn_ref(x, W_c, W_cp, W_qc, W_qr, W_kc, W_kr, W_v, W_o, W_idx, W_gate, W_sq, W_sk, W_sv, W_iout):
        import jax, jax.numpy as jnp
        import numpy as np
        B, S, H = (2, 256, 256)
        NH = 16
        Q_LORA, KV_LORA = (192, 64)
        D_K, D_R, D_V = (128, 64, 128)
        IH, ID, TOPK = (8, 128, 8)

        def _rope_tables(dim, end, base=10000.0):
            inv = 1.0 / base ** (np.arange(0, dim, 2)[:dim // 2].astype(np.float32) / dim)
            freqs = np.outer(np.arange(end, dtype=np.float32), inv)
            return (jnp.asarray(np.cos(freqs)), jnp.asarray(np.sin(freqs)))

        def _apply_rope(x, cos, sin):
            xr, xi = (x[..., 0::2], x[..., 1::2])
            c, s_ = (cos[None, None], sin[None, None])
            out_r = xr * c - xi * s_
            out_i = xr * s_ + xi * c
            return jnp.stack([out_r, out_i], axis=-1).reshape(x.shape)
        b, s, _ = x.shape
        cos, sin = _rope_tables(D_R, s)
        c = x @ W_c
        cp = x @ W_cp
        q_c = (cp @ W_qc).reshape(b, s, NH, D_K).transpose(0, 2, 1, 3)
        k_c = (c @ W_kc).reshape(b, s, NH, D_K).transpose(0, 2, 1, 3)
        q_r = (cp @ W_qr).reshape(b, s, NH, D_R).transpose(0, 2, 1, 3)
        k_r = jnp.broadcast_to((x @ W_kr)[:, None], (b, NH, s, D_R))
        v = (c @ W_v).reshape(b, s, NH, D_V).transpose(0, 2, 1, 3)
        q_r = _apply_rope(q_r, cos, sin)
        k_r = _apply_rope(k_r, cos, sin)
        q = jnp.concatenate([q_c, q_r], axis=-1)
        k = jnp.concatenate([k_c, k_r], axis=-1)
        scale = 1.0 / np.sqrt(D_K + D_R)
        scores = jnp.einsum('bhqd,bhkd->bhqk', q, k) * scale
        causal = jnp.triu(jnp.ones((s, s), dtype=bool), 1)
        scores = jnp.where(causal[None, None], -jnp.inf, scores)
        probs = jax.nn.softmax(scores.astype(jnp.float32), axis=-1).astype(q.dtype)
        attn = jnp.einsum('bhqk,bhkd->bhqd', probs, v)
        idx_states = (x @ W_idx).reshape(b, s, IH, ID)
        gate = x @ W_gate
        _, top_idx = jax.lax.top_k(gate.transpose(0, 2, 1), TOPK)
        ish = idx_states.transpose(0, 2, 1, 3)
        sel = jnp.take_along_axis(ish, top_idx[..., None], axis=2)
        sq, sk, sv = (sel @ W_sq, sel @ W_sk, sel @ W_sv)
        sprobs = jax.nn.softmax(jnp.einsum('bhqd,bhkd->bhqk', sq, sk) / np.sqrt(ID), axis=-1)
        sout = jnp.einsum('bhqk,bhkd->bhqd', sprobs, sv)
        sparse_out = sout.reshape(b, IH * TOPK, ID) @ W_iout
        io = sparse_out.reshape(b, IH, TOPK, H).mean(axis=2)
        io = jnp.broadcast_to(io[:, :, None, :D_V], (b, IH, s, D_V))
        io = jnp.repeat(io, NH // IH, axis=1)
        attn = attn + io
        out = attn.transpose(0, 2, 1, 3).reshape(b, s, NH * D_V) @ W_o
        return out

    def _L1_ffn_ref(hidden_states, W_r, b_r, W1, b1, W2, b2, A1, B1, A2, B2):
        import jax, jax.numpy as jnp
        import numpy as np
        E, R, K = (8, 8, 2)
        D, F = (256, 1024)
        B, S = (2, 256)
        SCALING = 16.0 / 8.0

        def act(x):
            return jax.nn.gelu(x, approximate=True)
        b, s, d = hidden_states.shape
        N = b * s
        x = hidden_states.reshape(N, d)
        probs = jax.nn.softmax(x @ W_r.T + b_r, axis=-1)
        w_topk, idx_topk = jax.lax.top_k(probs, K)
        base1 = x @ W1.T + b1
        u1 = jnp.einsum('nd,erd->ner', x, A1)
        B1_rf = B1.transpose(0, 2, 1).reshape(E * R, F)
        B2_rf = B2.transpose(0, 2, 1).reshape(E * R, d)
        res = jnp.zeros((N, d), hidden_states.dtype)
        for k in range(K):
            oh = jax.nn.one_hot(idx_topk[:, k], E, dtype=x.dtype)
            z1 = (u1 * oh[:, :, None]).reshape(N, E * R)
            h = act(base1 + z1 @ B1_rf * SCALING)
            u2 = jnp.einsum('nf,erf->ner', h, A2)
            z2 = (u2 * oh[:, :, None]).reshape(N, E * R)
            y = h @ W2.T + b2 + z2 @ B2_rf * SCALING
            res = res + w_topk[:, k:k + 1] * y
        return res.reshape(b, s, d)

    def _L2_attn_ref(x, wq, bq, wk, bk, wv, bv, wo, bo):
        import jax, jax.numpy as jnp
        import numpy as np
        D_MODEL = 256
        NUM_HEADS = 16
        D_K = D_MODEL // NUM_HEADS

        def _heads(t, B, S):
            return t.reshape(B, S, NUM_HEADS, D_K).transpose(0, 2, 1, 3)
        B, S, _ = x.shape
        Q = _heads(x @ wq.T + bq, B, S)
        K = _heads(x @ wk.T + bk, B, S)
        V = _heads(x @ wv.T + bv, B, S)
        Q = jax.nn.elu(Q) + 1.0
        K = jax.nn.elu(K) + 1.0
        KV = jnp.einsum('bhsd,bhse->bhde', K, V)
        QKV = jnp.einsum('bhsd,bhde->bhse', Q, KV)
        K_sum = jnp.sum(K, axis=-2)
        QK_sum = jnp.einsum('bhsd,bhd->bhs', Q, K_sum)
        out = QKV / (QK_sum[..., None] + 1e-08)
        out = out.transpose(0, 2, 1, 3).reshape(B, S, D_MODEL)
        return out @ wo.T + bo

    def _L2_ffn_ref(x, gate_w, w1, b1, w2, b2, shared_w1, shared_b1, shared_w2, shared_b2):
        import jax, jax.numpy as jnp
        import numpy as np
        K = 2

        def gelu(v):
            return jax.nn.gelu(v, approximate=False)
        B, S, D = x.shape
        E = gate_w.shape[1]
        xf = x.reshape(-1, D)
        logits = xf @ gate_w
        top_logits, top_idx = jax.lax.top_k(logits, K)
        top_gates = jax.nn.softmax(top_logits, axis=-1)
        gates = jnp.sum(jax.nn.one_hot(top_idx, E, dtype=xf.dtype) * top_gates[..., None], axis=1)
        h = gelu(jnp.einsum('nd,edh->neh', xf, w1) + b1)
        out_e = jnp.einsum('neh,ehd->ned', h, w2) + b2
        routed = jnp.einsum('ne,ned->nd', gates, out_e)
        shared = gelu(xf @ shared_w1 + shared_b1) @ shared_w2 + shared_b2
        return (routed + shared).reshape(B, S, D)

    def _L3_attn_ref(x, Wqk, bqk, Wv, bv, Wu, bu, Wo, bo, ln_g, ln_b):
        import jax, jax.numpy as jnp
        import numpy as np
        B, N, E = (4, 512, 256)
        H_DIM = 256
        HEADS = 16
        DH = H_DIM // HEADS
        LN_EPS = 1e-05

        def _heads(t):
            b, n, _ = t.shape
            return t.reshape(b, n, HEADS, DH).transpose(0, 2, 1, 3)

        def _layernorm(x, g, b):
            mu = jnp.mean(x, axis=-1, keepdims=True)
            var = jnp.mean(jnp.square(x - mu), axis=-1, keepdims=True)
            return (x - mu) * jax.lax.rsqrt(var + LN_EPS) * g + b
        q = x @ Wqk + bqk
        k = x @ Wqk + bqk
        v = jax.nn.silu(x @ Wv + bv)
        u = jax.nn.silu(x @ Wu + bu)
        q = jax.nn.elu(_heads(q))
        kh = jax.nn.elu(_heads(k))
        vh = _heads(v)
        kv = jnp.einsum('bhnd,bhne->bhde', kh, vh)
        out = jnp.einsum('bhnd,bhde->bhne', q, kv)
        out = out.transpose(0, 2, 1, 3).reshape(x.shape[0], x.shape[1], H_DIM)
        out = _layernorm(out, ln_g, ln_b)
        out = u * out
        return out @ Wo + bo

    def _L3_ffn_ref(x, weight, rram_variation):
        import jax, jax.numpy as jnp
        import numpy as np

        def ternary_quantize(t, threshold, scale):
            return jnp.where(t > threshold, scale, jnp.where(t < -threshold, -scale, 0.0)).astype(t.dtype)
        TH_X, SC_X = (0.33, 0.5)
        TH_W, SC_W = (0.2, 0.6)
        x_q = ternary_quantize(x, TH_X, SC_X)
        w_q = ternary_quantize(weight, TH_W, SC_W)
        w_rram = w_q + rram_variation
        return jnp.einsum('bsd,od->bso', x_q, w_rram)
    x = L0_attn_x
    x = x + _L0_attn_ref(_layernorm(x, axis=-1), L0_attn_q_kernel, L0_attn_k_kernel, L0_attn_v_kernel, L0_attn_out_kernel)
    x = x + _L0_ffn_ref(_layernorm(x, axis=-1), L0_ffn_weight, L0_ffn_bias)
    x = x + _L1_attn_ref(_layernorm(x, axis=-1), L1_attn_W_c, L1_attn_W_cp, L1_attn_W_qc, L1_attn_W_qr, L1_attn_W_kc, L1_attn_W_kr, L1_attn_W_v, L1_attn_W_o, L1_attn_W_idx, L1_attn_W_gate, L1_attn_W_sq, L1_attn_W_sk, L1_attn_W_sv, L1_attn_W_iout)
    x = x + _L1_ffn_ref(_layernorm(x, axis=-1), L1_ffn_W_r, L1_ffn_b_r, L1_ffn_W1, L1_ffn_b1, L1_ffn_W2, L1_ffn_b2, L1_ffn_A1, L1_ffn_B1, L1_ffn_A2, L1_ffn_B2)
    x = x + _L2_attn_ref(_layernorm(x, axis=-1), L2_attn_wq, L2_attn_bq, L2_attn_wk, L2_attn_bk, L2_attn_wv, L2_attn_bv, L2_attn_wo, L2_attn_bo)
    x = x + _L2_ffn_ref(_layernorm(x, axis=-1), L2_ffn_gate_w, L2_ffn_w1, L2_ffn_b1, L2_ffn_w2, L2_ffn_b2, L2_ffn_shared_w1, L2_ffn_shared_b1, L2_ffn_shared_w2, L2_ffn_shared_b2)
    x = x + _L3_attn_ref(_layernorm(x, axis=-1), L3_attn_Wqk, L3_attn_bqk, L3_attn_Wv, L3_attn_bv, L3_attn_Wu, L3_attn_bu, L3_attn_Wo, L3_attn_bo, L3_attn_ln_g, L3_attn_ln_b)
    x = x + _L3_ffn_ref(_layernorm(x, axis=-1), L3_ffn_weight, L3_ffn_rram_variation)
    return x

_drawn_inputs = setup_inputs


def setup_inputs(seed=0):
    import zlib

    import numpy as np

    out = dict(_drawn_inputs(seed))
    spreads = {'L1_ffn_b_r': (0.0, 0.8),
     'L1_ffn_b1': (0.0, 0.311),
     'L1_ffn_b2': (0.0, 0.709),
     'L3_attn_bqk': (0.0, 0.356),
     'L3_attn_bv': (0.0, 0.409),
     'L3_attn_bu': (0.0, 0.8),
     'L3_attn_bo': (0.0, 0.604),
     'L3_attn_ln_g': (1.0, 0.6),
     'L3_attn_ln_b': (0.0, 0.8)}
    factors = {'L0_attn_q_kernel': 5.867,
     'L0_attn_k_kernel': 5.776,
     'L0_ffn_bias': 2.759,
     'L1_attn_W_c': 6.384,
     'L1_attn_W_cp': 8.0,
     'L1_attn_W_qc': 8.0,
     'L1_attn_W_qr': 8.0,
     'L1_attn_W_kc': 8.0,
     'L1_attn_W_kr': 8.0,
     'L1_attn_W_v': 6.497,
     'L1_attn_W_o': 3.607,
     'L1_attn_W_idx': 3.915,
     'L1_attn_W_gate': 3.857,
     'L1_attn_W_sq': 8.0,
     'L1_attn_W_sk': 8.0,
     'L1_attn_W_sv': 4.083,
     'L1_attn_W_iout': 3.878,
     'L1_ffn_W_r': 4.933,
     'L1_ffn_A1': 7.259,
     'L1_ffn_B1': 7.388,
     'L1_ffn_A2': 7.141,
     'L1_ffn_B2': 7.142,
     'L2_attn_wq': 64.0,
     'L2_attn_bq': 200.0,
     'L2_attn_wk': 44.504,
     'L2_attn_bk': 200.0,
     'L2_ffn_w1': 64.0,
     'L2_ffn_b1': 64.0,
     'L2_ffn_w2': 49.4,
     'L2_ffn_shared_w1': 64.0,
     'L2_ffn_shared_b1': 64.0,
     'L2_ffn_shared_w2': 50.087,
     'L2_attn_wv': 4.602,
     'L2_attn_bv': 8.0,
     'L2_attn_wo': 4.063,
     'L2_attn_bo': 8.0,
     'L2_ffn_gate_w': 6.341,
     'L2_ffn_b2': 8.0,
     'L2_ffn_shared_b2': 8.0}
    for name, (base, spread) in spreads.items():
        noise = np.random.default_rng([zlib.crc32(name.encode()), seed]).standard_normal(out[name].shape)
        drawn = base * np.exp(spread * noise) if base else spread * noise
        out[name] = jnp.asarray(drawn.astype(out[name].dtype))
    for name, factor in factors.items():
        out[name] = (out[name] * factor).astype(out[name].dtype)
    return out
```

```python
from contextlib import ExitStack

import numpy as np

import concourse.bass as bass
from concourse import mybir

F32 = mybir.dt.float32
BF16 = mybir.dt.bfloat16
U32 = mybir.dt.uint32
ACT = mybir.ActivationFunctionType
ALU = mybir.AluOpType
AX = mybir.AxisListType

P = 128
NB, SEQ, D = 2, 1024, 256
TILES = SEQ // P
KC = D // P
BLK = 512
TPB = BLK // P
BLOCKS = NB * SEQ // BLK
BPB = SEQ // BLK
EPS = 1e-5

LAYERS = range(8)


def before(it, per, n):
    assert n >= 1
    return it * per + n


def now(it, per, n, credit=False):
    assert n + (per if credit else 0) >= 1
    return it * per + n + (per if credit else 0)


class Steps:

    def __init__(self, eng, sem, it=0, per=0):
        self.eng, self.sem, self.it, self.per, self.n = eng, sem, it, per, 0

    def mark(self, ins):
        self.n += 1
        ins.then_inc(self.sem, 1)
        return self.n

    def hold(self, n):
        self.eng.wait_ge(self.sem, now(self.it, self.per, n))

    def then(self, ins):
        self.hold(self.mark(ins))

    def close(self):
        assert self.per in (0, self.n), (self.per, self.n)


def hold_apart(eng, sem, value, apart):
    eng.wait_ge(sem, value)
    eng.sem_inc(apart, 1)


def spread(ap, shape):
    return ap.to_broadcast(shape)


RETIRED = []


def recycle_semaphores(nc):
    nc.clear_and_free_semaphores(RETIRED)
    RETIRED.clear()
    nc.all_engine_barrier()


class Phase:

    def __init__(self, nc, tag):
        self.nc, self.tag, self.stack, self.sems, self.named = nc, tag, ExitStack(), [], {}

    def __enter__(self):
        self.stack.__enter__()
        return self

    def __exit__(self, *what):
        RETIRED.extend(self.sems)
        return self.stack.__exit__(*what)

    def sb(self, name, shape, dt=F32):
        self.named[name] = self.stack.enter_context(self.nc.sbuf_tensor(f"{self.tag}_{name}", shape, dt))
        return self.named[name]

    def __getitem__(self, name):
        return self.named[name]

    def ps(self, name, shape, dt=F32):
        return self.stack.enter_context(self.nc.psum_tensor(f"{self.tag}_{name}", shape, dt))

    def sem(self, name):
        self.sems.append(self.nc.alloc_semaphore(f"{self.tag}_{name}"))
        return self.sems[-1]

    def block(self):
        return self.nc.Block()


def norm_phase(nc, G, tag, load=None, keep=None, ternary=None):
    with Phase(nc, tag) as ph:
        stats = ph.sb("stats", [P, TPB, 6])
        mv = ph.sb("mv", [P, TPB, 2])
        veps = ph.sb("veps", [P, TPB])
        rstd = ph.sb("rstd", [P, TPB])
        xn = ph.sb("xn", [P, TPB, D])
        low = ph.sb("low", [P, TPB, D]) if ternary else None
        turned = ph.ps("turned", [P, KC, BLK])
        var_ready = ph.sem("var_ready")
        rstd_ready = ph.sem("rstd_ready")
        xn_ready = ph.sem("xn_ready")
        turn_done = ph.sem("turn_done")
        out_done = ph.sem("out_done")
        kept = ph.sem("kept")
        dve_steps = ph.sem("dve_steps")
        apart = ph.sem("apart")
        apart_pool = ph.sem("apart_pool")
        per_steps = 3 * TPB + 2 if ternary else 2 * TPB
        x_flat = G.x[:].rearrange("p b i d -> p (b i) d")
        xnT_flat = G.xnT[:].rearrange("p k b t -> p k (b t)")
        keep_flat = keep[:].rearrange("p b i d -> p (b i) d") if keep is not None else None

        with ph.block() as block:
            if load:
                @block.sync
                def _(sp):
                    load(sp)

            @block.gpsimd
            def _(pool):
                if keep is not None:
                    pool.sem_inc(kept, 1)
                with pool.Fori(0, BLOCKS) as it:
                    pool.wait_ge(var_ready, now(it, 1, 1))
                    nc.gpsimd.tensor_tensor(rstd[:], veps[:], G.minus_half[:], ALU.pow)\
                        .then_inc(rstd_ready, 1)
                    if keep is not None:
                        hold_apart(pool, xn_ready, now(it, 1, 1), apart_pool)
                        nc.gpsimd.tensor_copy(keep_flat[:, bass.ds(it * TPB, TPB), :], xn[:])\
                            .then_inc(kept, 1)

            @block.vector
            def _(dve):
                with dve.Fori(0, BLOCKS) as it:
                    steps = Steps(dve, dve_steps, it, per_steps)
                    for j in range(TPB):
                        n = steps.mark(nc.vector.bn_stats(stats[:, j, :], x_flat[:, bass.ds(it * TPB + j, 1), :]))
                    hold_apart(dve, dve_steps, now(it, per_steps, n), apart)
                    for j in range(TPB):
                        n = steps.mark(nc.vector.bn_aggr(mv[:, j, :], stats[:, j, :]))
                    steps.hold(n)
                    nc.vector.tensor_scalar(veps[:], mv[:, :, 1], EPS, None, ALU.add).then_inc(var_ready, 1)
                    dve.wait_ge(rstd_ready, now(it, 1, 1))
                    if keep is not None:
                        dve.wait_ge(kept, before(it, 1, 1))
                    dve.wait_ge(turn_done, before(it, 1, 1))
                    for j in range(TPB):
                        ins = nc.vector.tensor_scalar(xn[:, j, :], x_flat[:, bass.ds(it * TPB + j, 1), :],
                                                      mv[:, j, 0:1], rstd[:, j:j + 1],
                                                      ALU.subtract, ALU.mult)
                        if ternary:
                            n = steps.mark(ins)
                    if ternary:
                        threshold, scale = ternary
                        steps.hold(n)
                        steps.then(nc.vector.tensor_scalar(low[:], xn[:], -threshold, scale, ALU.is_lt, ALU.mult))
                        steps.then(nc.vector.tensor_scalar(xn[:], xn[:], threshold, scale, ALU.is_gt, ALU.mult))
                        ins = nc.vector.tensor_tensor(xn[:], xn[:], low[:], ALU.subtract)
                    ins.then_inc(xn_ready, 1)
                    steps.close()

            @block.tensor
            def _(pe):
                pe.sem_inc(turn_done, 1)
                with pe.Fori(0, BLOCKS) as it:
                    pe.wait_ge(xn_ready, now(it, 1, 1))
                    pe.wait_ge(out_done, before(it, 1, 1))
                    for k in range(KC):
                        for j in range(TPB):
                            ins = nc.tensor.transpose(turned[:, k, j * P:(j + 1) * P],
                                                      xn[:, j, k * P:(k + 1) * P], G.ident[:])
                    ins.then_inc(turn_done, 1)

            @block.scalar
            def _(act):
                act.sem_inc(out_done, 1)
                with act.Fori(0, BLOCKS) as it:
                    act.wait_ge(turn_done, now(it, 1, 1, credit=True))
                    nc.scalar.copy(xnT_flat[:, :, bass.ds(it * BLK, BLK)], turned[:]).then_inc(out_done, 1)


NH, NKV, HD = 16, 4, 128
GROUP = NH // NKV
CAP = 50.0


def load_l0_attn(nc, G, W, sem):
    def load(sp):
        I = G.dram
        for dst, src in ((W.q[:], I["L0_attn_q_kernel"].rearrange("(k p) n -> p k n", p=P)),
                         (W.k[:], I["L0_attn_k_kernel"].rearrange("(k p) n -> p k n", p=P)),
                         (W.v[:], I["L0_attn_v_kernel"].rearrange("(k p) n -> p k n", p=P)),
                         (W.o[:], I["L0_attn_out_kernel"].rearrange("(h p) n -> p h n", p=P)),
                         (W.cos[:], I["l0_cos"]), (W.sin[:], I["l0_sin"])):
            sp.dma_start(dst, src).then_inc(sem, 16)
    return load


def l0_attn(nc, G):
    with Phase(nc, "l0w") as W:
        W.q = W.sb("q", [P, KC, NH * HD])
        W.k = W.sb("k", [P, KC, NKV * HD])
        W.v = W.sb("v", [P, KC, NKV * HD])
        W.o = W.sb("o", [P, NH, D])
        W.cos = W.sb("cos", [P, SEQ])
        W.sin = W.sb("sin", [P, SEQ])
        w_in = W.sem("w_in")
        LOADS = 6 * 16
        norm_phase(nc, G, "l0n", load=load_l0_attn(nc, G, W, w_in))
        l0_attn_tiles(nc, G, W, w_in, LOADS)


def l0_attn_tiles(nc, G, W, w_in, LOADS):
    with Phase(nc, "l0a") as ph:
        xs = ph.sb("xs", [P, KC, NB, P])
        qT = ph.sb("qT", [P, NH, NB, P])
        kT = ph.sb("kT", [P, 2, NKV, NB, P])
        v = ph.sb("v", [P, 2, NB, NKV, HD + 1])
        rope_a = ph.sb("rope_a", [P, 2, BLK])
        rope_b = ph.sb("rope_b", [P, 2, BLK])
        capped = ph.sb("capped", [P, 2, BLK])
        probs = ph.sb("probs", [P, 2, 2, BLK])
        rden = ph.sb("rden", [P, GROUP])
        enc = ph.sb("enc", [P, 2, GROUP, HD])
        encT = ph.sb("encT", [P, NB, NH, P])
        proj = ph.ps("proj", [P, 2, BLK])
        score = ph.ps("score", [P, 2, BLK])
        pv = ph.ps("pv", [P, 2, BLK])
        turned = ph.ps("turned", [P, BLK])
        y = ph.ps("y", [P, NB, D])

        UNITS = NKV * NB
        KB, QB = NKV // 2, NH // 2
        ROPES = KB + QB
        SCALE = float(HD) ** -0.5 / CAP

        xs_ready = ph.sem("xs_ready")
        moved = ph.sem("moved")
        proj_done = ph.sem("proj_done")
        roped = ph.sem("roped")
        rotated = ph.sem("rotated")
        v_ready = ph.sem("v_ready")
        score_done = ph.sem("score_done")
        tanh_done = ph.sem("tanh_done")
        exp_done = ph.sem("exp_done")
        masked = ph.sem("masked")
        pv_done = ph.sem("pv_done")
        enc_done = ph.sem("enc_done")
        turn_done = ph.sem("turn_done")
        encT_done = ph.sem("encT_done")
        y_done = ph.sem("y_done")
        x_added = ph.sem("x_added")
        dve_steps = ph.sem("dve_steps")
        apart = ph.sem("apart")
        cleared = ph.sem("cleared")
        BANKS = KB + NB + QB
        n_rope = {**{("k", j): j + 1 for j in range(KB)}, **{("q", j): KB + j + 1 for j in range(QB)}}

        def q_banks(u):
            g = u // NB + 1
            return (2 * g, 2 * g + 1) if u % NB == 0 and g < NKV else ()

        with ph.block() as block:
            @block.gpsimd
            def _(pool):
                nc.gpsimd.memset(kT[:], 0.0).then_inc(cleared, 1)
                nc.gpsimd.memset(v[:], 0.0).then_inc(cleared, 1)
                pool.wait_ge(cleared, 2)
                pool.sem_inc(rotated, ROPES)
                with pool.Fori(0, TILES) as it:
                    pool.wait_ge(proj_done, before(it, BANKS, BANKS))
                    nc.gpsimd.tensor_copy(xs[:], G.xnT[:, :, :, bass.ds(it * P, P)]).then_inc(xs_ready, 1)
                    hold_apart(pool, pv_done, before(it, UNITS, UNITS), apart)
                    nc.gpsimd.tensor_copy(kT[:, 1], kT[:, 0])
                    nc.gpsimd.tensor_copy(v[:, 1], v[:, 0]).then_inc(moved, 1)
                    hold_apart(pool, moved, now(it, 1, 1), apart)
                    nc.gpsimd.memset(v[:, 0, :, :, HD:HD + 1], 1.0)

                    def rotate(kind, j):
                        n = n_rope[kind, j]
                        pool.wait_ge(roped, now(it, ROPES, n, credit=True))
                        dst = kT[:, 0, 2 * j:2 * j + 2] if kind == "k" else qT[:, 2 * j:2 * j + 2]
                        nc.gpsimd.tensor_tensor(dst.rearrange("p h b t -> p (h b t)"),
                                                rope_a[:, n % 2], rope_b[:, n % 2], ALU.add)\
                            .then_inc(rotated, 1)

                    for j in range(KB):
                        rotate("k", j)
                    for j in range(2):
                        rotate("q", j)
                    for u in range(UNITS):
                        for j in q_banks(u):
                            rotate("q", j)
                        for c in range(2):
                            hold_apart(pool, exp_done, now(it, 2 * UNITS, 2 * u + c + 1), apart)
                            part = probs[:, u % 2, c].rearrange("p (h t) -> p h t", h=GROUP)
                            sign = 1 if c == 0 else -1
                            nc.gpsimd.affine_select(out=part, in_=part, compare_op=ALU.is_ge, fill=0.0,
                                                    base=0, pattern=[[0, GROUP], [sign, P]],
                                                    channel_multiplier=-sign).then_inc(masked, 1)

            @block.tensor
            def _(pe):
                pe.sem_inc(proj_done, BANKS)
                pe.sem_inc(pv_done, UNITS)
                pe.sem_inc(turn_done, UNITS)
                pe.sem_inc(y_done, 1)
                pe.wait_ge(w_in, LOADS)
                with pe.Fori(0, TILES) as it:
                    pe.wait_ge(xs_ready, now(it, 1, 1))

                    def free_bank(n):
                        n -= 2
                        back = n < 0
                        n %= BANKS
                        at = before if back else (lambda i, per, m: now(i, per, m, credit=True))
                        if KB <= n < KB + NB:
                            pe.wait_ge(v_ready, at(it, NB, n - KB + 1))
                        else:
                            pe.wait_ge(roped, at(it, ROPES, (n if n < KB else n - NB) + 1))

                    def project(w, n, j):
                        free_bank(n)
                        for h in range(2):
                            for k in range(KC):
                                ins = nc.tensor.matmul(proj[:, n % 2, h * NB * P:(h + 1) * NB * P],
                                                       w[:, k, (2 * j + h) * HD:(2 * j + h + 1) * HD],
                                                       xs[:, k].rearrange("p b t -> p (b t)"),
                                                       start=(k == 0), stop=(k == KC - 1))
                        ins.then_inc(proj_done, 1)

                    for j in range(KB):
                        project(W.k, j, j)
                    for b in range(NB):
                        n = KB + b
                        free_bank(n)
                        for k in range(KC):
                            ins = nc.tensor.matmul(proj[:, n % 2], xs[:, k, b], W.v[:, k, :],
                                                   start=(k == 0), stop=(k == KC - 1))
                        ins.then_inc(proj_done, 1)
                    for j in range(2):
                        project(W.q, KB + NB + j, j)

                    def scores(u):
                        g, b = u // NB, u % NB
                        pe.wait_ge(rotated, now(it, ROPES, n_rope["q", 2 * g + 1], credit=True))
                        for c in range(2):
                            if u:
                                pe.wait_ge(tanh_done, now(it, 2 * UNITS, 2 * (u - 1) + c + 1, credit=True))
                            else:
                                pe.wait_ge(tanh_done, before(it, 2 * UNITS, 2 * (UNITS - 1) + c + 1))
                            nc.tensor.matmul(score[:, c], kT[:, c, g, b],
                                             qT[:, g * GROUP:(g + 1) * GROUP, b, :],
                                             start=True, stop=True).then_inc(score_done, 1)

                    def weigh(u):
                        g, b = u // NB, u % NB
                        pe.wait_ge(masked, now(it, 2 * UNITS, 2 * u + 2))
                        if u == 0:
                            pe.wait_ge(v_ready, now(it, NB, NB, credit=True))
                            pe.wait_ge(moved, now(it, 1, 1))
                            pe.wait_ge(rotated, now(it, ROPES, 1, credit=True))
                        if u:
                            pe.wait_ge(enc_done, now(it, UNITS, u, credit=True))
                        else:
                            pe.wait_ge(enc_done, before(it, UNITS, UNITS))
                        for h in range(GROUP):
                            at = (h % 2) * (HD + 1)
                            for c in range(2):
                                ins = nc.tensor.matmul(pv[:, h // 2, at:at + HD + 1],
                                                       probs[:, u % 2, c, h * P:(h + 1) * P],
                                                       v[:, c, b, g, :], start=(c == 0), stop=(c == 1))
                        ins.then_inc(pv_done, 1)

                    def turn(u):
                        pe.wait_ge(enc_done, now(it, UNITS, u + 1, credit=True))
                        if u:
                            pe.wait_ge(encT_done, now(it, UNITS, u, credit=True))
                        else:
                            pe.wait_ge(encT_done, before(it, UNITS, UNITS))
                        for h in range(GROUP):
                            ins = nc.tensor.transpose(turned[:, h * P:(h + 1) * P], enc[:, u % 2, h], G.ident[:])
                        ins.then_inc(turn_done, 1)

                    for u in range(UNITS):
                        scores(u)
                        for j in q_banks(u):
                            project(W.q, KB + NB + j, j)
                        if u >= 1:
                            weigh(u - 1)
                        if u >= 2:
                            turn(u - 2)
                    weigh(UNITS - 1)
                    turn(UNITS - 2)
                    turn(UNITS - 1)
                    pe.wait_ge(encT_done, now(it, UNITS, UNITS, credit=True))
                    pe.wait_ge(x_added, before(it, 1, 1))
                    for b in range(NB):
                        for h in range(NH):
                            ins = nc.tensor.matmul(y[:, b], encT[:, b, h], W.o[:, h], start=(h == 0), stop=(h == NH - 1))
                    ins.then_inc(y_done, 1)

            @block.scalar
            def _(act):
                act.sem_inc(v_ready, NB)
                act.sem_inc(tanh_done, 2 * UNITS)
                act.sem_inc(encT_done, UNITS)
                with act.Fori(0, TILES) as it:
                    for b in range(NB):
                        act.wait_ge(proj_done, now(it, BANKS, KB + b + 1, credit=True))
                        if b == 0:
                            act.wait_ge(moved, now(it, 1, 1))
                        nc.scalar.copy(v[:, 0, b, :, 0:HD], proj[:, (KB + b) % 2].rearrange("p (g d) -> p g d", g=NKV))\
                            .then_inc(v_ready, 1)

                    def softmax_part(u):
                        for c in range(2):
                            act.wait_ge(score_done, now(it, 2 * UNITS, 2 * u + c + 1))
                            if u:
                                act.wait_ge(exp_done, now(it, 2 * UNITS, 2 * (u - 1) + c + 1))
                            nc.scalar.activation(capped[:, c], score[:, c], ACT.Tanh, scale=SCALE).then_inc(tanh_done, 1)
                        for c in range(2):
                            act.wait_ge(tanh_done, now(it, 2 * UNITS, 2 * u + c + 1, credit=True))
                            if c == 0:
                                act.wait_ge(pv_done, now(it, UNITS, u - 1, credit=True))
                            nc.scalar.activation(probs[:, u % 2, c], capped[:, c], ACT.Exp, scale=CAP)\
                                .then_inc(exp_done, 1)

                    def evacuate(u):
                        g, b = u // NB, u % NB
                        act.wait_ge(turn_done, now(it, UNITS, u + 1, credit=True))
                        if u == 0:
                            act.wait_ge(y_done, before(it, 1, 1))
                        nc.scalar.copy(encT[:, b, g * GROUP:(g + 1) * GROUP].rearrange("p h t -> p (h t)"), turned[:])\
                            .then_inc(encT_done, 1)

                    for u in range(UNITS):
                        softmax_part(u)
                        if u >= 2:
                            evacuate(u - 2)
                    evacuate(UNITS - 2)
                    evacuate(UNITS - 1)

            @block.vector
            def _(dve):
                dve.sem_inc(roped, ROPES)
                dve.sem_inc(enc_done, UNITS)
                dve.sem_inc(x_added, 1)
                dve.wait_ge(w_in, LOADS)
                H = HD // 2
                with dve.Fori(0, TILES) as it:
                    steps = Steps(dve, dve_steps, it, UNITS)
                    cos = spread(W.cos[:, bass.ds(it * P, P)].unsqueeze(1), [P, 4, P])
                    sin = W.sin[:, bass.ds(it * P, P)].unsqueeze(1)

                    def rope(kind, j):
                        n = n_rope[kind, j]
                        bank = (j if kind == "k" else KB + NB + j)
                        dve.wait_ge(proj_done, now(it, BANKS, bank + 1, credit=True))
                        dve.wait_ge(rotated, now(it, ROPES, n - 2, credit=True))
                        src = proj[:, bank % 2].rearrange("p (r t) -> p r t", t=P)
                        a = rope_a[:, n % 2].rearrange("p (r t) -> p r t", t=P)
                        b = rope_b[:, n % 2].rearrange("p (r t) -> p r t", t=P)
                        nc.vector.tensor_tensor(a, src, cos, ALU.mult)
                        nc.vector.tensor_tensor(b[0:H], src[H:HD], spread(sin[H:HD], [H, 4, P]), ALU.mult)
                        nc.vector.tensor_tensor(b[H:HD], src[0:H], spread(sin[0:H], [H, 4, P]), ALU.mult)\
                            .then_inc(roped, 1)

                    def normalise(u):
                        dve.wait_ge(pv_done, now(it, UNITS, u + 1, credit=True))
                        dve.wait_ge(turn_done, now(it, UNITS, u - 1, credit=True))
                        rows = pv[:, :, 0:2 * (HD + 1)].rearrange("p a (h d) -> p a h d", h=2)
                        r = rden[:].rearrange("p (a h d) -> p a h d", a=2, h=2)
                        steps.then(nc.vector.reciprocal(r, rows[:, :, :, HD:HD + 1]))
                        nc.vector.tensor_tensor(enc[:, u % 2].rearrange("p (a h) d -> p a h d", a=2),
                                                rows[:, :, :, 0:HD], spread(r, [P, 2, 2, HD]), ALU.mult)\
                            .then_inc(enc_done, 1)

                    for j in range(KB):
                        rope("k", j)
                    for j in range(2):
                        rope("q", j)
                    for u in range(UNITS):
                        for j in q_banks(u):
                            rope("q", j)
                        if u >= 1:
                            normalise(u - 1)
                    normalise(UNITS - 1)
                    dve.wait_ge(y_done, now(it, 1, 1, credit=True))
                    x_tile = G.x[:, :, bass.ds(it, 1), :].rearrange("p b i d -> p b (i d)")
                    nc.vector.tensor_tensor(x_tile, y[:], x_tile, ALU.add).then_inc(x_added, 1)
                    steps.close()



def staged_linear(nc, G, tag, wT, bias, w_in=None, loads=0):
    PAIRS = 2
    with Phase(nc, tag) as ph:
        xs = ph.sb("xs", [P, PAIRS, KC, NB, P])
        y = [ph.ps(f"y{j}", [P, NB, D]) for j in range(PAIRS)]
        xs_ready = ph.sem("xs_ready")
        y_done = ph.sem("y_done")
        x_added = ph.sem("x_added")
        dve_steps = ph.sem("dve_steps")
        apart = ph.sem("apart")
        with ph.block() as block:
            @block.gpsimd
            def _(pool):
                with pool.Fori(0, TILES // PAIRS) as it:
                    for j in range(PAIRS):
                        hold_apart(pool, y_done, before(it, PAIRS, j + 1), apart)
                        nc.gpsimd.tensor_copy(xs[:, j], G.xnT[:, :, :, bass.ds((it * PAIRS + j) * P, P)])\
                            .then_inc(xs_ready, 1)

            @block.tensor
            def _(pe):
                pe.sem_inc(y_done, PAIRS)
                if w_in is not None:
                    pe.wait_ge(w_in, loads)
                with pe.Fori(0, TILES // PAIRS) as it:
                    for j in range(PAIRS):
                        pe.wait_ge(xs_ready, now(it, PAIRS, j + 1))
                        pe.wait_ge(x_added, before(it, PAIRS, j + 1))
                        for b in range(NB):
                            for k in range(KC):
                                ins = nc.tensor.matmul(y[j][:, b], xs[:, j, k, b], wT[:, k], start=(k == 0), stop=(k == KC - 1))
                        ins.then_inc(y_done, 1)

            @block.vector
            def _(dve):
                dve.sem_inc(x_added, PAIRS)
                if w_in is not None:
                    dve.wait_ge(w_in, loads)
                with dve.Fori(0, TILES // PAIRS) as it:
                    steps = Steps(dve, dve_steps, it, PAIRS if bias is not None else 0)
                    for j in range(PAIRS):
                        dve.wait_ge(y_done, now(it, PAIRS, j + 1, credit=True))
                        x_tile = G.x[:, :, bass.ds(it * PAIRS + j, 1), :].rearrange("p b i d -> p b (i d)")
                        if bias is not None:
                            steps.then(nc.vector.tensor_tensor(x_tile, x_tile, spread(bias[:].unsqueeze(1), [P, NB, D]), ALU.add))
                        nc.vector.tensor_tensor(x_tile, y[j][:], x_tile, ALU.add).then_inc(x_added, 1)
                    steps.close()


def l0_ffn(nc, G):
    with Phase(nc, "f0w") as W:
        w = W.sb("w", [P, KC, D])
        bias = W.sb("bias", [P, D])
        wT = W.sb("wT", [P, KC, D])
        w_in = W.sem("w_in")

        def load(sp):
            sp.dma_start(w[:], G.dram["L0_ffn_weight"].rearrange("(k p) n -> p k n", p=P)).then_inc(w_in, 16)
            sp.dma_start(bias[:], G.dram["L0_ffn_bias"].partition_broadcast(P)).then_inc(w_in, 16)
        norm_phase(nc, G, "f0n", load=load)
        with Phase(nc, "f0b") as ph:
            alpha = ph.sb("alpha", [P, KC])
            bw = ph.sb("bw", [P, KC, D])
            turned = ph.ps("turned", [P, KC, D])
            steps_sem, bw_ready, turn_done = ph.sem("steps"), ph.sem("bw_ready"), ph.sem("turn_done")
            with ph.block() as block:
                @block.vector
                def _(dve):
                    steps = Steps(dve, steps_sem)
                    dve.wait_ge(w_in, 2 * 16)
                    nc.vector.tensor_reduce(alpha[:], w[:], AX.X, ALU.add, apply_absolute_value=True)
                    steps.then(nc.vector.tensor_scalar(bw[:], w[:], 0.0, 2.0, ALU.is_ge, ALU.mult))
                    steps.then(nc.vector.tensor_scalar(alpha[:], alpha[:], 1.0 / D, None, ALU.mult))
                    for k in range(KC):
                        n = steps.mark(nc.vector.tensor_scalar(bw[:, k], bw[:, k], -1.0, alpha[:, k:k + 1], ALU.add, ALU.mult))
                    steps.hold(n)
                    steps.then(nc.vector.tensor_tensor(bw[:], bw[:], w[:], ALU.subtract))
                    nc.vector.tensor_tensor(bw[:], bw[:], w[:], ALU.add).then_inc(bw_ready, 1)
                    dve.wait_ge(turn_done, 1)
                    nc.vector.tensor_copy(wT[:], turned[:])

                @block.tensor
                def _(pe):
                    pe.wait_ge(bw_ready, 1)
                    for k in range(KC):
                        for o in range(KC):
                            ins = nc.tensor.transpose(turned[:, k, o * P:(o + 1) * P], bw[:, o, k * P:(k + 1) * P], G.ident[:])
                    ins.then_inc(turn_done, 1)
        staged_linear(nc, G, "f0l", wT, bias)


QL, KVL, DR, DK, DV = 192, 64, 64, 128, 128
PAIRS = NH // 2
QREST = QL - P
IH, ID, TOPK = 8, 128, 8
SEL = IH * TOPK
BIG = -1e30


def load_l1_attn(nc, G, W, sem):
    def load(sp):
        I = G.dram
        for dst, src in ((W.early["qcT"][:], I["l1_qcT"]), (W.early["kcT"][:], I["l1_kcT"]), (W.early["vT"][:], I["l1_vT"]),
                         (W.early["o"][:], I["L1_attn_W_o"].rearrange("(h p) n -> p h n", p=P)),
                         (W.q0[:, :, 0:2 * P], I["l1_qr"][0:P]), (W.q1[:, :, 0:2 * P], I["l1_qr"][P:QL]),
                         (W.early["k"][:], I["l1_k"].rearrange("(k p) n -> p k n", p=P)),
                         (W.early["cp"][:], I["L1_attn_W_cp"].rearrange("(k p) n -> p k n", p=P)),
                         (W.early["gate"][:], I["L1_attn_W_gate"].rearrange("(k p) n -> p k n", p=P)),
                         (W.early["idx"][:], I["L1_attn_W_idx"].rearrange("(k p) n -> p k n", p=P)),
                         (W.early["sq"][:], I["L1_attn_W_sq"]), (W.early["sk"][:], I["L1_attn_W_sk"]), (W.early["sv"][:], I["L1_attn_W_sv"]),
                         (W.early["iout"][:], I["L1_attn_W_iout"][:, 0:DV]),
                         (W.cos[:], I["l1_cos"]), (W.sin[:], I["l1_sin"]),
                         (W.early["iota"][:], I["l1_iota"]), (W.early["same"][:], I["l1_same"]), (W.early["mean"][:], I["l1_mean"])):
            sp.dma_start(dst, src).then_inc(sem, 16)
            W.loads += 16
    return load


def l1_attn(nc, G):
    with Phase(nc, "l1w") as W:
        W.loads = 0
        W.q0 = W.sb("q0", [P, PAIRS, 3 * P])
        W.q1 = W.sb("q1", [QREST, PAIRS, 3 * P])
        W.m = W.sb("m", [P, PAIRS, D])
        W.cos = W.sb("cos", [P, SEQ])
        W.sin = W.sb("sin", [P, SEQ])
        W.kA = W.sb("kA", [P, NB, SEQ])
        W.kB = W.sb("kB", [P, NB, SEQ])
        W.cp0 = W.sb("cp0", [P, NB, SEQ])
        W.cp1 = W.sb("cp1", [QREST, NB, SEQ])
        W.c = W.sb("c", [P, NB, TILES, KVL + 1])
        W.row = W.sb("row", [P, NB, D])
        W.w_in = W.sem("w_in")
        with Phase(nc, "l1v") as V:
            for name, shape in (("qcT", [P, NH, QL]), ("kcT", [P, NH, KVL]), ("vT", [P, NH, KVL]), ("o", [P, NH, D]),
                                ("k", [P, KC, 3 * DR]), ("cp", [P, KC, QL]), ("gate", [P, KC, IH]),
                                ("idx", [P, KC, IH * ID]), ("sq", [ID, ID]), ("sk", [ID, ID]), ("sv", [ID, ID]),
                                ("iout", [ID, DV]), ("iota", [P, TILES]), ("same", [P, P]), ("mean", [P, NB * IH]),
                                ("xn", [P, NB, TILES, D]), ("gateT", [IH, NB, SEQ])):
                V.sb(name, shape)
            W.early = V
            norm_phase(nc, G, "l1n", load=load_l1_attn(nc, G, W, W.w_in), keep=W.early["xn"])
            l1_weights(nc, G, W)
            l1_latents(nc, G, W)
            l1_sparse(nc, G, W)
        for b in range(NB):
            with Phase(nc, f"l1q{b}") as Q:
                Q.q = Q.sb("q", [P, PAIRS, 2, SEQ])
                l1_queries(nc, G, W, Q, b)
                l1_attend(nc, G, W, Q, b)


def l1_weights(nc, G, W):
    with Phase(nc, "l1p") as ph:
        ab = ph.ps("ab", [P, 2, BLK])
        rest = ph.ps("rest", [QREST, 2, BLK])
        m = ph.ps("m", [P, PAIRS // 2, 2, D])
        made = ph.sem("made")
        with ph.block() as block:
            @block.tensor
            def _(pe):
                pe.wait_ge(W.w_in, W.loads)
                for h in range(NH):
                    pair, odd = h // 2, h % 2
                    at = (pair % 4) * P + (0 if odd else KVL)
                    nc.tensor.matmul(ab[:, pair // 4, at:at + KVL], W.early["qcT"][:, h, 0:P], W.early["kcT"][:, h], start=True, stop=True)
                    nc.tensor.matmul(rest[:, pair // 4, at:at + KVL], W.early["qcT"][:, h, P:QL], W.early["kcT"][:, h], start=True, stop=True)
                    ins = nc.tensor.matmul(m[odd * KVL:(odd + 1) * KVL, pair // 2, pair % 2], W.early["vT"][:, h], W.early["o"][:, h],
                                           start=True, stop=True)
                ins.then_inc(made, 1)

            @block.scalar
            def _(act):
                act.wait_ge(made, 1)
                nc.scalar.copy(W.m[:], m[:].rearrange("p a b n -> p (a b) n"))

            @block.vector
            def _(dve):
                dve.wait_ge(W.w_in, W.loads)
                dve.wait_ge(made, 1)
                nc.vector.tensor_copy(W.q0[:, :, 2 * P:3 * P], ab[:].rearrange("p a (b n) -> p (a b) n", n=P))
                nc.vector.tensor_copy(W.q1[:, :, 2 * P:3 * P], rest[:].rearrange("p a (b n) -> p (a b) n", n=P))


def l1_latents(nc, G, W):
    with Phase(nc, "l1l") as ph:
        xs = ph.sb("xs", [P, KC, BLK])
        rope_a = ph.sb("rope_a", [DR, BLK])
        rope_b = ph.sb("rope_b", [DR, BLK])
        key = ph.ps("key", [P, BLK])
        swapped = ph.ps("swapped", [DR, BLK])
        cp0, cp1 = ph.ps("cp0", [P, BLK]), ph.ps("cp1", [QREST, BLK])
        gate = ph.ps("gate", [IH, BLK])
        ctok = ph.ps("ctok", [P, TPB, KVL])
        xs_ready = ph.sem("xs_ready")
        key_done = ph.sem("key_done")
        all_done = ph.sem("all_done")
        act_done = ph.sem("act_done")
        dve_done = ph.sem("dve_done")
        dve_steps = ph.sem("dve_steps")
        apart = ph.sem("apart")
        flat = lambda t: t[:].rearrange("p b t -> p (b t)")
        xnT = G.xnT[:].rearrange("p k b t -> p k (b t)")
        c_flat = W.c[:].rearrange("p b i d -> p (b i) d")
        with ph.block() as block:
            @block.gpsimd
            def _(pool):
                nc.gpsimd.memset(W.c[:, :, :, KVL:KVL + 1], 1.0)
                with pool.Fori(0, BLOCKS) as it:
                    hold_apart(pool, all_done, before(it, 1, 1), apart)
                    nc.gpsimd.tensor_copy(xs[:], xnT[:, :, bass.ds(it * BLK, BLK)]).then_inc(xs_ready, 1)

            @block.tensor
            def _(pe):
                pe.sem_inc(all_done, 1)
                pe.wait_ge(W.w_in, W.loads)
                with pe.Fori(0, BLOCKS) as it:
                    def product(out, w):
                        for k in range(KC):
                            ins = nc.tensor.matmul(out, w(k), xs[:, k], start=(k == 0), stop=(k == KC - 1))
                        return ins
                    pe.wait_ge(xs_ready, now(it, 1, 1))
                    pe.wait_ge(act_done, before(it, 1, 1))
                    pe.wait_ge(dve_done, before(it, 1, 1))
                    product(key[:], lambda k: W.early["k"][:, k, 0:P])
                    product(swapped[:], lambda k: W.early["k"][:, k, P:P + DR]).then_inc(key_done, 1)
                    product(cp0[:], lambda k: W.early["cp"][:, k, 0:P])
                    product(cp1[:], lambda k: W.early["cp"][:, k, P:QL])
                    product(gate[:], lambda k: W.early["gate"][:, k])
                    for j in range(TPB):
                        for k in range(KC):
                            ins = nc.tensor.matmul(ctok[:, j], xs[:, k, j * P:(j + 1) * P], W.early["k"][:, k, DR:P],
                                                   start=(k == 0), stop=(k == KC - 1))
                    ins.then_inc(all_done, 1)

            @block.scalar
            def _(act):
                act.sem_inc(act_done, 1)
                with act.Fori(0, BLOCKS) as it:
                    cols = bass.ds(it * BLK, BLK)
                    act.wait_ge(key_done, now(it, 1, 1))
                    nc.scalar.copy(flat(W.kA)[DR:P, cols], key[DR:P])
                    nc.scalar.copy(flat(W.kB)[0:KVL, cols], key[DR:P])
                    act.wait_ge(all_done, now(it, 1, 1, credit=True))
                    nc.scalar.copy(flat(W.cp0)[:, cols], cp0[:])
                    nc.scalar.copy(flat(W.cp1)[:, cols], cp1[:])
                    nc.scalar.copy(flat(W.early["gateT"])[:, cols], gate[:])
                    nc.scalar.copy(c_flat[:, bass.ds(it * TPB, TPB), 0:KVL], ctok[:]).then_inc(act_done, 1)

            @block.vector
            def _(dve):
                dve.sem_inc(dve_done, 1)
                dve.wait_ge(W.w_in, W.loads)
                with dve.Fori(0, BLOCKS) as it:
                    steps = Steps(dve, dve_steps, it, 1)
                    cols = bass.ds(it * BLK, BLK)
                    pos = bass.ds((it % BPB) * BLK, BLK)
                    dve.wait_ge(key_done, now(it, 1, 1))
                    nc.vector.tensor_tensor(rope_a[:], key[0:DR], W.cos[0:DR, pos], ALU.mult)
                    steps.then(nc.vector.tensor_tensor(rope_b[:], swapped[:], W.sin[0:DR, pos], ALU.mult))
                    nc.vector.tensor_tensor(flat(W.kA)[0:DR, cols], rope_a[:], rope_b[:], ALU.add)
                    nc.vector.tensor_tensor(flat(W.kB)[DR:P, cols], rope_a[:], rope_b[:], ALU.add).then_inc(dve_done, 1)
                    steps.close()


def l1_sparse(nc, G, W):
    with Phase(nc, "l1s") as ph:
        top = ph.sb("top", [IH, NB, TOPK])
        index = ph.sb("index", [IH, NB, TOPK], U32)
        index_f = ph.sb("index_f", [IH, NB, TOPK])
        own = ph.sb("own", [IH, NB, IH, TOPK])
        ones = ph.sb("ones", [IH, P])
        pick = ph.sb("pick", [P, NB, TILES, SEL])
        selx = ph.sb("selx", [P, KC, NB, SEL])
        selT = ph.sb("selT", [ID, IH, NB * TOPK])
        sqT, skT, sv = (ph.sb(n, [P, P]) for n in ("sqT", "skT", "sv"))
        logits = ph.sb("logits", [P, P])
        top1 = ph.sb("top1", [P, 1])
        total = ph.sb("total", [P, 1])
        probs = ph.sb("probs", [P, P])
        weight = ph.sb("weight", [P, NB * IH])
        outT = ph.sb("outT", [P, NB * IH])
        ioT = ph.sb("ioT", [P, NB * IH])
        index_p = ph.ps("index_p", [P, NB, SEL])
        selx_p = ph.ps("selx_p", [P, KC, NB, SEL])
        selT_p = ph.ps("selT_p", [ID, IH, NB * TOPK])
        work = ph.ps("work", [P, 4, P])
        row_p = ph.ps("row_p", [P, NB, D])
        dve_sem, pe_sem = ph.sem("dve"), ph.sem("pe")
        exp_done = ph.sem("exp_done")
        marks = {}
        with ph.block() as block:
            @block.vector
            def _(dve):
                steps = Steps(dve, dve_sem)
                nc.vector.memset(ones[:], 1.0)
                for b in range(NB):
                    steps.then(nc.vector.max(top[:, b], W.early["gateT"][:, b]))
                    steps.then(nc.vector.max_index(index[:, b], top[:, b], W.early["gateT"][:, b]))
                steps.then(nc.vector.tensor_copy(index_f[:], index[:]))
                for b in range(NB):
                    n = steps.mark(nc.vector.tensor_tensor(
                        own[:, b], spread(index_f[:, b].unsqueeze(1), [IH, IH, TOPK]),
                        spread(G.ident[0:IH, 0:IH].unsqueeze(2), [IH, IH, TOPK]), ALU.mult))
                marks["own"] = n
                dve.wait_ge(pe_sem, 1)
                for i in range(TILES):
                    n = steps.mark(nc.vector.tensor_scalar(pick[:, :, i], index_p[:], W.early["iota"][:, i:i + 1], None, ALU.is_equal))
                marks["pick"] = n

                def copy(name, dst, src, after):
                    dve.wait_ge(pe_sem, after)
                    marks[name] = steps.mark(nc.vector.tensor_copy(dst, src))
                copy("selx", selx[:], selx_p[:], 2)
                copy("selT", selT[:], selT_p[:], 3)
                dve.wait_ge(pe_sem, 4)
                nc.vector.tensor_copy(sqT[:], work[:, 0])
                nc.vector.tensor_copy(skT[:], work[:, 1])
                copy("sqkv", sv[:], work[:, 2], 4)
                dve.wait_ge(pe_sem, 5)
                steps.then(nc.vector.scalar_tensor_tensor(logits[:], work[:, 3], float(ID) ** -0.5, W.early["same"][:], ALU.mult, ALU.add))
                steps.then(nc.vector.tensor_reduce(top1[:], logits[:], AX.X, ALU.max, negate=True))
                marks["top1"] = steps.n
                dve.wait_ge(exp_done, 1)
                steps.then(nc.vector.reciprocal(total[:], total[:]))
                marks["probs"] = steps.mark(nc.vector.tensor_scalar(probs[:], probs[:], total[:], None, ALU.mult))
                copy("weight", weight[:], work[:, 0, 0:NB * IH], 6)
                copy("outT", outT[:], work[:, 1, 0:NB * IH], 7)
                copy("ioT", ioT[:], work[:, 2, 0:NB * IH], 8)
                dve.wait_ge(pe_sem, 9)
                nc.vector.tensor_copy(W.row[:], row_p[:])

            @block.scalar
            def _(act):
                act.wait_ge(dve_sem, marks["top1"])
                nc.scalar.activation(probs[:], logits[:], ACT.Exp, bias=top1[:], accum_out=total[:]).then_inc(exp_done, 1)

            @block.tensor
            def _(pe):
                pe.wait_ge(dve_sem, marks["own"])
                for b in range(NB):
                    ins = nc.tensor.matmul(index_p[:, b], ones[:], own[:, b].rearrange("p h k -> p (h k)"), start=True, stop=True)
                ins.then_inc(pe_sem, 1)
                pe.wait_ge(dve_sem, marks["pick"])
                for b in range(NB):
                    for k in range(KC):
                        for i in range(TILES):
                            ins = nc.tensor.matmul(selx_p[:, k, b], W.early["xn"][:, b, i, k * P:(k + 1) * P], pick[:, b, i],
                                                   start=(i == 0), stop=(i == TILES - 1))
                ins.then_inc(pe_sem, 1)
                pe.wait_ge(dve_sem, marks["selx"])
                for h in range(IH):
                    for k in range(KC):
                        ins = nc.tensor.matmul(selT_p[:, h], W.early["idx"][:, k, h * ID:(h + 1) * ID],
                                               selx[:, k, :, h * TOPK:(h + 1) * TOPK], start=(k == 0), stop=(k == KC - 1))
                ins.then_inc(pe_sem, 1)
                pe.wait_ge(dve_sem, marks["selT"])
                sel = selT[:].rearrange("p h r -> p (h r)")
                nc.tensor.matmul(work[:, 0], W.early["sq"][:], sel, start=True, stop=True)
                nc.tensor.matmul(work[:, 1], W.early["sk"][:], sel, start=True, stop=True)
                nc.tensor.matmul(work[:, 2], sel, W.early["sv"][:], start=True, stop=True).then_inc(pe_sem, 1)
                pe.wait_ge(dve_sem, marks["sqkv"])
                nc.tensor.matmul(work[:, 3], sqT[:], skT[:], start=True, stop=True).then_inc(pe_sem, 1)
                pe.wait_ge(dve_sem, marks["probs"])
                nc.tensor.matmul(work[:, 0, 0:NB * IH], probs[:], W.early["mean"][:], start=True, stop=True).then_inc(pe_sem, 1)
                pe.wait_ge(dve_sem, marks["weight"])
                nc.tensor.matmul(work[:, 1, 0:NB * IH], sv[:], weight[:], start=True, stop=True).then_inc(pe_sem, 1)
                pe.wait_ge(dve_sem, marks["outT"])
                nc.tensor.matmul(work[:, 2, 0:NB * IH], W.early["iout"][:], outT[:], start=True, stop=True).then_inc(pe_sem, 1)
                pe.wait_ge(dve_sem, marks["ioT"])
                for b in range(NB):
                    for h in range(NH):
                        at = (h // (NH // IH)) * NB + b
                        ins = nc.tensor.matmul(row_p[:, b], spread(ioT[:, at:at + 1], [P, P]), W.early["o"][:, h],
                                               start=(h == 0), stop=(h == NH - 1))
                ins.then_inc(pe_sem, 1)


def l1_queries(nc, G, W, Q, b):
    with Phase(nc, f"l1r{b}") as ph:
        rope_a = ph.sb("rope_a", [P, 2, BLK])
        rope_b = ph.sb("rope_b", [P, 2, BLK])
        rotary = [ph.ps(f"rotary{j}", [P, BLK]) for j in range(2)]
        swapped = [ph.ps(f"swapped{j}", [P, BLK]) for j in range(2)]
        latent = [ph.ps(f"latent{j}", [P, BLK]) for j in range(2)]
        rope_in = ph.sem("rope_in")
        latent_in = ph.sem("latent_in")
        roped = ph.sem("roped")
        added = ph.sem("added")
        copied = ph.sem("copied")
        with ph.block() as block:
            @block.tensor
            def _(pe):
                with pe.Fori(0, BPB) as it:
                    for p in range(PAIRS):
                        def product(out, part):
                            nc.tensor.matmul(out[:], W.q0[:, p, part * P:(part + 1) * P],
                                             W.cp0[:, b, bass.ds(it * BLK, BLK)], start=True, stop=False)
                            return nc.tensor.matmul(out[:], W.q1[:, p, part * P:(part + 1) * P],
                                                    W.cp1[:, b, bass.ds(it * BLK, BLK)], start=False, stop=True)
                        pe.wait_ge(roped, it * PAIRS + p + 1)
                        product(rotary[p % 2], 0)
                        product(swapped[p % 2], 1).then_inc(rope_in, 1)
                        pe.wait_ge(copied, it * PAIRS + p + 1)
                        product(latent[p % 2], 2).then_inc(latent_in, 1)

            @block.vector
            def _(dve):
                dve.sem_inc(roped, 2)
                with dve.Fori(0, BPB) as it:
                    pos = bass.ds(it * BLK, BLK)
                    for p in range(PAIRS):
                        dve.wait_ge(rope_in, now(it, PAIRS, p + 1))
                        dve.wait_ge(added, it * PAIRS + p + 1)
                        nc.vector.tensor_tensor(rope_a[:, p % 2], rotary[p % 2][:], W.cos[:, pos], ALU.mult)
                        nc.vector.tensor_tensor(rope_b[:, p % 2], swapped[p % 2][:], W.sin[:, pos], ALU.mult).then_inc(roped, 1)

            @block.gpsimd
            def _(pool):
                pool.sem_inc(added, 2)
                with pool.Fori(0, BPB) as it:
                    for p in range(PAIRS):
                        pool.wait_ge(roped, it * PAIRS + p + 3)
                        for odd in range(2):
                            half = slice(odd * DR, (odd + 1) * DR)
                            ins = nc.gpsimd.tensor_tensor(Q.q[half, p, odd, bass.ds(it * BLK, BLK)],
                                                          rope_a[half, p % 2], rope_b[half, p % 2], ALU.add)
                        ins.then_inc(added, 1)

            @block.scalar
            def _(act):
                act.sem_inc(copied, 2)
                with act.Fori(0, BPB) as it:
                    for p in range(PAIRS):
                        act.wait_ge(latent_in, now(it, PAIRS, p + 1))
                        nc.scalar.copy(Q.q[KVL:P, p, 0, bass.ds(it * BLK, BLK)], latent[p % 2][KVL:P])
                        nc.scalar.copy(Q.q[0:KVL, p, 1, bass.ds(it * BLK, BLK)], latent[p % 2][0:KVL]).then_inc(copied, 1)


def l1_attend(nc, G, W, Q, b):
    with Phase(nc, f"l1a{b}") as ph:
        qs = ph.sb("qs", [P, 2, P])
        neg_max = ph.sb("neg_max", [P, 2])
        shift = ph.sb("shift", [P, 2])
        probs = ph.sb("probs", [P, 2, SEQ])
        probsT = ph.sb("probsT", [P, 2, TILES, P])
        rden = ph.sb("rden", [P, 2])
        pc = ph.sb("pc", [P, 2, NH, KVL])
        pcT = ph.sb("pcT", [P, PAIRS, P])
        identb = ph.sb("identb", [P, P], BF16)
        future = ph.sb("future", [P, P], BF16)
        score = [ph.ps(f"score{j}", [P, SEQ]) for j in range(2)]
        turned = [ph.ps(f"turned{j}", [P, BLK]) for j in range(2)]
        pv = [ph.ps(f"pv{j}", [P, BLK]) for j in range(2)]
        const = ph.sem("const")
        qs_ready = ph.sem("qs_ready")
        score_done = ph.sem("score_done")
        max_done = ph.sem("max_done")
        shift_ready = ph.sem("shift_ready")
        exp_done = ph.sem("exp_done")
        turn_done = [ph.sem(f"turn_done{j}") for j in range(2)]
        evac = [ph.sem(f"evac{j}") for j in range(2)]
        pv_done = ph.sem("pv_done")
        rden_done = ph.sem("rden_done")
        pc_done = ph.sem("pc_done")
        y_done = ph.sem("y_done")
        x_added = ph.sem("x_added")
        row_added = ph.sem("row_added")
        SCALE = 1.0 / float(np.sqrt(DK + DR))
        CHUNK = 4

        def chunks(i):
            return -(-(i + 1) // CHUNK)

        uses = [1]
        for i in range(TILES):
            uses.append(uses[-1] + (NH // 2 if chunks(i) == 1 else NH) + 1)

        def use(i, it, k, c):
            return uses[i] + (it if chunks(i) == 1 else 2 * it + k)

        with ph.block() as block:
            def tile_loop(eng, i, body):
                with eng.Fori(0, PAIRS - 1) as it:
                    body(i, it, False)
                body(i, PAIRS - 1, True)

            @block.gpsimd
            def _(pool):
                nc.gpsimd.memset(identb[:], 0.0).then_inc(const, 1)
                nc.gpsimd.memset(future[:], 0.0).then_inc(const, 1)
                pool.wait_ge(const, 2)
                nc.gpsimd.affine_select(out=identb[:], in_=identb[:], compare_op=ALU.not_equal, fill=1.0,
                                        base=0, pattern=[[-1, P]], channel_multiplier=1).then_inc(const, 1)
                nc.gpsimd.affine_select(out=future[:], in_=future[:], compare_op=ALU.is_ge, fill=BIG,
                                        base=0, pattern=[[-1, P]], channel_multiplier=1).then_inc(const, 1)

                def stage(i, pair, k, n):
                    if not isinstance(n, int) or n >= 2:
                        hold_apart(pool, score_done, n - 1, const)
                    nc.gpsimd.tensor_copy(qs[:, k], Q.q[:, pair, k, i * P:(i + 1) * P]).then_inc(qs_ready, 1)

                for i in range(TILES):
                    for k in range(2):
                        stage(i, 0, k, NH * i + k)

                    with pool.Fori(0, PAIRS - 1) as it:
                        for k in range(2):
                            n = it * 2 + (NH * i + 2 + k)
                            hold_apart(pool, score_done, n - 1, const)
                            nc.gpsimd.tensor_copy(qs[:, k], Q.q[:, bass.ds(it + 1, 1), k, i * P:(i + 1) * P]
                                                  .rearrange("p a t -> p (a t)")).then_inc(qs_ready, 1)

            @block.tensor
            def _(pe):
                pe.sem_inc(pv_done, 2)
                for bank in range(2):
                    pe.sem_inc(turn_done[bank], 1)
                pe.wait_ge(const, 4)

                def scores(i, k, n):
                    pe.wait_ge(qs_ready, n + 1)
                    if not isinstance(n, int) or n >= 2:
                        pe.wait_ge(exp_done, n - 1)
                    keys = (W.kA, W.kB)[k]
                    width = (i + 1) * P
                    for c in range(chunks(i)):
                        lo, hi = c * BLK, min(width, (c + 1) * BLK)
                        nc.tensor.matmul(score[k][:, lo:hi], qs[:, k], keys[:, b, lo:hi], start=True,
                                         stop=(hi < width), skip_group_check=True)
                    nc.tensor.matmul(score[k][:, width - P:width], identb[:], future[:], start=False, stop=True,
                                     skip_group_check=True).then_inc(score_done, 1)

                def turn(i, it, k):
                    n = it * 2 + (NH * i + k)
                    pe.wait_ge(exp_done, n + 1)
                    for c in range(chunks(i)):
                        bank = (k + c) % 2
                        pe.wait_ge(evac[bank], use(i, it, k, c))
                        for j in range(c * CHUNK, min(i + 1, (c + 1) * CHUNK)):
                            ins = nc.tensor.transpose(turned[bank][:, (j % CHUNK) * P:(j % CHUNK + 1) * P],
                                                      probs[:, k, j * P:(j + 1) * P], G.ident[:])
                        ins.then_inc(turn_done[bank], 1)

                def weigh(i, it, k):
                    n = it * 2 + (NH * i + k)
                    for c in range(chunks(i)):
                        pe.wait_ge(evac[(k + c) % 2], use(i, it, k, c) + 1)
                    pe.wait_ge(pc_done, n + 1)
                    for j in range(i + 1):
                        ins = nc.tensor.matmul(pv[k][:, 0:KVL + 1], probsT[:, k, j], W.c[:, b, j],
                                               start=(j == 0), stop=(j == i))
                    ins.then_inc(pv_done, 1)

                def body(i, it, last):
                    for k in range(2):
                        turn(i, it, k)
                        if not last:
                            scores(i, k, it * 2 + (NH * i + 2 + k))
                        weigh(i, it, k)

                def tail(i):
                    pe.wait_ge(pc_done, NH * (i + 1) + 2)
                    for bank in range(2):
                        pe.wait_ge(evac[bank], uses[i + 1] - 1)
                        for p in range(4):
                            ins = nc.tensor.transpose(turned[bank][:, p * P:(p + 1) * P],
                                                      pc[:, i % 2, 2 * (4 * bank + p):2 * (4 * bank + p) + 2], G.ident[:])
                        ins.then_inc(turn_done[bank], 1)
                    for bank in range(2):
                        pe.wait_ge(evac[bank], uses[i + 1])
                    for p in range(PAIRS):
                        ins = nc.tensor.matmul(pv[0][:, 0:D], pcT[:, p], W.m[:, p], start=(p == 0), stop=(p == PAIRS - 1))
                    ins.then_inc(y_done, 1)
                    pe.wait_ge(x_added, i + 1)

                for k in range(2):
                    scores(0, k, k)
                for i in range(TILES):
                    tile_loop(pe, i, body)
                    if i + 1 < TILES:
                        for k in range(2):
                            scores(i + 1, k, NH * (i + 1) + k)
                    tail(i)

            def empty(eng, bank, i, it, k):
                copy = nc.scalar.copy if bank == 0 else nc.vector.tensor_copy
                n = it * 2 + (NH * i + k)
                for c in range(chunks(i)):
                    if (k + c) % 2 == bank:
                        tiles = min(i + 1, (c + 1) * CHUNK) - c * CHUNK
                        eng.wait_ge(turn_done[bank], use(i, it, k, c) + 1)
                        eng.wait_ge(pv_done, n + 1)
                        copy(probsT[:, k, c * CHUNK:c * CHUNK + tiles].rearrange("p j t -> p (j t)"),
                             turned[bank][:, 0:tiles * P]).then_inc(evac[bank], 1)

            def empty_tail(eng, bank, i):
                copy = nc.scalar.copy if bank == 0 else nc.vector.tensor_copy
                eng.wait_ge(turn_done[bank], uses[i + 1])
                if i:
                    eng.wait_ge(y_done, i)
                copy(pcT[:, 4 * bank:4 * bank + 4].rearrange("p j t -> p (j t)"), turned[bank][:])\
                    .then_inc(evac[bank], 1)

            @block.scalar
            def _(act):
                act.sem_inc(evac[0], 1)

                def exponential(i, k, n):
                    act.wait_ge(shift_ready, n + 1)
                    nc.scalar.activation(probs[:, k, 0:(i + 1) * P], score[k][:, 0:(i + 1) * P], ACT.Exp,
                                         bias=shift[:, k:k + 1], scale=SCALE).then_inc(exp_done, 1)

                def body(i, it, last):
                    for k in range(2):
                        empty(act, 0, i, it, k)
                        if not last:
                            for bank in range(2):
                                if chunks(i) == 2 or k == bank:
                                    act.wait_ge(turn_done[bank], use(i, it, k, 0) + 1)
                            exponential(i, k, it * 2 + (NH * i + 2 + k))

                for k in range(2):
                    exponential(0, k, k)
                for i in range(TILES):
                    tile_loop(act, i, body)
                    if i + 1 < TILES:
                        for k in range(2):
                            for bank in range(2):
                                act.wait_ge(turn_done[bank], uses[i + 1] - 1)
                            exponential(i + 1, k, NH * (i + 1) + k)
                    empty_tail(act, 0, i)

            @block.vector
            def _(dve):
                dve.sem_inc(pc_done, 2)
                dve.sem_inc(evac[1], 1)

                def maximum(i, k, n):
                    dve.wait_ge(score_done, n + 1)
                    nc.vector.tensor_reduce(neg_max[:, k:k + 1], score[k][:, 0:(i + 1) * P], AX.X, ALU.max, negate=True)\
                        .then_inc(max_done, 1)
                    dve.wait_ge(max_done, n + 1)
                    if not isinstance(n, int) or n >= 2:
                        dve.wait_ge(exp_done, n - 1)
                    nc.vector.tensor_scalar(shift[:, k:k + 1], neg_max[:, k:k + 1], SCALE, None, ALU.mult)\
                        .then_inc(shift_ready, 1)

                def normalise(i, it, k):
                    n = it * 2 + (NH * i + k)
                    dve.wait_ge(pv_done, n + 3)
                    nc.vector.reciprocal(rden[:, k:k + 1], pv[k][:, KVL:KVL + 1]).then_inc(rden_done, 1)
                    dve.wait_ge(rden_done, n + 1)
                    dst = pc[:, i % 2, bass.ds(it * 2 + k, 1)] if not isinstance(it, int) else pc[:, i % 2, 2 * it + k:2 * it + k + 1]
                    nc.vector.tensor_scalar(dst.rearrange("p a d -> p (a d)"), pv[k][:, 0:KVL], rden[:, k:k + 1], None, ALU.mult)\
                        .then_inc(pc_done, 1)

                def body(i, it, last):
                    for k in range(2):
                        empty(dve, 1, i, it, k)
                        if not last:
                            maximum(i, k, it * 2 + (NH * i + 2 + k))
                        normalise(i, it, k)

                for k in range(2):
                    maximum(0, k, k)
                for i in range(TILES):
                    tile_loop(dve, i, body)
                    if i + 1 < TILES:
                        for k in range(2):
                            maximum(i + 1, k, NH * (i + 1) + k)
                    empty_tail(dve, 1, i)
                    nc.vector.tensor_tensor(G.x[:, b, i], G.x[:, b, i], W.row[:, b], ALU.add).then_inc(row_added, 1)
                    dve.wait_ge(row_added, i + 1)
                    dve.wait_ge(y_done, i + 1)
                    nc.vector.tensor_tensor(G.x[:, b, i], pv[0][:, 0:D], G.x[:, b, i], ALU.add).then_inc(x_added, 1)


E1, R1, F1 = 8, 8, 1024
FM = F1 // P
SCALING = 16.0 / 8.0


def route(nc, dve, steps, apart, logits, top, index, index_f, hot, iota8):
    hold_apart(dve, steps.sem, now(steps.it, steps.per, steps.n), apart)
    for j in range(TPB):
        n = steps.mark(nc.vector.max(top[:, j], logits[:, j]))
    hold_apart(dve, steps.sem, now(steps.it, steps.per, n), apart)
    for j in range(TPB):
        n = steps.mark(nc.vector.max_index(index[:, j], top[:, j], logits[:, j]))
    steps.hold(n)
    steps.then(nc.vector.tensor_copy(index_f[:], index[:, :, 0:2]))
    for k in range(2):
        n = steps.mark(nc.vector.tensor_tensor(hot[:, :, k], spread(iota8[:].unsqueeze(1), [P, TPB, 8]),
                                               spread(index_f[:, :, k:k + 1], [P, TPB, 8]), ALU.is_equal))
    steps.hold(n)
ROUTE_STEPS = 2 * TPB + 3


def l1_ffn(nc, G):
    with Phase(nc, "f1w") as W:
        shapes = {"ra": ([P, KC, E1 + E1 * R1], G.dram["f1_ra"].rearrange("(k p) n -> p k n", p=P)),
                  "w1": ([P, KC, F1], G.dram["f1_w1"].rearrange("(k p) n -> p k n", p=P)),
                  "b1": ([P, FM], G.dram["f1_b1"]), "B1": ([P, F1], G.dram["f1_B1"]),
                  "A2": ([P, FM, E1 * R1], G.dram["f1_A2"].rearrange("(m p) n -> p m n", p=P)),
                  "w2": ([P, FM, D], G.dram["f1_w2"].rearrange("(m p) n -> p m n", p=P)),
                  "B2": ([P, D], G.dram["f1_B2"]),
                  "b2": ([P, D], G.dram["L1_ffn_b2"].partition_broadcast(P)),
                  "br": ([P, E1], G.dram["L1_ffn_b_r"].partition_broadcast(P)),
                  "iota8": ([P, E1], G.dram["iota8"].partition_broadcast(P))}
        w_in = W.sem("w_in")
        for name, (shape, _) in shapes.items():
            W.sb(name, shape)

        def load(sp):
            for name, (_, src) in shapes.items():
                sp.dma_start(W[name][:], src).then_inc(w_in, 16)
        norm_phase(nc, G, "f1n", load=load)
        l1_ffn_blocks(nc, G, W, w_in, 16 * len(shapes))


def l1_ffn_blocks(nc, G, W, w_in, LOADS):
    with Phase(nc, "f1b") as ph:
        xs = ph.sb("xs", [P, KC, BLK])
        logits = ph.sb("logits", [P, TPB, E1])
        top = ph.sb("top", [P, TPB, 8])
        index = ph.sb("index", [P, TPB, 8], U32)
        index_f = ph.sb("index_f", [P, TPB, 2])
        hot = ph.sb("hot", [P, TPB, 2, E1])
        slot = ph.sb("slot", [P, TPB, 2, E1])
        hot_w = ph.sb("hot_w", [P, TPB, 2, E1])
        expo = ph.sb("expo", [P, TPB, 8])
        total = ph.sb("total", [P, TPB])
        w = ph.sb("w", [P, TPB, 2])
        w_sum = ph.sb("w_sum", [P, TPB])
        z = ph.sb("z", [P, TPB, 2, E1, R1])
        wide = ph.sb("wide", [P, TPB, 2 * E1, R1])
        zT = ph.sb("zT", [P, BLK])
        wideT = ph.sb("wideT", [P, BLK])
        wb = ph.sb("wb", [P, 2, BLK])
        h = ph.sb("h", [P, 2, 2, BLK])
        h_w = ph.sb("h_w", [P, 2, 2, BLK])
        h_sum = ph.sb("h_sum", [P, FM, BLK])
        z2T = ph.sb("z2T", [P, BLK])
        HB = 3
        hid = [ph.ps(f"hid{j}", [P, BLK]) for j in range(HB)]
        first = ph.ps("first", [P, TPB, E1 + E1 * R1])
        turned = [ph.ps(f"turned{j}", [P, BLK]) for j in range(2)]
        u2 = ph.ps("u2", [P, BLK])
        y = ph.ps("y", [P, 2, D])
        xs_ready = ph.sem("xs_ready")
        first_done = ph.sem("first_done")
        top_ready = ph.sem("top_ready")
        expo_done = ph.sem("expo_done")
        z_ready = ph.sem("z_ready")
        turn_done = ph.sem("turn_done")
        turn_out = ph.sem("turn_out")
        hid_done = ph.sem("hid_done")
        h_done = ph.sem("h_done")
        u2_done = ph.sem("u2_done")
        hw_dve = ph.sem("hw_dve")
        hw_pool = ph.sem("hw_pool")
        sum_done = ph.sem("sum_done")
        z2_ready = ph.sem("z2_ready")
        y_done = ph.sem("y_done")
        x_added = ph.sem("x_added")
        dve_steps = ph.sem("dve_steps")
        apart, apart_pool = ph.sem("apart"), ph.sem("apart_pool")
        xnT = G.xnT[:].rearrange("p k b t -> p k (b t)")
        x_flat = G.x[:].rearrange("p b i d -> p (b i) d")
        ER = E1 * R1
        with ph.block() as block:
            @block.gpsimd
            def _(pool):
                pool.sem_inc(hw_pool, FM)
                with pool.Fori(0, BLOCKS) as it:
                    hold_apart(pool, u2_done, before(it, FM, FM), apart_pool)
                    nc.gpsimd.tensor_copy(xs[:], xnT[:, :, bass.ds(it * BLK, BLK)]).then_inc(xs_ready, 1)
                    pool.wait_ge(turn_out, now(it, 4, 4, credit=True))
                    for m in range(FM):
                        pool.wait_ge(h_done, now(it, 2 * FM, 2 * m + 2, credit=True))
                        if m >= 2:
                            pool.wait_ge(sum_done, now(it, FM, m - 1, credit=True))
                        nc.gpsimd.tensor_tensor(h_w[:, m % 2, 1], h[:, m % 2, 1], wb[:, 1], ALU.mult).then_inc(hw_pool, 1)

            @block.tensor
            def _(pe):
                pe.sem_inc(u2_done, FM)
                pe.sem_inc(y_done, 2)
                pe.wait_ge(w_in, LOADS)
                with pe.Fori(0, BLOCKS) as it:
                    pe.wait_ge(xs_ready, now(it, 1, 1))
                    for j in range(TPB):
                        for k in range(KC):
                            ins = nc.tensor.matmul(first[:, j], xs[:, k, j * P:(j + 1) * P], W["ra"][:, k],
                                                   start=(k == 0), stop=(k == KC - 1))
                    ins.then_inc(first_done, 1)

                    def base(m):
                        if m >= HB:
                            pe.wait_ge(h_done, now(it, 2 * FM, 2 * (m - HB) + 2, credit=True))
                        else:
                            pe.wait_ge(h_done, before(it, 2 * FM, 2 * FM))
                        for k in range(KC):
                            nc.tensor.matmul(hid[m % HB][:], W["w1"][:, k, m * P:(m + 1) * P], xs[:, k],
                                             start=(k == 0), stop=False, skip_group_check=True)

                    def rank0(m):
                        nc.tensor.matmul(hid[m % HB][:], W["B1"][0:ER, m * P:(m + 1) * P], zT[0:ER], start=False, stop=True,
                                         skip_group_check=True).then_inc(hid_done, 1)

                    def rank1(m):
                        pe.wait_ge(h_done, now(it, 2 * FM, 2 * m + 1, credit=True))
                        nc.tensor.matmul(hid[m % HB][:], W["B1"][ER:2 * ER, m * P:(m + 1) * P], zT[ER:2 * ER], start=False,
                                         stop=True, skip_group_check=True).then_inc(hid_done, 1)

                    def adapter2(m):
                        pe.wait_ge(h_done, now(it, 2 * FM, 2 * m + 2, credit=True))
                        for k in range(2):
                            ins = nc.tensor.matmul(u2[k * ER:(k + 1) * ER], W["A2"][:, m], h[:, m % 2, k],
                                                   start=(m == 0), stop=(m == FM - 1))
                        ins.then_inc(u2_done, 1)

                    base(0)
                    base(1)
                    pe.wait_ge(z_ready, now(it, 1, 1))
                    for bank in range(4):
                        if bank >= 2:
                            pe.wait_ge(turn_out, now(it, 4, bank - 1, credit=True))
                        else:
                            pe.wait_ge(turn_out, before(it, 4, 3 + bank))
                        for j in range(TPB):
                            out = turned[bank % 2][:, j * P:(j + 1) * P]
                            if bank == 0:
                                ins = nc.tensor.transpose(out, z[:, j].rearrange("p k e r -> p (k e r)"), G.ident[:])
                            elif bank == 1:
                                ins = nc.tensor.transpose(out, wide[:, j].rearrange("p k r -> p (k r)"), G.ident[:])
                            else:
                                ins = nc.tensor.matmul(out, spread(w[:, j, bank - 2:bank - 1], [P, P]), G.ident[:],
                                                       start=True, stop=True)
                        ins.then_inc(turn_done, 1)
                    pe.wait_ge(turn_out, now(it, 4, 1, credit=True))
                    rank0(0)
                    rank0(1)
                    for m in range(FM):
                        if m + 2 < FM:
                            base(m + 2)
                            rank0(m + 2)
                        rank1(m)
                        if m >= 1:
                            adapter2(m - 1)
                    adapter2(FM - 1)
                    for c in range(2):
                        pe.wait_ge(x_added, before(it, 2, 2) if c == 0 else now(it, 2, 1, credit=True))
                        pe.wait_ge(sum_done, now(it, FM, FM, credit=True))
                        pe.wait_ge(z2_ready, now(it, 1, 1))
                        for j in range(2):
                            cols = slice((2 * c + j) * P, (2 * c + j + 1) * P)
                            for m in range(FM):
                                nc.tensor.matmul(y[:, j], h_sum[:, m, cols], W["w2"][:, m], start=(m == 0), stop=False)
                            ins = nc.tensor.matmul(y[:, j], z2T[:, cols], W["B2"][:], start=False, stop=True)
                        ins.then_inc(y_done, 1)

            @block.scalar
            def _(act):
                act.sem_inc(h_done, 2 * FM)
                act.sem_inc(turn_out, 4)
                act.wait_ge(w_in, LOADS)
                with act.Fori(0, BLOCKS) as it:
                    act.wait_ge(top_ready, now(it, 1, 1))
                    nc.scalar.activation(expo[:], expo[:], ACT.Exp).then_inc(expo_done, 1)
                    for bank, dst in enumerate((zT[:], wideT[:], wb[:, 0], wb[:, 1])):
                        act.wait_ge(turn_done, now(it, 4, bank + 1))
                        if bank == 2:
                            act.wait_ge(sum_done, before(it, FM, FM))
                        nc.scalar.copy(dst, turned[bank % 2][:]).then_inc(turn_out, 1)

                    def hidden(m, k):
                        act.wait_ge(hid_done, now(it, 2 * FM, hid_order.index((m, k)) + 1))
                        if m >= 2:
                            act.wait_ge(u2_done, now(it, FM, m - 1, credit=True))
                            act.wait_ge(hw_pool, now(it, FM, m - 1, credit=True))
                            act.wait_ge(hw_dve, now(it, FM, m - 1))
                        nc.scalar.activation(h[:, m % 2, k], hid[m % HB][:], ACT.Gelu_apprx_tanh, bias=W["b1"][:, m:m + 1])\
                            .then_inc(h_done, 1)
                    hid_order = [(0, 0), (1, 0)]
                    for m in range(FM):
                        if m + 2 < FM:
                            hid_order.append((m + 2, 0))
                        hid_order.append((m, 1))
                    for m in range(FM):
                        hidden(m, 0)
                        hidden(m, 1)

            @block.vector
            def _(dve):
                dve.sem_inc(sum_done, FM)
                dve.sem_inc(x_added, 2)
                dve.wait_ge(w_in, LOADS)
                with dve.Fori(0, BLOCKS) as it:
                    steps = Steps(dve, dve_steps, it, ROUTE_STEPS + 14)
                    dve.wait_ge(first_done, now(it, 1, 1))
                    steps.mark(nc.vector.tensor_tensor(logits[:], first[:, :, 0:E1], spread(W["br"][:].unsqueeze(1), [P, TPB, E1]), ALU.add))
                    route(nc, dve, steps, apart, logits, top, index, index_f, hot, W["iota8"])
                    nc.vector.tensor_tensor(expo[:], top[:], spread(top[:, :, 0:1], [P, TPB, 8]), ALU.subtract).then_inc(top_ready, 1)
                    steps.then(nc.vector.tensor_scalar(hot[:], hot[:], SCALING, None, ALU.mult))
                    nc.vector.tensor_copy(slot[:, :, 0], hot[:, :, 0])
                    steps.then(nc.vector.tensor_tensor(slot[:, :, 1], hot[:, :, 1], hot[:, :, 0], ALU.subtract))
                    for k in range(2):
                        n = steps.mark(nc.vector.tensor_tensor(
                            z[:, :, k], first[:, :, E1:].rearrange("p j (e r) -> p j e r", r=R1),
                            spread(slot[:, :, k].unsqueeze(3), [P, TPB, E1, R1]), ALU.mult))
                    dve.wait_ge(expo_done, now(it, 1, 1))
                    steps.then(nc.vector.tensor_reduce(total[:], expo[:], AX.X, ALU.add))
                    steps.then(nc.vector.reciprocal(total[:], total[:]))
                    steps.then(nc.vector.tensor_tensor(w[:], expo[:, :, 0:2], spread(total[:].unsqueeze(2), [P, TPB, 2]), ALU.mult))
                    steps.then(nc.vector.tensor_reduce(w_sum[:], w[:], AX.X, ALU.add))
                    steps.then(nc.vector.tensor_tensor(hot_w[:], hot[:], spread(w[:].unsqueeze(3), [P, TPB, 2, E1]), ALU.mult))
                    nc.vector.tensor_copy(wide[:], spread(hot_w[:].rearrange("p j k e -> p j (k e)").unsqueeze(3), [P, TPB, 2 * E1, R1]))\
                        .then_inc(z_ready, 1)
                    for j in range(TPB):
                        x_tile = x_flat[:, bass.ds(it * TPB + j, 1), :].rearrange("p a d -> p (a d)")
                        n = steps.mark(nc.vector.scalar_tensor_tensor(x_tile, W["b2"][:], w_sum[:, j:j + 1], x_tile, ALU.mult, ALU.add))
                    steps.hold(n)
                    dve.wait_ge(turn_out, now(it, 4, 4, credit=True))
                    for m in range(FM):
                        dve.wait_ge(h_done, now(it, 2 * FM, 2 * m + 1, credit=True))
                        nc.vector.tensor_tensor(h_w[:, m % 2, 0], h[:, m % 2, 0], wb[:, 0], ALU.mult).then_inc(hw_dve, 1)
                        dve.wait_ge(hw_dve, now(it, FM, m + 1))
                        dve.wait_ge(hw_pool, now(it, FM, m + 1, credit=True))
                        if m == 0:
                            dve.wait_ge(y_done, before(it, 2, 2))
                        nc.vector.tensor_tensor(h_sum[:, m], h_w[:, m % 2, 0], h_w[:, m % 2, 1], ALU.add).then_inc(sum_done, 1)
                    dve.wait_ge(u2_done, now(it, FM, FM, credit=True))
                    nc.vector.tensor_tensor(z2T[:], u2[:], wideT[:], ALU.mult).then_inc(z2_ready, 1)
                    for c in range(2):
                        dve.wait_ge(y_done, now(it, 2, c + 1, credit=True))
                        x_tiles = x_flat[:, bass.ds(it * TPB + 2 * c, 2), :]
                        nc.vector.tensor_tensor(x_tiles, y[:], x_tiles, ALU.add).then_inc(x_added, 1)
                    steps.close()


LH, LD = 16, 16
HPC = P // LD


def linear_attn(nc, G, tag, gated):
    with Phase(nc, tag + "w") as W:
        pre = "L3_attn_" if gated else "L2_attn_"
        wide = [P, 3 * D]
        loads = {"w": ([P, KC, 3 * D], G.dram[tag + "_w"].rearrange("(k p) n -> p k n", p=P)),
                 "b": (wide, G.dram[tag + "_b"].partition_broadcast(P)),
                 "wo": ([P, KC, D], G.dram[tag + "_wo"].rearrange("(k p) n -> p k n", p=P)),
                 "bo": ([P, D], G.dram[pre + "bo"].partition_broadcast(P)),
                 "same_head": ([P, P], G.dram["same_head"]), "head_of": ([P, HPC], G.dram["head_of"])}
        if gated:
            loads["ln_g"] = ([P, D], G.dram["L3_attn_ln_g"].partition_broadcast(P))
            loads["ln_b"] = ([P, D], G.dram["L3_attn_ln_b"].partition_broadcast(P))
        for name, (shape, _) in loads.items():
            W.sb(name, shape)
        W.w_in = W.sem("w_in")
        W.loads = 16 * len(loads)
        W.k = W.sb("k_all", [P, NB, TILES, D])
        W.v = W.sb("v_all", [P, NB, TILES, KC, P + 1])
        W.u = W.sb("u_all", [P, NB, TILES, D]) if gated else None
        W.qT = W.sb("qT", [P, KC, NB, SEQ])
        W.kv = W.sb("kv", [P, NB, KC, P + HPC])

        def load(sp):
            for name, (_, src) in loads.items():
                sp.dma_start(W[name][:], src).then_inc(W.w_in, 16)
        norm_phase(nc, G, tag + "n", load=load)
        linear_project(nc, G, W, tag + "p", gated)
        linear_state(nc, G, W, tag + "s")
        linear_output(nc, G, W, tag + "o", gated)


def linear_project(nc, G, W, tag, gated):
    with Phase(nc, tag) as ph:
        xs = ph.sb("xs", [P, KC, NB, P])
        s = ph.sb("s", [P, NB, 3 * D])
        expo = ph.sb("expo", [P, NB, 2 * D])
        low = ph.sb("low", [P, NB, 2 * D])
        relu = ph.sb("relu", [P, NB, 2 * D])
        q = ph.sb("q", [P, NB, D])
        half = ph.sb("half", [P, NB, 2 * D]) if gated else None
        tanh = ph.sb("tanh", [P, NB, 2 * D]) if gated else None
        prod = [ph.ps(f"prod{b}", [P, 2 * BLK]) for b in range(NB)]
        turned = [ph.ps(f"turned{b}", [P, KC, P]) for b in range(NB)]
        QK = D if gated else 2 * D
        xs_ready = ph.sem("xs_ready")
        prod_done = ph.sem("prod_done")
        s_ready = ph.sem("s_ready")
        expo_done = ph.sem("expo_done")
        stored = ph.sem("stored")
        turn_done = ph.sem("turn_done")
        turn_out = ph.sem("turn_out")
        dve_steps = ph.sem("dve_steps")
        apart = ph.sem("apart")
        with ph.block() as block:
            @block.gpsimd
            def _(pool):
                nc.gpsimd.memset(W.v[:, :, :, :, P:P + 1], 1.0)
                with pool.Fori(0, TILES) as it:
                    hold_apart(pool, prod_done, before(it, NB, NB), apart)
                    nc.gpsimd.tensor_copy(xs[:], G.xnT[:, :, :, bass.ds(it * P, P)]).then_inc(xs_ready, 1)

            @block.tensor
            def _(pe):
                pe.sem_inc(prod_done, NB)
                pe.sem_inc(turn_done, NB)
                pe.wait_ge(W.w_in, W.loads)
                with pe.Fori(0, TILES) as it:
                    pe.wait_ge(xs_ready, now(it, 1, 1))
                    for b in range(NB):
                        pe.wait_ge(s_ready, before(it, NB, b + 1))
                        for lo, hi in ((0, BLK), (BLK, 3 * D)):
                            for k in range(KC):
                                ins = nc.tensor.matmul(prod[b][:, lo:hi], xs[:, k, b], W["w"][:, k, lo:hi],
                                                       start=(k == 0), stop=(k == KC - 1))
                        ins.then_inc(prod_done, 1)
                    for b in range(NB):
                        pe.wait_ge(stored, now(it, NB, b + 1, credit=True))
                        pe.wait_ge(turn_out, before(it, NB, b + 1))
                        for k in range(KC):
                            ins = nc.tensor.transpose(turned[b][:, k], q[:, b, k * P:(k + 1) * P], G.ident[:])
                        ins.then_inc(turn_done, 1)

            @block.scalar
            def _(act):
                act.sem_inc(turn_out, NB)
                with act.Fori(0, TILES) as it:
                    for b in range(NB):
                        act.wait_ge(s_ready, now(it, NB, b + 1, credit=True))
                        act.wait_ge(stored, before(it, NB, NB))
                        if gated:
                            nc.scalar.activation(tanh[:, b], s[:, b, D:3 * D], ACT.Tanh, scale=0.5)
                            nc.scalar.activation(half[:, b], s[:, b, D:3 * D], ACT.Copy, scale=0.5)
                        nc.scalar.activation(expo[:, b, 0:QK], low[:, b, 0:QK], ACT.Exp).then_inc(expo_done, 1)
                    for b in range(NB):
                        act.wait_ge(turn_done, now(it, NB, b + 1, credit=True))
                        nc.scalar.copy(W.qT[:, :, b, bass.ds(it * P, P)], turned[b][:]).then_inc(turn_out, 1)

            @block.vector
            def _(dve):
                dve.sem_inc(s_ready, NB)
                dve.sem_inc(stored, NB)
                dve.wait_ge(W.w_in, W.loads)
                with dve.Fori(0, TILES) as it:
                    steps = Steps(dve, dve_steps, it, 3 * NB)
                    for b in range(NB):
                        dve.wait_ge(prod_done, now(it, NB, b + 1, credit=True))
                        steps.then(nc.vector.tensor_tensor(s[:, b], prod[b][:, 0:3 * D], W["b"][:], ALU.add))
                        nc.vector.tensor_scalar(low[:, b, 0:QK], s[:, b, 0:QK], 0.0, None, ALU.min).then_inc(s_ready, 1)
                    for b in range(NB):
                        steps.then(nc.vector.tensor_scalar(relu[:, b, 0:QK], s[:, b, 0:QK], 0.0, -1.0 if gated else 0.0, ALU.max, ALU.add))
                        dve.wait_ge(expo_done, now(it, NB, b + 1))
                        dve.wait_ge(turn_done, before(it, NB, b + 1))
                        steps.then(nc.vector.tensor_tensor(q[:, b], expo[:, b, 0:D], relu[:, b, 0:D], ALU.add))
                        k_dst = W.k[:, b, bass.ds(it, 1)].rearrange("p a d -> p (a d)")
                        v_dst = W.v[:, b, bass.ds(it, 1), :, 0:P].rearrange("p a k d -> p (a k) d")
                        if gated:
                            nc.vector.tensor_copy(k_dst, q[:, b])
                            u_dst = W.u[:, b, bass.ds(it, 1)].rearrange("p a d -> p (a d)")
                            nc.vector.scalar_tensor_tensor(u_dst, tanh[:, b, D:2 * D], 1.0, half[:, b, D:2 * D], ALU.add, ALU.mult)
                            nc.vector.scalar_tensor_tensor(v_dst, tanh[:, b, 0:D].rearrange("p (k d) -> p k d", k=KC), 1.0,
                                                           half[:, b, 0:D].rearrange("p (k d) -> p k d", k=KC), ALU.add, ALU.mult)\
                                .then_inc(stored, 1)
                        else:
                            nc.vector.tensor_tensor(k_dst, expo[:, b, D:2 * D], relu[:, b, D:2 * D], ALU.add)
                            nc.vector.tensor_copy(v_dst, s[:, b, 2 * D:3 * D].rearrange("p (k d) -> p k d", k=KC)).then_inc(stored, 1)
                    steps.close()


def linear_state(nc, G, W, tag):
    with Phase(nc, tag) as ph:
        acc = [ph.ps(f"acc{b}", [P, KC, P + 1]) for b in range(NB)]
        acc_done = ph.sem("acc_done")
        with ph.block() as block:
            @block.tensor
            def _(pe):
                for b in range(NB):
                    for k in range(KC):
                        for i in range(TILES):
                            ins = nc.tensor.matmul(acc[b][:, k], W.k[:, b, i, k * P:(k + 1) * P], W.v[:, b, i, k],
                                                   start=(i == 0), stop=(i == TILES - 1))
                    ins.then_inc(acc_done, 1)

            @block.vector
            def _(dve):
                for b in range(NB):
                    dve.wait_ge(acc_done, b + 1)
                    nc.vector.tensor_tensor(W.kv[:, b, :, 0:P], acc[b][:, :, 0:P], spread(W["same_head"][:].unsqueeze(1), [P, KC, P]), ALU.mult)
                    nc.vector.tensor_tensor(W.kv[:, b, :, P:P + HPC], spread(acc[b][:, :, P:P + 1], [P, KC, HPC]),
                                            spread(W["head_of"][:].unsqueeze(1), [P, KC, HPC]), ALU.mult)


def linear_output(nc, G, W, tag, gated):
    with Phase(nc, tag) as ph:
        qs = ph.sb("qs", [P, KC, NB, P])
        den = ph.sb("den", [P, NB, KC, HPC])
        out = ph.sb("out", [P, NB, D])
        outT = ph.sb("outT", [P, NB, KC, P])
        stats = ph.sb("stats", [P, NB, 6])
        mv = ph.sb("mv", [P, NB, 2])
        veps = ph.sb("veps", [P, NB])
        rstd = ph.sb("rstd", [P, NB])
        prod = [ph.ps(f"prod{b}", [P, KC, P + HPC]) for b in range(NB)]
        turned = [ph.ps(f"turned{b}", [P, KC, P]) for b in range(NB)]
        y = ph.ps("y", [P, NB, D])
        qs_ready = ph.sem("qs_ready")
        prod_done = ph.sem("prod_done")
        var_ready, rstd_ready = ph.sem("var_ready"), ph.sem("rstd_ready")
        out_ready = ph.sem("out_ready")
        turn_done = ph.sem("turn_done")
        turn_out = ph.sem("turn_out")
        y_done = ph.sem("y_done")
        x_added = ph.sem("x_added")
        dve_steps = ph.sem("dve_steps")
        apart, apart_pool = ph.sem("apart"), ph.sem("apart_pool")
        N = P if gated else P + HPC
        with ph.block() as block:
            @block.gpsimd
            def _(pool):
                with pool.Fori(0, TILES) as it:
                    hold_apart(pool, prod_done, before(it, NB, NB), apart_pool)
                    nc.gpsimd.tensor_copy(qs[:], W.qT[:, :, :, bass.ds(it * P, P)]).then_inc(qs_ready, 1)
                    if gated:
                        pool.wait_ge(var_ready, now(it, 1, 1))
                        nc.gpsimd.tensor_tensor(rstd[:], veps[:], G.minus_half[:, 0:NB], ALU.pow).then_inc(rstd_ready, 1)

            @block.tensor
            def _(pe):
                pe.sem_inc(prod_done, NB)
                pe.sem_inc(turn_done, NB)
                pe.sem_inc(y_done, 1)
                with pe.Fori(0, TILES) as it:
                    pe.wait_ge(qs_ready, now(it, 1, 1))
                    for b in range(NB):
                        pe.wait_ge(out_ready, before(it, NB, b + 1))
                        for k in range(KC):
                            ins = nc.tensor.matmul(prod[b][:, k, 0:N], qs[:, k, b], W.kv[:, b, k, 0:N], start=True, stop=True)
                        ins.then_inc(prod_done, 1)
                    for b in range(NB):
                        pe.wait_ge(out_ready, now(it, NB, b + 1, credit=True))
                        pe.wait_ge(turn_out, before(it, NB, b + 1))
                        for k in range(KC):
                            ins = nc.tensor.transpose(turned[b][:, k], out[:, b, k * P:(k + 1) * P], G.ident[:])
                        ins.then_inc(turn_done, 1)
                    pe.wait_ge(x_added, before(it, 1, 1))
                    for b in range(NB):
                        pe.wait_ge(turn_out, now(it, NB, b + 1, credit=True))
                        for k in range(KC):
                            ins = nc.tensor.matmul(y[:, b], outT[:, b, k], W["wo"][:, k], start=(k == 0), stop=(k == KC - 1))
                    ins.then_inc(y_done, 1)

            @block.scalar
            def _(act):
                act.sem_inc(turn_out, NB)
                with act.Fori(0, TILES) as it:
                    for b in range(NB):
                        act.wait_ge(turn_done, now(it, NB, b + 1, credit=True))
                        if b == 0:
                            act.wait_ge(y_done, before(it, 1, 1))
                        nc.scalar.copy(outT[:, b], turned[b][:]).then_inc(turn_out, 1)

            @block.vector
            def _(dve):
                dve.sem_inc(out_ready, NB)
                dve.sem_inc(x_added, 1)
                with dve.Fori(0, TILES) as it:
                    steps = Steps(dve, dve_steps, it, 5 * NB + 1 if gated else 2 * NB + 1)
                    x_tile = G.x[:, :, bass.ds(it, 1), :].rearrange("p b i d -> p b (i d)")
                    steps.then(nc.vector.tensor_tensor(x_tile, x_tile, spread(W["bo"][:].unsqueeze(1), [P, NB, D]), ALU.add))
                    if gated:
                        for b in range(NB):
                            dve.wait_ge(prod_done, now(it, NB, b + 1, credit=True))
                            n = steps.mark(nc.vector.bn_stats(stats[:, b], prod[b][:, :, 0:P]))
                        hold_apart(dve, dve_steps, now(it, steps.per, n), apart)
                        for b in range(NB):
                            n = steps.mark(nc.vector.bn_aggr(mv[:, b], stats[:, b]))
                        steps.hold(n)
                        nc.vector.tensor_scalar(veps[:], mv[:, :, 1], EPS, None, ALU.add).then_inc(var_ready, 1)
                        dve.wait_ge(rstd_ready, now(it, 1, 1))
                        for b in range(NB):
                            dve.wait_ge(turn_done, before(it, NB, b + 1))
                            o = out[:, b].rearrange("p (k d) -> p k d", k=KC)
                            u_src = W.u[:, b, bass.ds(it, 1)].rearrange("p a d -> p (a d)")
                            steps.then(nc.vector.tensor_scalar(o, prod[b][:, :, 0:P], mv[:, b, 0:1], rstd[:, b:b + 1], ALU.subtract, ALU.mult))
                            steps.then(nc.vector.tensor_tensor(out[:, b], out[:, b], W["ln_g"][:], ALU.mult))
                            steps.then(nc.vector.tensor_tensor(out[:, b], out[:, b], W["ln_b"][:], ALU.add))
                            nc.vector.tensor_tensor(out[:, b], out[:, b], u_src, ALU.mult).then_inc(out_ready, 1)
                    else:
                        for b in range(NB):
                            dve.wait_ge(prod_done, now(it, NB, b + 1, credit=True))
                            steps.then(nc.vector.tensor_scalar(den[:, b], prod[b][:, :, P:P + HPC], 1e-8, None, ALU.add))
                            steps.then(nc.vector.reciprocal(den[:, b], den[:, b]))
                            dve.wait_ge(turn_done, before(it, NB, b + 1))
                            nc.vector.tensor_tensor(out[:, b].rearrange("p (k h d) -> p k h d", k=KC, h=HPC),
                                                    prod[b][:, :, 0:P].rearrange("p k (h d) -> p k h d", h=HPC),
                                                    spread(den[:, b].unsqueeze(3), [P, KC, HPC, LD]), ALU.mult).then_inc(out_ready, 1)
                    dve.wait_ge(y_done, now(it, 1, 1, credit=True))
                    nc.vector.tensor_tensor(x_tile, y[:], x_tile, ALU.add).then_inc(x_added, 1)
                    steps.close()


def l2_attn(nc, G):
    linear_attn(nc, G, "l2", False)


def l3_attn(nc, G):
    linear_attn(nc, G, "l3", True)


E2, SH = 8, 256
HC = E2 + SH // P


def l2_ffn(nc, G):
    with Phase(nc, "f2w") as W:
        loads = {"gate": ([P, KC, E2], G.dram["L2_ffn_gate_w"].rearrange("(k p) n -> p k n", p=P)),
                 "w1": ([P, KC, HC * P], G.dram["f2_w1"].rearrange("(k p) n -> p k n", p=P)),
                 "b1": ([P, HC], G.dram["f2_b1"]),
                 "w2": ([P, HC, D], G.dram["f2_w2"].rearrange("(c p) n -> p c n", p=P)),
                 "b2": ([E2, D], G.dram["L2_ffn_b2"]),
                 "sb2": ([P, D], G.dram["L2_ffn_shared_b2"].partition_broadcast(P)),
                 "iota8": ([P, E2], G.dram["iota8"].partition_broadcast(P))}
        for name, (shape, _) in loads.items():
            W.sb(name, shape)
        w_in = W.sem("w_in")

        def load(sp):
            for name, (_, src) in loads.items():
                sp.dma_start(W[name][:], src).then_inc(w_in, 16)
        norm_phase(nc, G, "f2n", load=load)
        l2_ffn_blocks(nc, G, W, w_in, 16 * len(loads))


def l2_ffn_blocks(nc, G, W, w_in, LOADS):
    with Phase(nc, "f2b") as ph:
        xs = ph.sb("xs", [P, KC, BLK])
        logits = ph.sb("logits", [P, TPB, E2])
        top = ph.sb("top", [P, TPB, 8])
        index = ph.sb("index", [P, TPB, 8], U32)
        index_f = ph.sb("index_f", [P, TPB, 2])
        hot = ph.sb("hot", [P, TPB, 2, E2])
        expo = ph.sb("expo", [P, TPB])
        g = ph.sb("g", [P, TPB, 2])
        hot_g = ph.sb("hot_g", [P, TPB, 2, E2])
        gates = ph.sb("gates", [P, TPB, E2])
        gatesT = ph.sb("gatesT", [E2, TPB, P])
        h = ph.sb("h", [P, HC, BLK])
        OB = 3
        first = ph.ps("first", [P, TPB, E2])
        turned = ph.ps("turned", [E2, TPB, P])
        hid = [ph.ps(f"hid{j}", [P, BLK]) for j in range(2)]
        shared = ph.ps("shared", [P, D])
        out = [ph.ps(f"out{j}", [P, 2, D]) for j in range(OB)]
        xs_ready = ph.sem("xs_ready")
        first_done = ph.sem("first_done")
        gap_ready = ph.sem("gap_ready")
        expo_done = ph.sem("expo_done")
        gates_ready = ph.sem("gates_ready")
        turn_done = ph.sem("turn_done")
        turn_out = ph.sem("turn_out")
        hid_done = ph.sem("hid_done")
        h_done = ph.sem("h_done")
        shared_done = ph.sem("shared_done")
        out_done = ph.sem("out_done")
        shared_read = ph.sem("shared_read")
        out_read = ph.sem("out_read")
        dve_steps = ph.sem("dve_steps")
        apart, apart_pool = ph.sem("apart"), ph.sem("apart_pool")
        OUTS = TPB * E2 // 2
        xnT = G.xnT[:].rearrange("p k b t -> p k (b t)")
        x_flat = G.x[:].rearrange("p b i d -> p (b i) d")
        with ph.block() as block:
            @block.gpsimd
            def _(pool):
                with pool.Fori(0, BLOCKS) as it:
                    hold_apart(pool, hid_done, before(it, HC, HC), apart_pool)
                    nc.gpsimd.tensor_copy(xs[:], xnT[:, :, bass.ds(it * BLK, BLK)]).then_inc(xs_ready, 1)

            @block.tensor
            def _(pe):
                pe.sem_inc(hid_done, HC)
                pe.sem_inc(out_done, OUTS)
                pe.wait_ge(w_in, LOADS)
                with pe.Fori(0, BLOCKS) as it:
                    pe.wait_ge(xs_ready, now(it, 1, 1))
                    for j in range(TPB):
                        for k in range(KC):
                            ins = nc.tensor.matmul(first[:, j], xs[:, k, j * P:(j + 1) * P], W["gate"][:, k],
                                                   start=(k == 0), stop=(k == KC - 1))
                    ins.then_inc(first_done, 1)
                    for c in range(HC):
                        pe.wait_ge(h_done, now(it, HC, c - 1, credit=True) if c >= 2 else before(it, HC, HC - 1 + c))
                        for k in range(KC):
                            ins = nc.tensor.matmul(hid[c % 2][:], W["w1"][:, k, c * P:(c + 1) * P], xs[:, k],
                                                   start=(k == 0), stop=(k == KC - 1))
                        ins.then_inc(hid_done, 1)
                    pe.wait_ge(gates_ready, now(it, 1, 1))
                    for j in range(TPB):
                        ins = nc.tensor.transpose(turned[:, j], gates[:, j], G.ident[:])
                    ins.then_inc(turn_done, 1)
                    pe.wait_ge(turn_out, now(it, 1, 1))
                    pe.wait_ge(h_done, now(it, HC, HC, credit=True))
                    for j in range(TPB):
                        cols = slice(j * P, (j + 1) * P)
                        pe.wait_ge(shared_read, it * TPB + j + 1)
                        nc.tensor.matmul(shared[:], gatesT[:, j], W["b2"][:], start=True, stop=False)
                        for c in range(E2, HC):
                            ins = nc.tensor.matmul(shared[:], h[:, c, cols], W["w2"][:, c], start=False, stop=(c == HC - 1))
                        ins.then_inc(shared_done, 1)
                        for e in range(0, E2, 2):
                            n = j * (E2 // 2) + e // 2
                            pe.wait_ge(out_read, now(it, OUTS, n - OB + 1, credit=True))
                            for d in range(2):
                                ins = nc.tensor.matmul(out[n % OB][:, d], h[:, e + d, cols], W["w2"][:, e + d], start=True, stop=True)
                            ins.then_inc(out_done, 1)

            @block.scalar
            def _(act):
                act.sem_inc(h_done, HC)
                act.wait_ge(w_in, LOADS)
                with act.Fori(0, BLOCKS) as it:
                    act.wait_ge(gap_ready, now(it, 1, 1))
                    nc.scalar.activation(expo[:], expo[:], ACT.Exp).then_inc(expo_done, 1)
                    act.wait_ge(out_done, before(it, OUTS, OUTS))
                    for c in range(HC):
                        act.wait_ge(hid_done, now(it, HC, c + 1, credit=True))
                        nc.scalar.activation(h[:, c], hid[c % 2][:], ACT.Gelu, bias=W["b1"][:, c:c + 1]).then_inc(h_done, 1)
                    act.wait_ge(turn_done, now(it, 1, 1))
                    nc.scalar.copy(gatesT[:], turned[:]).then_inc(turn_out, 1)

            @block.vector
            def _(dve):
                dve.sem_inc(shared_read, 1)
                dve.sem_inc(out_read, OUTS)
                dve.wait_ge(w_in, LOADS)
                with dve.Fori(0, BLOCKS) as it:
                    steps = Steps(dve, dve_steps, it, ROUTE_STEPS + 5 + TPB * (1 + E2))
                    dve.wait_ge(first_done, now(it, 1, 1))
                    steps.mark(nc.vector.tensor_copy(logits[:], first[:]))
                    route(nc, dve, steps, apart, logits, top, index, index_f, hot, W["iota8"])
                    nc.vector.tensor_tensor(expo[:], top[:, :, 1], top[:, :, 0], ALU.subtract).then_inc(gap_ready, 1)
                    dve.wait_ge(expo_done, now(it, 1, 1))
                    steps.then(nc.vector.tensor_scalar(g[:, :, 0], expo[:], 1.0, None, ALU.add))
                    steps.then(nc.vector.reciprocal(g[:, :, 0], g[:, :, 0]))
                    steps.then(nc.vector.tensor_tensor(g[:, :, 1], expo[:], g[:, :, 0], ALU.mult))
                    steps.then(nc.vector.tensor_tensor(hot_g[:], hot[:], spread(g[:].unsqueeze(3), [P, TPB, 2, E2]), ALU.mult))
                    nc.vector.tensor_tensor(gates[:], hot_g[:, :, 0], hot_g[:, :, 1], ALU.add).then_inc(gates_ready, 1)
                    dve.wait_ge(gates_ready, now(it, 1, 1))
                    for j in range(TPB):
                        x_tile = x_flat[:, bass.ds(it * TPB + j, 1), :].rearrange("p a d -> p (a d)")
                        steps.then(nc.vector.tensor_tensor(x_tile, x_tile, W["sb2"][:], ALU.add))
                        dve.wait_ge(shared_done, now(it, TPB, j + 1))
                        nc.vector.tensor_tensor(x_tile, shared[:], x_tile, ALU.add).then_inc(shared_read, 1)
                        dve.wait_ge(shared_read, it * TPB + j + 2)
                        for e in range(E2):
                            n = j * (E2 // 2) + e // 2
                            dve.wait_ge(out_done, now(it, OUTS, n + 1, credit=True))
                            ins = nc.vector.scalar_tensor_tensor(x_tile, out[n % OB][:, e % 2], gates[:, j, e:e + 1], x_tile, ALU.mult, ALU.add)
                            steps.then(ins)
                            if e % 2:
                                dve.sem_inc(out_read, 1)
                    steps.close()



def l3_ffn(nc, G):
    with Phase(nc, "f3w") as W:
        w = W.sb("w", [P, KC, D])
        variation = W.sb("variation", [P, KC, D])
        low = W.sb("low", [P, KC, D])
        wT = W.sb("wT", [P, KC, D])
        w_in, steps_sem = W.sem("w_in"), W.sem("steps")
        TH_X, SC_X, TH_W, SC_W = 0.33, 0.5, 0.2, 0.6

        def load(sp):
            sp.dma_start(w[:], G.dram["f3_w"].rearrange("(k p) n -> p k n", p=P)).then_inc(w_in, 16)
            sp.dma_start(variation[:], G.dram["f3_v"].rearrange("(k p) n -> p k n", p=P)).then_inc(w_in, 16)
        norm_phase(nc, G, "f3n", load=load, ternary=(TH_X, SC_X))
        with nc.Block() as block:
            @block.vector
            def _(dve):
                steps = Steps(dve, steps_sem)
                dve.wait_ge(w_in, 2 * 16)
                nc.vector.tensor_scalar(low[:], w[:], -TH_W, SC_W, ALU.is_lt, ALU.mult)
                steps.then(nc.vector.tensor_scalar(wT[:], w[:], TH_W, SC_W, ALU.is_gt, ALU.mult))
                steps.then(nc.vector.tensor_tensor(wT[:], wT[:], low[:], ALU.subtract))
                nc.vector.tensor_tensor(wT[:], wT[:], variation[:], ALU.add)
        staged_linear(nc, G, "f3l", wT, None)


BRANCHES = [l0_attn, l0_ffn, l1_attn, l1_ffn, l2_attn, l2_ffn, l3_attn, l3_ffn]


SEMS_OF_A_BRANCH = 80


def program(nc, dram, out):
    RETIRED.clear()
    with Phase(nc, "g") as G:
        G.dram = dram
        G.x = G.sb("x", [P, NB, TILES, D])
        G.xnT = G.sb("xnT", [P, KC, NB, SEQ])
        G.ident = G.sb("ident", [P, P])
        G.minus_half = G.sb("minus_half", [P, TPB])
        x_in, const = G.sem("x_in"), G.sem("const")
        stored = G.sem("stored")
        with nc.Block() as block:
            @block.sync
            def _(sp):
                for b in range(NB):
                    sp.dma_start(G.x[:, b], dram["L0_attn_x"][b].rearrange("(i p) d -> p i d", p=P)).then_inc(x_in, 16)
                sp.wait_ge(x_in, 16 * NB)

            @block.gpsimd
            def _(pool):
                nc.gpsimd.memset(G.minus_half[:], -0.5)
                nc.gpsimd.memset(G.ident[:], 0.0).then_inc(const, 1)
                pool.wait_ge(const, 1)
                nc.gpsimd.affine_select(out=G.ident[:], in_=G.ident[:], compare_op=ALU.not_equal, fill=1.0,
                                        base=0, pattern=[[-1, P]], channel_multiplier=1)
        for n in LAYERS:
            BRANCHES[n](nc, G)
            if nc.free_len() < SEMS_OF_A_BRANCH:
                recycle_semaphores(nc)
        with nc.Block() as block:
            @block.sync
            def _(sp):
                for b in range(NB):
                    sp.dma_start(out[b].rearrange("(i p) d -> p i d", p=P), G.x[:, b]).then_inc(stored, 16)
                sp.wait_ge(stored, 16 * NB)


def rope_tables():
    fraction = np.arange(0, HD, 2, dtype=np.float32) / np.float32(HD)
    inv = (np.float32(1.0) / np.power(np.float32(10000.0), fraction)).astype(np.float32)
    angle = np.outer(np.arange(SEQ, dtype=np.float32), inv).astype(np.float32)
    cos, sin = np.cos(angle).T, np.sin(angle).T
    return np.concatenate([cos, cos]), np.concatenate([sin, -sin])


def l1_layouts(i):
    places = np.concatenate([np.arange(0, DR, 2), np.arange(1, DR, 2)])
    swapped = np.concatenate([np.arange(1, DR, 2), np.arange(0, DR, 2)])
    by_head = lambda w, d: w.reshape(w.shape[0], NH, d).transpose(2, 1, 0)
    qr = i["L1_attn_W_qr"].reshape(QL, PAIRS, 2, DR)
    kr = i["L1_attn_W_kr"]
    inv = 1.0 / 10000.0 ** (np.arange(0, DR, 2)[:DR // 2].astype(np.float32) / DR)
    angle = np.outer(np.arange(SEQ, dtype=np.float32), inv)
    cos, sin = np.cos(angle).T.astype(np.float32), np.sin(angle).T.astype(np.float32)
    rows = np.arange(P)
    order = rows // TOPK
    return {
        "l1_qcT": by_head(i["L1_attn_W_qc"], DK), "l1_kcT": by_head(i["L1_attn_W_kc"], DK),
        "l1_vT": by_head(i["L1_attn_W_v"], DV), "L1_attn_W_o": i["L1_attn_W_o"],
        "l1_qr": np.concatenate([qr[..., places].reshape(QL, PAIRS, P), qr[..., swapped].reshape(QL, PAIRS, P)], axis=2),
        "l1_k": np.concatenate([kr[:, places], i["L1_attn_W_c"], kr[:, swapped]], axis=1),
        **{n: i[n] for n in ("L1_attn_W_cp", "L1_attn_W_gate", "L1_attn_W_idx", "L1_attn_W_sq",
                             "L1_attn_W_sk", "L1_attn_W_sv", "L1_attn_W_iout")},
        "l1_cos": np.concatenate([cos] * 4), "l1_sin": np.concatenate([-sin, sin] * 2),
        "l1_iota": (rows[:, None] + P * np.arange(TILES)).astype(np.float32),
        "l1_same": np.where(order[:, None] == order, 0.0, BIG).astype(np.float32),
        "l1_mean": ((order[:, None] == np.arange(NB * IH)) / TOPK).astype(np.float32),
    }


def ffn_layouts(i):
    B1 = i["L1_ffn_B1"].transpose(0, 2, 1).reshape(E1 * R1, F1)
    B2 = i["L1_ffn_B2"].transpose(0, 2, 1).reshape(E1 * R1, D)
    return {
        "f1_ra": np.concatenate([i["L1_ffn_W_r"].T, i["L1_ffn_A1"].reshape(E1 * R1, D).T], axis=1),
        "f1_w1": i["L1_ffn_W1"].T, "f1_b1": i["L1_ffn_b1"].reshape(FM, P).T, "f1_B1": np.concatenate([B1, B1]),
        "f1_A2": i["L1_ffn_A2"].reshape(E1 * R1, F1).T, "f1_w2": i["L1_ffn_W2"].T, "f1_B2": np.concatenate([B2, B2]),
        "L1_ffn_b2": i["L1_ffn_b2"], "L1_ffn_b_r": i["L1_ffn_b_r"],
        "iota8": np.arange(8, dtype=np.float32),
        "L2_ffn_gate_w": i["L2_ffn_gate_w"], "L2_ffn_b2": i["L2_ffn_b2"], "L2_ffn_shared_b2": i["L2_ffn_shared_b2"],
        "f2_w1": np.concatenate([i["L2_ffn_w1"].transpose(1, 0, 2).reshape(D, E2 * P), i["L2_ffn_shared_w1"]], axis=1),
        "f2_b1": np.concatenate([i["L2_ffn_b1"], i["L2_ffn_shared_b1"].reshape(SH // P, P)]).T,
        "f2_w2": np.concatenate([i["L2_ffn_w2"].reshape(E2 * P, D), i["L2_ffn_shared_w2"]]),
        "f3_w": i["L3_ffn_weight"].T, "f3_v": i["L3_ffn_rram_variation"].T,
    }


def linear_layouts(i):
    two, three = (lambda n: i["L2_attn_" + n]), (lambda n: i["L3_attn_" + n])
    head = np.arange(P) // LD
    return {
        "l2_w": np.concatenate([two(n).T for n in ("wq", "wk", "wv")], axis=1),
        "l2_b": np.concatenate([two(n) for n in ("bq", "bk", "bv")]),
        "l2_wo": two("wo").T, "L2_attn_bo": two("bo"),
        "l3_w": np.concatenate([three(n) for n in ("Wqk", "Wv", "Wu")], axis=1),
        "l3_b": np.concatenate([three(n) for n in ("bqk", "bv", "bu")]),
        "l3_wo": three("Wo"), "L3_attn_bo": three("bo"), "L3_attn_ln_g": three("ln_g"), "L3_attn_ln_b": three("ln_b"),
        "same_head": (head[:, None] == head).astype(np.float32),
        "head_of": (head[:, None] == np.arange(HPC)).astype(np.float32),
    }


def layouts(i):
    cos, sin = rope_tables()
    return {
        "L0_attn_x": i["L0_attn_x"],
        "L0_attn_q_kernel": i["L0_attn_q_kernel"], "L0_attn_k_kernel": i["L0_attn_k_kernel"],
        "L0_attn_v_kernel": i["L0_attn_v_kernel"], "L0_attn_out_kernel": i["L0_attn_out_kernel"],
        "l0_cos": cos, "l0_sin": sin,
        "L0_ffn_weight": i["L0_ffn_weight"], "L0_ffn_bias": i["L0_ffn_bias"],
        **l1_layouts(i), **ffn_layouts(i), **linear_layouts(i),
    }


def kernel(**inputs):
    import numpy as _np
    import concourse.bacc as _bacc
    from concourse import mybir as _mybir
    from concourse.bass_utils import run_bass_kernel_spmd as _run

    nc = _bacc.Bacc("TRN2", target_bir_lowering=False, num_devices=1)
    arrays, dram = {}, {}
    for name, a in layouts({k: _np.asarray(v) for k, v in inputs.items()}).items():
        arrays[f"in_{name}"] = a = _np.ascontiguousarray(a)
        dram[name] = nc.dram_tensor(f"in_{name}", a.shape, _mybir.dt.from_np(a.dtype), kind="ExternalInput").ap()
    out = nc.dram_tensor("out_0_dram", (NB, SEQ, D), F32, kind="ExternalOutput").ap()
    program(nc, dram, out)
    r = _run(nc, [arrays], core_ids=[0])
    return r.results[0]["out_0_dram"]
```

```python
from contextlib import ExitStack

import numpy as np

import concourse.bass as bass
from concourse import mybir

F32 = mybir.dt.float32
BF16 = mybir.dt.bfloat16
U32 = mybir.dt.uint32
ACT = mybir.ActivationFunctionType
ALU = mybir.AluOpType
AX = mybir.AxisListType

P = 128
NB, SEQ, D = 2, 1024, 256
TILES = SEQ // P
KC = D // P
BLK = 512
TPB = BLK // P
BLOCKS = NB * SEQ // BLK
BPB = SEQ // BLK
EPS = 1e-5

LAYERS = range(8)


def before(it, per, n):
    assert n >= 1
    return it * per + n


def now(it, per, n, credit=False):
    assert n + (per if credit else 0) >= 1
    return it * per + n + (per if credit else 0)


class Steps:

    def __init__(self, eng, sem, it=0, per=0):
        self.eng, self.sem, self.it, self.per, self.n = eng, sem, it, per, 0

    def mark(self, ins):
        self.n += 1
        ins.then_inc(self.sem, 1)
        return self.n

    def hold(self, n):
        self.eng.wait_ge(self.sem, now(self.it, self.per, n))

    def then(self, ins):
        self.hold(self.mark(ins))

    def close(self):
        assert self.per in (0, self.n), (self.per, self.n)


def hold_apart(eng, sem, value, apart):
    eng.wait_ge(sem, value)
    eng.sem_inc(apart, 1)


def spread(ap, shape):
    return ap.to_broadcast(shape)


RETIRED = []


def recycle_semaphores(nc):
    nc.clear_and_free_semaphores(RETIRED)
    RETIRED.clear()
    nc.all_engine_barrier()


class Phase:

    def __init__(self, nc, tag):
        self.nc, self.tag, self.stack, self.sems, self.named = nc, tag, ExitStack(), [], {}

    def __enter__(self):
        self.stack.__enter__()
        return self

    def __exit__(self, *what):
        RETIRED.extend(self.sems)
        return self.stack.__exit__(*what)

    def sb(self, name, shape, dt=F32):
        self.named[name] = self.stack.enter_context(self.nc.sbuf_tensor(f"{self.tag}_{name}", shape, dt))
        return self.named[name]

    def __getitem__(self, name):
        return self.named[name]

    def ps(self, name, shape, dt=F32):
        return self.stack.enter_context(self.nc.psum_tensor(f"{self.tag}_{name}", shape, dt))

    def sem(self, name):
        self.sems.append(self.nc.alloc_semaphore(f"{self.tag}_{name}"))
        return self.sems[-1]

    def block(self):
        return self.nc.Block()


def norm_phase(nc, G, tag, load=None, keep=None, ternary=None):
    with Phase(nc, tag) as ph:
        stats = ph.sb("stats", [P, 2, TPB, 6])
        mv = ph.sb("mv", [P, BLOCKS * TPB, 2])
        veps = ph.sb("veps", [P, BLOCKS * TPB])
        neg_mean = ph.sb("neg_mean", [P, BLOCKS * TPB])
        rstd = ph.sb("rstd", [P, BLOCKS * TPB])
        shift = ph.sb("shift", [P, BLOCKS * TPB])
        xn = None if keep is not None else ph.sb("xn", [P, 2, TPB, D])
        low = ph.sb("low", [P, TPB, D]) if ternary else None
        turned = [ph.ps(f"turned{j}", [P, KC, BLK]) for j in range(2)]
        agg_done = ph.sem("agg_done")
        var_ready = ph.sem("var_ready")
        rstd_ready = ph.sem("rstd_ready")
        xn_ready = ph.sem("xn_ready")
        tern_ready = ph.sem("tern_ready")
        turn_done = ph.sem("turn_done")
        out_act = ph.sem("out_act")
        out_dve = ph.sem("out_dve")
        dve_steps = ph.sem("dve_steps")
        x_flat = G.x[:].rearrange("p b i d -> p (b i) d")
        xnT_flat = G.xnT[:].rearrange("p k b t -> p k (b t)")
        keep_flat = keep[:].rearrange("p b i d -> p (b i) d") if keep is not None else None

        def rows(n):
            return slice(n * TPB, (n + 1) * TPB)

        def normal(n, j):
            return keep_flat[:, n * TPB + j] if keep is not None else xn[:, n % 2, j]

        with ph.block() as block:
            if load:
                @block.sync
                def _(sp):
                    load(sp)

            @block.gpsimd
            def _(pool):
                for n in range(BLOCKS):
                    pool.wait_ge(var_ready, 2 * n + 2)
                    nc.gpsimd.tensor_tensor(rstd[:, rows(n)], veps[:, rows(n)], G.minus_half[:], ALU.pow)\
                        .then_inc(rstd_ready, 1)
                    pool.wait_ge(rstd_ready, 2 * n + 1)
                    nc.gpsimd.tensor_tensor(shift[:, rows(n)], neg_mean[:, rows(n)], rstd[:, rows(n)], ALU.mult)\
                        .then_inc(rstd_ready, 1)

            @block.vector
            def _(dve):
                steps = Steps(dve, dve_steps)
                for n in range(BLOCKS):
                    for j in range(TPB):
                        s = steps.mark(nc.vector.bn_stats(stats[:, n % 2, j], x_flat[:, n * TPB + j]))
                    steps.hold(s)
                    for j in range(TPB):
                        nc.vector.bn_aggr(mv[:, n * TPB + j], stats[:, n % 2, j]).then_inc(agg_done, 1)
                    dve.wait_ge(agg_done, (n + 1) * TPB)
                    nc.vector.tensor_scalar(veps[:, rows(n)], mv[:, rows(n), 1], EPS, None, ALU.add).then_inc(var_ready, 1)
                    nc.vector.tensor_scalar(neg_mean[:, rows(n)], mv[:, rows(n), 0], -1.0, None, ALU.mult).then_inc(var_ready, 1)
                for n in range(BLOCKS):
                    if ternary:
                        threshold, scale = ternary
                        part = xn[:, n % 2]
                        dve.wait_ge(xn_ready, n + 1)
                        steps.then(nc.vector.tensor_scalar(low[:], part, -threshold, scale, ALU.is_lt, ALU.mult))
                        steps.then(nc.vector.tensor_scalar(part, part, threshold, scale, ALU.is_gt, ALU.mult))
                        nc.vector.tensor_tensor(part, part, low[:], ALU.subtract).then_inc(tern_ready, 1)
                        dve.wait_ge(tern_ready, n + 1)
                    dve.wait_ge(turn_done, n + 1)
                    nc.vector.tensor_copy(xnT_flat[:, 1, n * BLK:(n + 1) * BLK], turned[n % 2][:, 1]).then_inc(out_dve, 1)

            @block.tensor
            def _(pe):
                for n in range(BLOCKS):
                    pe.wait_ge(tern_ready if ternary else xn_ready, n + 1)
                    if n >= 2:
                        pe.wait_ge(out_act, n - 1)
                        pe.wait_ge(out_dve, n - 1)
                    for k in range(KC):
                        for j in range(TPB):
                            ins = nc.tensor.transpose(turned[n % 2][:, k, j * P:(j + 1) * P],
                                                      normal(n, j)[:, k * P:(k + 1) * P], G.ident[:])
                    ins.then_inc(turn_done, 1)

            @block.scalar
            def _(act):
                def empty(n):
                    act.wait_ge(turn_done, n + 1)
                    nc.scalar.copy(xnT_flat[:, 0, n * BLK:(n + 1) * BLK], turned[n % 2][:, 0]).then_inc(out_act, 1)

                for n in range(BLOCKS):
                    act.wait_ge(rstd_ready, 2 * n + 2)
                    if n >= 2:
                        act.wait_ge(turn_done, n - 1)
                    for j in range(TPB):
                        at = slice(n * TPB + j, n * TPB + j + 1)
                        ins = nc.scalar.activation(normal(n, j), x_flat[:, n * TPB + j], ACT.Identity,
                                                   bias=shift[:, at], scale=rstd[:, at])
                    ins.then_inc(xn_ready, 1)
                    if n:
                        empty(n - 1)
                empty(BLOCKS - 1)


NH, NKV, HD = 16, 4, 128
GROUP = NH // NKV
CAP = 50.0


def load_l0_attn(nc, G, W, sem):
    def load(sp):
        I = G.dram
        for dst, src in ((W.q[:], I["L0_attn_q_kernel"].rearrange("(k p) n -> p k n", p=P)),
                         (W.k[:], I["L0_attn_k_kernel"].rearrange("(k p) n -> p k n", p=P)),
                         (W.v[:], I["L0_attn_v_kernel"].rearrange("(k p) n -> p k n", p=P)),
                         (W.o[:], I["L0_attn_out_kernel"].rearrange("(h p) n -> p h n", p=P)),
                         (W.cos[:], I["l0_cos"]), (W.sin[:], I["l0_sin"])):
            sp.dma_start(dst, src).then_inc(sem, 16)
    return load


def l0_attn(nc, G):
    with Phase(nc, "l0w") as W:
        W.q = W.sb("q", [P, KC, NH * HD])
        W.k = W.sb("k", [P, KC, NKV * HD])
        W.v = W.sb("v", [P, KC, NKV * HD])
        W.o = W.sb("o", [P, NH, D])
        W.cos = W.sb("cos", [P, SEQ])
        W.sin = W.sb("sin", [P, SEQ])
        w_in = W.sem("w_in")
        LOADS = 6 * 16
        norm_phase(nc, G, "l0n", load=load_l0_attn(nc, G, W, w_in))
        l0_attn_tiles(nc, G, W, w_in, LOADS)


def l0_attn_tiles(nc, G, W, w_in, LOADS):
    with Phase(nc, "l0a") as ph:
        xs = ph.sb("xs", [P, KC, NB, P])
        qT = ph.sb("qT", [P, NH, NB, P])
        kT = ph.sb("kT", [P, 2, NKV, NB, P])
        v = ph.sb("v", [P, 2, NB, NKV, HD + 1])
        rope_a = ph.sb("rope_a", [P, 2, BLK])
        rope_b = ph.sb("rope_b", [P, 2, BLK])
        capped = ph.sb("capped", [P, 2, BLK])
        probs = ph.sb("probs", [P, 2, 2, BLK])
        rden = ph.sb("rden", [P, GROUP])
        enc = ph.sb("enc", [P, 2, GROUP, HD])
        encT = ph.sb("encT", [P, NB, NH, P])
        proj = ph.ps("proj", [P, 2, BLK])
        score = ph.ps("score", [P, 2, BLK])
        pv = ph.ps("pv", [P, 2, BLK])
        turned = ph.ps("turned", [P, BLK])
        y = ph.ps("y", [P, NB, D])

        UNITS = NKV * NB
        KB, QB = NKV // 2, NH // 2
        ROPES = KB + QB
        SCALE = float(HD) ** -0.5 / CAP

        xs_ready = ph.sem("xs_ready")
        proj_done = ph.sem("proj_done")
        roped = ph.sem("roped")
        rotated = ph.sem("rotated")
        v_ready = ph.sem("v_ready")
        score_done = ph.sem("score_done")
        tanh_done = ph.sem("tanh_done")
        exp_done = ph.sem("exp_done")
        masked = ph.sem("masked")
        pv_done = ph.sem("pv_done")
        enc_done = ph.sem("enc_done")
        turn_done = ph.sem("turn_done")
        encT_done = ph.sem("encT_done")
        y_done = ph.sem("y_done")
        x_added = ph.sem("x_added")
        dve_steps = ph.sem("dve_steps")
        apart = ph.sem("apart")
        cleared = ph.sem("cleared")
        BANKS = KB + NB + QB
        n_rope = {**{("k", j): j + 1 for j in range(KB)}, **{("q", j): KB + j + 1 for j in range(QB)}}

        def q_banks(u):
            g = u // NB + 1
            return (2 * g, 2 * g + 1) if u % NB == 0 and g < NKV else ()

        def turns(eng, begin, body):
            begin(0, 0)
            with eng.Fori(0, TILES // 2 - 1) as it:
                for par in range(2):
                    body(it * 2 + par, par, it * 2 + par + 1)
            body(TILES - 2, 0, TILES - 1)
            body(TILES - 1, 1, None)

        with ph.block() as block:
            @block.gpsimd
            def _(pool):
                nc.gpsimd.memset(kT[:], 0.0).then_inc(cleared, 1)
                nc.gpsimd.memset(v[:], 0.0).then_inc(cleared, 1)
                pool.sem_inc(rotated, ROPES)

                def stage(t):
                    hold_apart(pool, proj_done, before(t, BANKS, BANKS), apart)
                    nc.gpsimd.tensor_copy(xs[:], G.xnT[:, :, :, bass.ds(t * P, P)]).then_inc(xs_ready, 1)

                def rotate(t, par, kind, j):
                    n = n_rope[kind, j]
                    pool.wait_ge(roped, now(t, ROPES, n, credit=True))
                    dst = kT[:, par, 2 * j:2 * j + 2] if kind == "k" else qT[:, 2 * j:2 * j + 2]
                    nc.gpsimd.tensor_tensor(dst.rearrange("p h b t -> p (h b t)"),
                                            rope_a[:, n % 2], rope_b[:, n % 2], ALU.add)\
                        .then_inc(rotated, 1)

                def begin(t, par):
                    for j in range(KB):
                        rotate(t, par, "k", j)
                    hold_apart(pool, pv_done, before(t, UNITS, UNITS), apart)
                    nc.gpsimd.memset(v[:, par, :, :, HD:HD + 1], 1.0)
                    for j in range(2):
                        rotate(t, par, "q", j)

                def mask(t, u):
                    for c in range(2):
                        hold_apart(pool, exp_done, now(t, 2 * UNITS, 2 * u + c + 1), apart)
                        part = probs[:, u % 2, c].rearrange("p (h t) -> p h t", h=GROUP)
                        sign = 1 if c == 0 else -1
                        nc.gpsimd.affine_select(out=part, in_=part, compare_op=ALU.is_ge, fill=0.0,
                                                base=0, pattern=[[0, GROUP], [sign, P]],
                                                channel_multiplier=-sign).then_inc(masked, 1)

                def body(t, par, nxt):
                    for u in range(UNITS):
                        for j in q_banks(u):
                            rotate(t, par, "q", j)
                        mask(t, u)
                        if u == UNITS - 3 and nxt is not None:
                            stage(nxt)
                    if nxt is not None:
                        begin(nxt, 1 - par)

                pool.wait_ge(cleared, 2)
                stage(0)
                turns(pool, begin, body)

            @block.tensor
            def _(pe):
                pe.sem_inc(proj_done, BANKS)
                pe.sem_inc(pv_done, UNITS)
                pe.sem_inc(turn_done, UNITS)
                pe.sem_inc(y_done, 1)
                pe.wait_ge(w_in, LOADS)

                def free_bank(t, n):
                    n -= 2
                    back = n < 0
                    n %= BANKS
                    at = before if back else (lambda i, per, m: now(i, per, m, credit=True))
                    if KB <= n < KB + NB:
                        pe.wait_ge(v_ready, at(t, NB, n - KB + 1))
                    else:
                        pe.wait_ge(roped, at(t, ROPES, (n if n < KB else n - NB) + 1))

                def project(t, w, n, j):
                    free_bank(t, n)
                    for h in range(2):
                        for k in range(KC):
                            ins = nc.tensor.matmul(proj[:, n % 2, h * NB * P:(h + 1) * NB * P],
                                                   w[:, k, (2 * j + h) * HD:(2 * j + h + 1) * HD],
                                                   xs[:, k].rearrange("p b t -> p (b t)"),
                                                   start=(k == 0), stop=(k == KC - 1))
                    ins.then_inc(proj_done, 1)

                def project_keys(t):
                    pe.wait_ge(xs_ready, now(t, 1, 1))
                    for j in range(KB):
                        project(t, W.k, j, j)

                def project_rest(t):
                    for b in range(NB):
                        n = KB + b
                        free_bank(t, n)
                        for k in range(KC):
                            ins = nc.tensor.matmul(proj[:, n % 2], xs[:, k, b], W.v[:, k, :],
                                                   start=(k == 0), stop=(k == KC - 1))
                        ins.then_inc(proj_done, 1)
                    for j in range(2):
                        project(t, W.q, KB + NB + j, j)

                def scores(t, par, u):
                    g, b = u // NB, u % NB
                    pe.wait_ge(rotated, now(t, ROPES, n_rope["q", 2 * g + 1], credit=True))
                    for c in range(2):
                        if u:
                            pe.wait_ge(tanh_done, now(t, 2 * UNITS, 2 * (u - 1) + c + 1, credit=True))
                        else:
                            pe.wait_ge(tanh_done, before(t, 2 * UNITS, 2 * (UNITS - 1) + c + 1))
                        nc.tensor.matmul(score[:, c], kT[:, par ^ c, g, b],
                                         qT[:, g * GROUP:(g + 1) * GROUP, b, :],
                                         start=True, stop=True).then_inc(score_done, 1)

                def weigh(t, par, u):
                    g, b = u // NB, u % NB
                    pe.wait_ge(masked, now(t, 2 * UNITS, 2 * u + 2))
                    if u == 0:
                        pe.wait_ge(v_ready, now(t, NB, NB, credit=True))
                    if u:
                        pe.wait_ge(enc_done, now(t, UNITS, u, credit=True))
                    else:
                        pe.wait_ge(enc_done, before(t, UNITS, UNITS))
                    for h in range(GROUP):
                        at = (h % 2) * (HD + 1)
                        for c in range(2):
                            ins = nc.tensor.matmul(pv[:, h // 2, at:at + HD + 1],
                                                   probs[:, u % 2, c, h * P:(h + 1) * P],
                                                   v[:, par ^ c, b, g, :], start=(c == 0), stop=(c == 1))
                    ins.then_inc(pv_done, 1)

                def turn(t, u):
                    pe.wait_ge(enc_done, now(t, UNITS, u + 1, credit=True))
                    if u:
                        pe.wait_ge(encT_done, now(t, UNITS, u, credit=True))
                    else:
                        pe.wait_ge(encT_done, before(t, UNITS, UNITS))
                    for h in range(GROUP):
                        ins = nc.tensor.transpose(turned[:, h * P:(h + 1) * P], enc[:, u % 2, h], G.ident[:])
                    ins.then_inc(turn_done, 1)

                def begin(t, par):
                    project_keys(t)
                    project_rest(t)

                def body(t, par, nxt):
                    for u in range(UNITS):
                        scores(t, par, u)
                        for j in q_banks(u):
                            project(t, W.q, KB + NB + j, j)
                        if u >= 1:
                            weigh(t, par, u - 1)
                        if u >= 2:
                            turn(t, u - 2)
                    if nxt is not None:
                        project_keys(nxt)
                    weigh(t, par, UNITS - 1)
                    turn(t, UNITS - 2)
                    if nxt is not None:
                        project_rest(nxt)
                    turn(t, UNITS - 1)
                    pe.wait_ge(x_added, before(t, 1, 1))
                    for b in range(NB):
                        pe.wait_ge(encT_done, now(t, UNITS, UNITS - NB + 1 + b, credit=True))
                        for h in range(NH):
                            ins = nc.tensor.matmul(y[:, b], encT[:, b, h], W.o[:, h], start=(h == 0), stop=(h == NH - 1))
                    ins.then_inc(y_done, 1)

                turns(pe, begin, body)

            @block.scalar
            def _(act):
                act.sem_inc(v_ready, NB)
                act.sem_inc(tanh_done, 2 * UNITS)
                act.sem_inc(encT_done, UNITS)
                act.wait_ge(cleared, 2)

                def begin(t, par):
                    for b in range(NB):
                        act.wait_ge(proj_done, now(t, BANKS, KB + b + 1, credit=True))
                        nc.scalar.copy(v[:, par, b, :, 0:HD], proj[:, (KB + b) % 2].rearrange("p (g d) -> p g d", g=NKV))\
                            .then_inc(v_ready, 1)

                def softmax_part(t, u):
                    for c in range(2):
                        act.wait_ge(score_done, now(t, 2 * UNITS, 2 * u + c + 1))
                        if u:
                            act.wait_ge(exp_done, now(t, 2 * UNITS, 2 * (u - 1) + c + 1))
                        nc.scalar.activation(capped[:, c], score[:, c], ACT.Tanh, scale=SCALE).then_inc(tanh_done, 1)
                    for c in range(2):
                        act.wait_ge(tanh_done, now(t, 2 * UNITS, 2 * u + c + 1, credit=True))
                        if c == 0:
                            act.wait_ge(pv_done, now(t, UNITS, u - 1, credit=True))
                        nc.scalar.activation(probs[:, u % 2, c], capped[:, c], ACT.Exp, scale=CAP)\
                            .then_inc(exp_done, 1)

                def evacuate(t, u):
                    g, b = u // NB, u % NB
                    act.wait_ge(turn_done, now(t, UNITS, u + 1, credit=True))
                    if u == 0:
                        act.wait_ge(y_done, before(t, 1, 1))
                    nc.scalar.copy(encT[:, b, g * GROUP:(g + 1) * GROUP].rearrange("p h t -> p (h t)"), turned[:])\
                        .then_inc(encT_done, 1)

                def body(t, par, nxt):
                    for u in range(UNITS):
                        softmax_part(t, u)
                        if u >= 2:
                            evacuate(t, u - 2)
                    evacuate(t, UNITS - 2)
                    if nxt is not None:
                        begin(nxt, 1 - par)
                    evacuate(t, UNITS - 1)

                turns(act, begin, body)

            @block.vector
            def _(dve):
                dve.sem_inc(roped, ROPES)
                dve.sem_inc(enc_done, UNITS)
                dve.sem_inc(x_added, 1)
                dve.wait_ge(w_in, LOADS)
                H = HD // 2

                def rope(t, kind, j):
                    cos = spread(W.cos[:, bass.ds(t * P, P)].unsqueeze(1), [P, 4, P])
                    sin = W.sin[:, bass.ds(t * P, P)].unsqueeze(1)
                    n = n_rope[kind, j]
                    bank = (j if kind == "k" else KB + NB + j)
                    dve.wait_ge(proj_done, now(t, BANKS, bank + 1, credit=True))
                    dve.wait_ge(rotated, now(t, ROPES, n - 2, credit=True))
                    src = proj[:, bank % 2].rearrange("p (r t) -> p r t", t=P)
                    a = rope_a[:, n % 2].rearrange("p (r t) -> p r t", t=P)
                    b = rope_b[:, n % 2].rearrange("p (r t) -> p r t", t=P)
                    nc.vector.tensor_tensor(a, src, cos, ALU.mult)
                    nc.vector.tensor_tensor(b[0:H], src[H:HD], spread(sin[H:HD], [H, 4, P]), ALU.mult)
                    nc.vector.tensor_tensor(b[H:HD], src[0:H], spread(sin[0:H], [H, 4, P]), ALU.mult)\
                        .then_inc(roped, 1)

                def begin(t, par):
                    for j in range(KB):
                        rope(t, "k", j)
                    for j in range(2):
                        rope(t, "q", j)

                def body(t, par, nxt):
                    steps = Steps(dve, dve_steps, t, UNITS)

                    def normalise(u):
                        dve.wait_ge(pv_done, now(t, UNITS, u + 1, credit=True))
                        dve.wait_ge(turn_done, now(t, UNITS, u - 1, credit=True))
                        rows = pv[:, :, 0:2 * (HD + 1)].rearrange("p a (h d) -> p a h d", h=2)
                        r = rden[:].rearrange("p (a h d) -> p a h d", a=2, h=2)
                        steps.then(nc.vector.reciprocal(r, rows[:, :, :, HD:HD + 1]))
                        nc.vector.tensor_tensor(enc[:, u % 2].rearrange("p (a h) d -> p a h d", a=2),
                                                rows[:, :, :, 0:HD], spread(r, [P, 2, 2, HD]), ALU.mult)\
                            .then_inc(enc_done, 1)

                    for u in range(UNITS):
                        for j in q_banks(u):
                            rope(t, "q", j)
                        if u >= 1:
                            normalise(u - 1)
                    if nxt is not None:
                        for j in range(KB):
                            rope(nxt, "k", j)
                    normalise(UNITS - 1)
                    if nxt is not None:
                        for j in range(2):
                            rope(nxt, "q", j)
                    dve.wait_ge(y_done, now(t, 1, 1, credit=True))
                    x_tile = G.x[:, :, bass.ds(t, 1), :].rearrange("p b i d -> p b (i d)")
                    nc.vector.tensor_tensor(x_tile, y[:], x_tile, ALU.add).then_inc(x_added, 1)
                    steps.close()

                turns(dve, begin, body)



def staged_linear(nc, G, tag, wT, bias, w_in=None, loads=0):
    PAIRS = 2
    with Phase(nc, tag) as ph:
        xs = ph.sb("xs", [P, PAIRS, KC, NB, P])
        y = [ph.ps(f"y{j}", [P, NB, D]) for j in range(PAIRS)]
        xs_ready = ph.sem("xs_ready")
        y_done = ph.sem("y_done")
        x_added = ph.sem("x_added")
        dve_steps = ph.sem("dve_steps")
        apart = ph.sem("apart")
        with ph.block() as block:
            @block.gpsimd
            def _(pool):
                with pool.Fori(0, TILES // PAIRS) as it:
                    for j in range(PAIRS):
                        hold_apart(pool, y_done, before(it, PAIRS, j + 1), apart)
                        nc.gpsimd.tensor_copy(xs[:, j], G.xnT[:, :, :, bass.ds((it * PAIRS + j) * P, P)])\
                            .then_inc(xs_ready, 1)

            @block.tensor
            def _(pe):
                pe.sem_inc(y_done, PAIRS)
                if w_in is not None:
                    pe.wait_ge(w_in, loads)
                with pe.Fori(0, TILES // PAIRS) as it:
                    for j in range(PAIRS):
                        pe.wait_ge(xs_ready, now(it, PAIRS, j + 1))
                        pe.wait_ge(x_added, before(it, PAIRS, j + 1))
                        for b in range(NB):
                            for k in range(KC):
                                ins = nc.tensor.matmul(y[j][:, b], xs[:, j, k, b], wT[:, k], start=(k == 0), stop=(k == KC - 1))
                        ins.then_inc(y_done, 1)

            @block.vector
            def _(dve):
                dve.sem_inc(x_added, PAIRS)
                if w_in is not None:
                    dve.wait_ge(w_in, loads)
                with dve.Fori(0, TILES // PAIRS) as it:
                    steps = Steps(dve, dve_steps, it, PAIRS if bias is not None else 0)
                    for j in range(PAIRS):
                        dve.wait_ge(y_done, now(it, PAIRS, j + 1, credit=True))
                        x_tile = G.x[:, :, bass.ds(it * PAIRS + j, 1), :].rearrange("p b i d -> p b (i d)")
                        if bias is not None:
                            steps.then(nc.vector.tensor_tensor(x_tile, x_tile, spread(bias[:].unsqueeze(1), [P, NB, D]), ALU.add))
                        nc.vector.tensor_tensor(x_tile, y[j][:], x_tile, ALU.add).then_inc(x_added, 1)
                    steps.close()


def l0_ffn(nc, G):
    with Phase(nc, "f0w") as W:
        w = W.sb("w", [P, KC, D])
        bias = W.sb("bias", [P, D])
        wT = W.sb("wT", [P, KC, D])
        w_in = W.sem("w_in")

        def load(sp):
            sp.dma_start(w[:], G.dram["L0_ffn_weight"].rearrange("(k p) n -> p k n", p=P)).then_inc(w_in, 16)
            sp.dma_start(bias[:], G.dram["L0_ffn_bias"].partition_broadcast(P)).then_inc(w_in, 16)
        norm_phase(nc, G, "f0n", load=load)
        with Phase(nc, "f0b") as ph:
            alpha = ph.sb("alpha", [P, KC])
            bw = ph.sb("bw", [P, KC, D])
            turned = ph.ps("turned", [P, KC, D])
            steps_sem, bw_ready, turn_done = ph.sem("steps"), ph.sem("bw_ready"), ph.sem("turn_done")
            with ph.block() as block:
                @block.vector
                def _(dve):
                    steps = Steps(dve, steps_sem)
                    dve.wait_ge(w_in, 2 * 16)
                    nc.vector.tensor_reduce(alpha[:], w[:], AX.X, ALU.add, apply_absolute_value=True)
                    steps.then(nc.vector.tensor_scalar(bw[:], w[:], 0.0, 2.0, ALU.is_ge, ALU.mult))
                    steps.then(nc.vector.tensor_scalar(alpha[:], alpha[:], 1.0 / D, None, ALU.mult))
                    for k in range(KC):
                        n = steps.mark(nc.vector.tensor_scalar(bw[:, k], bw[:, k], -1.0, alpha[:, k:k + 1], ALU.add, ALU.mult))
                    steps.hold(n)
                    steps.then(nc.vector.tensor_tensor(bw[:], bw[:], w[:], ALU.subtract))
                    nc.vector.tensor_tensor(bw[:], bw[:], w[:], ALU.add).then_inc(bw_ready, 1)
                    dve.wait_ge(turn_done, 1)
                    nc.vector.tensor_copy(wT[:], turned[:])

                @block.tensor
                def _(pe):
                    pe.wait_ge(bw_ready, 1)
                    for k in range(KC):
                        for o in range(KC):
                            ins = nc.tensor.transpose(turned[:, k, o * P:(o + 1) * P], bw[:, o, k * P:(k + 1) * P], G.ident[:])
                    ins.then_inc(turn_done, 1)
        staged_linear(nc, G, "f0l", wT, bias)


QL, KVL, DR, DK, DV = 192, 64, 64, 128, 128
PAIRS = NH // 2
QREST = QL - P
IH, ID, TOPK = 8, 128, 8
SEL = IH * TOPK
BIG = -1e30


def load_l1_attn(nc, G, W, sem):
    def load(sp):
        I = G.dram
        for dst, src in ((W.early["qcT"][:], I["l1_qcT"]), (W.early["kcT"][:], I["l1_kcT"]), (W.early["vT"][:], I["l1_vT"]),
                         (W.early["o"][:], I["L1_attn_W_o"].rearrange("(h p) n -> p h n", p=P)),
                         (W.q0[:, :, 0:P], I["l1_qr"][0:P]), (W.q1[:, :, 0:P], I["l1_qr"][P:QL]),
                         (W.early["k"][:], I["l1_k"].rearrange("(k p) n -> p k n", p=P)),
                         (W.early["cp"][:], I["L1_attn_W_cp"].rearrange("(k p) n -> p k n", p=P)),
                         (W.early["gate"][:], I["L1_attn_W_gate"].rearrange("(k p) n -> p k n", p=P)),
                         (W.early["idx"][:], I["L1_attn_W_idx"].rearrange("(k p) n -> p k n", p=P)),
                         (W.early["sq"][:], I["L1_attn_W_sq"]), (W.early["sk"][:], I["L1_attn_W_sk"]), (W.early["sv"][:], I["L1_attn_W_sv"]),
                         (W.early["iout"][:], I["L1_attn_W_iout"][:, 0:DV]),
                         (W.cos[:], I["l1_cos"]), (W.sin[:], I["l1_sin"]),
                         (W.early["iota"][:], I["l1_iota"]), (W.early["same"][:], I["l1_same"]), (W.early["mean"][:], I["l1_mean"])):
            sp.dma_start(dst, src).then_inc(sem, 16)
            W.loads += 16
    return load


def l1_attn(nc, G):
    with Phase(nc, "l1w") as W:
        W.loads = 0
        W.q0 = W.sb("q0", [P, PAIRS, 2 * P])
        W.q1 = W.sb("q1", [QREST, PAIRS, 2 * P])
        W.m = W.sb("m", [P, PAIRS, D])
        W.cos = W.sb("cos", [P, SEQ])
        W.sin = W.sb("sin", [P, SEQ])
        W.kA = W.sb("kA", [P, NB, SEQ])
        W.kB = W.sb("kB", [P, NB, SEQ])
        W.cp0 = W.sb("cp0", [P, NB, SEQ])
        W.cp1 = W.sb("cp1", [QREST, NB, SEQ])
        W.c = W.sb("c", [P, NB, TILES, KVL])
        W.row = W.sb("row", [P, NB, D])
        W.w_in = W.sem("w_in")
        with Phase(nc, "l1v") as V:
            for name, shape in (("qcT", [P, NH, QL]), ("kcT", [P, NH, KVL]), ("vT", [P, NH, KVL]), ("o", [P, NH, D]),
                                ("k", [P, KC, 3 * DR]), ("cp", [P, KC, QL]), ("gate", [P, KC, IH]),
                                ("idx", [P, KC, IH * ID]), ("sq", [ID, ID]), ("sk", [ID, ID]), ("sv", [ID, ID]),
                                ("iout", [ID, DV]), ("iota", [P, TILES]), ("same", [P, P]), ("mean", [P, NB * IH]),
                                ("xn", [P, NB, TILES, D]), ("gateT", [IH, NB, SEQ])):
                V.sb(name, shape)
            W.early = V
            norm_phase(nc, G, "l1n", load=load_l1_attn(nc, G, W, W.w_in), keep=W.early["xn"])
            l1_weights(nc, G, W)
            l1_latents(nc, G, W)
            l1_sparse(nc, G, W)
        for b in range(NB):
            with Phase(nc, f"l1q{b}") as Q:
                Q.q = Q.sb("q", [P, PAIRS, 2, SEQ])
                l1_queries(nc, G, W, Q, b)
                l1_attend(nc, G, W, Q, b)


def l1_weights(nc, G, W):
    with Phase(nc, "l1p") as ph:
        ab = ph.ps("ab", [P, 2, BLK])
        rest = ph.ps("rest", [QREST, 2, BLK])
        m = ph.ps("m", [P, PAIRS // 2, 2, D])
        made = ph.sem("made")
        with ph.block() as block:
            @block.tensor
            def _(pe):
                pe.wait_ge(W.w_in, W.loads)
                for h in range(NH):
                    pair, odd = h // 2, h % 2
                    at = (pair % 4) * P + (0 if odd else KVL)
                    nc.tensor.matmul(ab[:, pair // 4, at:at + KVL], W.early["qcT"][:, h, 0:P], W.early["kcT"][:, h], start=True, stop=True)
                    nc.tensor.matmul(rest[:, pair // 4, at:at + KVL], W.early["qcT"][:, h, P:QL], W.early["kcT"][:, h], start=True, stop=True)
                    ins = nc.tensor.matmul(m[odd * KVL:(odd + 1) * KVL, pair // 2, pair % 2], W.early["vT"][:, h], W.early["o"][:, h],
                                           start=True, stop=True)
                ins.then_inc(made, 1)

            @block.scalar
            def _(act):
                act.wait_ge(made, 1)
                nc.scalar.copy(W.m[:], m[:].rearrange("p a b n -> p (a b) n"))

            @block.vector
            def _(dve):
                dve.wait_ge(W.w_in, W.loads)
                dve.wait_ge(made, 1)
                nc.vector.tensor_copy(W.q0[:, :, P:2 * P], ab[:].rearrange("p a (b n) -> p (a b) n", n=P))
                nc.vector.tensor_copy(W.q1[:, :, P:2 * P], rest[:].rearrange("p a (b n) -> p (a b) n", n=P))


def l1_latents(nc, G, W):
    with Phase(nc, "l1l") as ph:
        xs = ph.sb("xs", [P, KC, BLK])
        rope_a = ph.sb("rope_a", [DR, BLK])
        rope_b = ph.sb("rope_b", [DR, BLK])
        key = ph.ps("key", [P, BLK])
        swapped = ph.ps("swapped", [DR, BLK])
        cp0, cp1 = ph.ps("cp0", [P, BLK]), ph.ps("cp1", [QREST, BLK])
        gate = ph.ps("gate", [IH, BLK])
        ctok = ph.ps("ctok", [P, TPB, KVL])
        xs_ready = ph.sem("xs_ready")
        key_done = ph.sem("key_done")
        all_done = ph.sem("all_done")
        act_done = ph.sem("act_done")
        dve_done = ph.sem("dve_done")
        dve_steps = ph.sem("dve_steps")
        apart = ph.sem("apart")
        flat = lambda t: t[:].rearrange("p b t -> p (b t)")
        xnT = G.xnT[:].rearrange("p k b t -> p k (b t)")
        c_flat = W.c[:].rearrange("p b i d -> p (b i) d")
        with ph.block() as block:
            @block.gpsimd
            def _(pool):
                with pool.Fori(0, BLOCKS) as it:
                    hold_apart(pool, all_done, before(it, 1, 1), apart)
                    nc.gpsimd.tensor_copy(xs[:], xnT[:, :, bass.ds(it * BLK, BLK)]).then_inc(xs_ready, 1)

            @block.tensor
            def _(pe):
                pe.sem_inc(all_done, 1)
                pe.wait_ge(W.w_in, W.loads)
                with pe.Fori(0, BLOCKS) as it:
                    def product(out, w):
                        for k in range(KC):
                            ins = nc.tensor.matmul(out, w(k), xs[:, k], start=(k == 0), stop=(k == KC - 1))
                        return ins
                    pe.wait_ge(xs_ready, now(it, 1, 1))
                    pe.wait_ge(act_done, before(it, 1, 1))
                    pe.wait_ge(dve_done, before(it, 1, 1))
                    product(key[:], lambda k: W.early["k"][:, k, 0:P])
                    product(swapped[:], lambda k: W.early["k"][:, k, P:P + DR]).then_inc(key_done, 1)
                    product(cp0[:], lambda k: W.early["cp"][:, k, 0:P])
                    product(cp1[:], lambda k: W.early["cp"][:, k, P:QL])
                    product(gate[:], lambda k: W.early["gate"][:, k])
                    for j in range(TPB):
                        for k in range(KC):
                            ins = nc.tensor.matmul(ctok[:, j], xs[:, k, j * P:(j + 1) * P], W.early["k"][:, k, DR:P],
                                                   start=(k == 0), stop=(k == KC - 1))
                    ins.then_inc(all_done, 1)

            @block.scalar
            def _(act):
                act.sem_inc(act_done, 1)
                with act.Fori(0, BLOCKS) as it:
                    cols = bass.ds(it * BLK, BLK)
                    act.wait_ge(key_done, now(it, 1, 1))
                    nc.scalar.copy(flat(W.kA)[DR:P, cols], key[DR:P])
                    nc.scalar.copy(flat(W.kB)[0:KVL, cols], key[DR:P])
                    act.wait_ge(all_done, now(it, 1, 1, credit=True))
                    nc.scalar.copy(flat(W.cp0)[:, cols], cp0[:])
                    nc.scalar.copy(flat(W.cp1)[:, cols], cp1[:])
                    nc.scalar.copy(flat(W.early["gateT"])[:, cols], gate[:])
                    nc.scalar.copy(c_flat[:, bass.ds(it * TPB, TPB), 0:KVL], ctok[:]).then_inc(act_done, 1)

            @block.vector
            def _(dve):
                dve.sem_inc(dve_done, 1)
                dve.wait_ge(W.w_in, W.loads)
                with dve.Fori(0, BLOCKS) as it:
                    steps = Steps(dve, dve_steps, it, 1)
                    cols = bass.ds(it * BLK, BLK)
                    pos = bass.ds((it % BPB) * BLK, BLK)
                    dve.wait_ge(key_done, now(it, 1, 1))
                    nc.vector.tensor_tensor(rope_a[:], key[0:DR], W.cos[0:DR, pos], ALU.mult)
                    steps.then(nc.vector.tensor_tensor(rope_b[:], swapped[:], W.sin[0:DR, pos], ALU.mult))
                    nc.vector.tensor_tensor(flat(W.kA)[0:DR, cols], rope_a[:], rope_b[:], ALU.add)
                    nc.vector.tensor_tensor(flat(W.kB)[DR:P, cols], rope_a[:], rope_b[:], ALU.add).then_inc(dve_done, 1)
                    steps.close()


def l1_sparse(nc, G, W):
    with Phase(nc, "l1s") as ph:
        top = ph.sb("top", [IH, NB, TOPK])
        index = ph.sb("index", [IH, NB, TOPK], U32)
        index_f = ph.sb("index_f", [IH, NB, TOPK])
        own = ph.sb("own", [IH, NB, IH, TOPK])
        ones = ph.sb("ones", [IH, P])
        pick = ph.sb("pick", [P, NB, TILES, SEL])
        selx = ph.sb("selx", [P, KC, NB, SEL])
        selT = ph.sb("selT", [ID, IH, NB * TOPK])
        sqT, skT, sv = (ph.sb(n, [P, P]) for n in ("sqT", "skT", "sv"))
        logits = ph.sb("logits", [P, P])
        top1 = ph.sb("top1", [P, 1])
        total = ph.sb("total", [P, 1])
        probs = ph.sb("probs", [P, P])
        weight = ph.sb("weight", [P, NB * IH])
        outT = ph.sb("outT", [P, NB * IH])
        ioT = ph.sb("ioT", [P, NB * IH])
        index_p = ph.ps("index_p", [P, NB, SEL])
        selx_p = ph.ps("selx_p", [P, KC, NB, SEL])
        selT_p = ph.ps("selT_p", [ID, IH, NB * TOPK])
        work = ph.ps("work", [P, 4, P])
        row_p = ph.ps("row_p", [P, NB, D])
        dve_sem, pe_sem = ph.sem("dve"), ph.sem("pe")
        exp_done = ph.sem("exp_done")
        marks = {}
        with ph.block() as block:
            @block.vector
            def _(dve):
                steps = Steps(dve, dve_sem)
                nc.vector.memset(ones[:], 1.0)
                for b in range(NB):
                    steps.then(nc.vector.max(top[:, b], W.early["gateT"][:, b]))
                    steps.then(nc.vector.max_index(index[:, b], top[:, b], W.early["gateT"][:, b]))
                steps.then(nc.vector.tensor_copy(index_f[:], index[:]))
                for b in range(NB):
                    n = steps.mark(nc.vector.tensor_tensor(
                        own[:, b], spread(index_f[:, b].unsqueeze(1), [IH, IH, TOPK]),
                        spread(G.ident[0:IH, 0:IH].unsqueeze(2), [IH, IH, TOPK]), ALU.mult))
                marks["own"] = n
                dve.wait_ge(pe_sem, 1)
                for i in range(TILES):
                    n = steps.mark(nc.vector.tensor_scalar(pick[:, :, i], index_p[:], W.early["iota"][:, i:i + 1], None, ALU.is_equal))
                marks["pick"] = n

                def copy(name, dst, src, after):
                    dve.wait_ge(pe_sem, after)
                    marks[name] = steps.mark(nc.vector.tensor_copy(dst, src))
                copy("selx", selx[:], selx_p[:], 2)
                copy("selT", selT[:], selT_p[:], 3)
                dve.wait_ge(pe_sem, 4)
                nc.vector.tensor_copy(sqT[:], work[:, 0])
                nc.vector.tensor_copy(skT[:], work[:, 1])
                copy("sqkv", sv[:], work[:, 2], 4)
                dve.wait_ge(pe_sem, 5)
                steps.then(nc.vector.scalar_tensor_tensor(logits[:], work[:, 3], float(ID) ** -0.5, W.early["same"][:], ALU.mult, ALU.add))
                steps.then(nc.vector.tensor_reduce(top1[:], logits[:], AX.X, ALU.max, negate=True))
                marks["top1"] = steps.n
                dve.wait_ge(exp_done, 1)
                steps.then(nc.vector.reciprocal(total[:], total[:]))
                marks["probs"] = steps.mark(nc.vector.tensor_scalar(probs[:], probs[:], total[:], None, ALU.mult))
                copy("weight", weight[:], work[:, 0, 0:NB * IH], 6)
                copy("outT", outT[:], work[:, 1, 0:NB * IH], 7)
                copy("ioT", ioT[:], work[:, 2, 0:NB * IH], 8)
                dve.wait_ge(pe_sem, 9)
                nc.vector.tensor_copy(W.row[:], row_p[:])

            @block.scalar
            def _(act):
                act.wait_ge(dve_sem, marks["top1"])
                nc.scalar.activation(probs[:], logits[:], ACT.Exp, bias=top1[:], accum_out=total[:]).then_inc(exp_done, 1)

            @block.tensor
            def _(pe):
                pe.wait_ge(dve_sem, marks["own"])
                for b in range(NB):
                    ins = nc.tensor.matmul(index_p[:, b], ones[:], own[:, b].rearrange("p h k -> p (h k)"), start=True, stop=True)
                ins.then_inc(pe_sem, 1)
                pe.wait_ge(dve_sem, marks["pick"])
                for b in range(NB):
                    for k in range(KC):
                        for i in range(TILES):
                            ins = nc.tensor.matmul(selx_p[:, k, b], W.early["xn"][:, b, i, k * P:(k + 1) * P], pick[:, b, i],
                                                   start=(i == 0), stop=(i == TILES - 1))
                ins.then_inc(pe_sem, 1)
                pe.wait_ge(dve_sem, marks["selx"])
                for h in range(IH):
                    for k in range(KC):
                        ins = nc.tensor.matmul(selT_p[:, h], W.early["idx"][:, k, h * ID:(h + 1) * ID],
                                               selx[:, k, :, h * TOPK:(h + 1) * TOPK], start=(k == 0), stop=(k == KC - 1))
                ins.then_inc(pe_sem, 1)
                pe.wait_ge(dve_sem, marks["selT"])
                sel = selT[:].rearrange("p h r -> p (h r)")
                nc.tensor.matmul(work[:, 0], W.early["sq"][:], sel, start=True, stop=True)
                nc.tensor.matmul(work[:, 1], W.early["sk"][:], sel, start=True, stop=True)
                nc.tensor.matmul(work[:, 2], sel, W.early["sv"][:], start=True, stop=True).then_inc(pe_sem, 1)
                pe.wait_ge(dve_sem, marks["sqkv"])
                nc.tensor.matmul(work[:, 3], sqT[:], skT[:], start=True, stop=True).then_inc(pe_sem, 1)
                pe.wait_ge(dve_sem, marks["probs"])
                nc.tensor.matmul(work[:, 0, 0:NB * IH], probs[:], W.early["mean"][:], start=True, stop=True).then_inc(pe_sem, 1)
                pe.wait_ge(dve_sem, marks["weight"])
                nc.tensor.matmul(work[:, 1, 0:NB * IH], sv[:], weight[:], start=True, stop=True).then_inc(pe_sem, 1)
                pe.wait_ge(dve_sem, marks["outT"])
                nc.tensor.matmul(work[:, 2, 0:NB * IH], W.early["iout"][:], outT[:], start=True, stop=True).then_inc(pe_sem, 1)
                pe.wait_ge(dve_sem, marks["ioT"])
                for b in range(NB):
                    for h in range(NH):
                        at = (h // (NH // IH)) * NB + b
                        ins = nc.tensor.matmul(row_p[:, b], spread(ioT[:, at:at + 1], [P, P]), W.early["o"][:, h],
                                               start=(h == 0), stop=(h == NH - 1))
                ins.then_inc(pe_sem, 1)


def l1_queries(nc, G, W, Q, b):
    with Phase(nc, f"l1r{b}") as ph:
        rope_a = ph.sb("rope_a", [P, 2, BLK])
        rope_b = ph.sb("rope_b", [P, 2, BLK])
        swapped = ph.sb("swapped", [P, 2, BLK])
        rotary = [ph.ps(f"rotary{j}", [P, BLK]) for j in range(2)]
        latent = [ph.ps(f"latent{j}", [P, BLK]) for j in range(2)]
        rotary_in = ph.sem("rotary_in")
        latent_in = ph.sem("latent_in")
        cos_done = ph.sem("cos_done")
        swap_done = ph.sem("swap_done")
        roped = ph.sem("roped")
        added = ph.sem("added")
        copied = ph.sem("copied")
        with ph.block() as block:
            @block.tensor
            def _(pe):
                with pe.Fori(0, BPB) as it:
                    for p in range(PAIRS):
                        def product(out, part):
                            nc.tensor.matmul(out[:], W.q0[:, p, part * P:(part + 1) * P],
                                             W.cp0[:, b, bass.ds(it * BLK, BLK)], start=True, stop=False)
                            return nc.tensor.matmul(out[:], W.q1[:, p, part * P:(part + 1) * P],
                                                    W.cp1[:, b, bass.ds(it * BLK, BLK)], start=False, stop=True)
                        pe.wait_ge(swap_done, it * PAIRS + p + 1)
                        product(rotary[p % 2], 0).then_inc(rotary_in, 1)
                        pe.wait_ge(copied, it * PAIRS + p + 1)
                        product(latent[p % 2], 1).then_inc(latent_in, 1)

            @block.vector
            def _(dve):
                dve.sem_inc(roped, 2)
                with dve.Fori(0, BPB) as it:
                    pos = bass.ds(it * BLK, BLK)

                    def times_sin(p):
                        dve.wait_ge(swap_done, it * PAIRS + p + 3)
                        nc.vector.tensor_tensor(rope_b[:, p % 2], swapped[:, p % 2], W.sin[:, pos], ALU.mult).then_inc(roped, 1)

                    for p in range(PAIRS):
                        dve.wait_ge(rotary_in, now(it, PAIRS, p + 1))
                        dve.wait_ge(added, it * PAIRS + p + 1)
                        nc.vector.tensor_tensor(rope_a[:, p % 2], rotary[p % 2][:], W.cos[:, pos], ALU.mult).then_inc(cos_done, 1)
                        if p:
                            times_sin(p - 1)
                    times_sin(PAIRS - 1)

            @block.gpsimd
            def _(pool):
                pool.sem_inc(added, 2)
                with pool.Fori(0, BPB) as it:
                    for p in range(PAIRS):
                        pool.wait_ge(roped, it * PAIRS + p + 3)
                        for odd in range(2):
                            half = slice(odd * DR, (odd + 1) * DR)
                            ins = nc.gpsimd.tensor_tensor(Q.q[half, p, odd, bass.ds(it * BLK, BLK)],
                                                          rope_a[half, p % 2], rope_b[half, p % 2], ALU.add)
                        ins.then_inc(added, 1)

            @block.scalar
            def _(act):
                act.sem_inc(copied, 2)
                act.sem_inc(swap_done, 2)
                H = DR // 2
                with act.Fori(0, BPB) as it:
                    for p in range(PAIRS):
                        act.wait_ge(cos_done, now(it, PAIRS, p + 1))
                        act.wait_ge(roped, it * PAIRS + p + 1)
                        for half in range(4):
                            other = half ^ 1
                            ins = nc.scalar.copy(swapped[half * H:(half + 1) * H, p % 2], rotary[p % 2][other * H:(other + 1) * H])
                        ins.then_inc(swap_done, 1)
                        act.wait_ge(latent_in, now(it, PAIRS, p + 1))
                        nc.scalar.copy(Q.q[KVL:P, p, 0, bass.ds(it * BLK, BLK)], latent[p % 2][KVL:P])
                        nc.scalar.copy(Q.q[0:KVL, p, 1, bass.ds(it * BLK, BLK)], latent[p % 2][0:KVL]).then_inc(copied, 1)


def l1_attend(nc, G, W, Q, b):
    with Phase(nc, f"l1a{b}") as ph:
        U = 4
        TURNS = NH // U
        CHUNK = BLK // P
        SCALE = 1.0 / float(np.sqrt(DK + DR))
        qs = ph.sb("qs", [P, U, P])
        neg_max = ph.sb("neg_max", [P, U])
        shift = ph.sb("shift", [P, U])
        row_sum = ph.sb("row_sum", [P, U])
        rden = ph.sb("rden", [P, U])
        rden_rows = ph.sb("rden_rows", [P, P])
        probs = ph.sb("probs", [P, U * BLK])
        probsT = ph.sb("probsT", [P, 2, TILES, P])
        pcT = ph.sb("pcT", [P, 2, PAIRS, P])
        identb = ph.sb("identb", [P, P], BF16)
        future = ph.sb("future", [P, P], BF16)
        score = ph.ps("score", [P, U * BLK])
        turned = [ph.ps(f"turned{j}", [P, BLK]) for j in range(2)]
        pv = ph.ps("pv", [P, 2, BLK // P, P])
        y = pv[:, 0, 2:4].rearrange("p a t -> p (a t)")
        const = ph.sem("const")
        apart = ph.sem("apart")
        qs_ready = ph.sem("qs_ready")
        score_done = ph.sem("score_done")
        max_done = ph.sem("max_done")
        shift_ready = ph.sem("shift_ready")
        exp_done = ph.sem("exp_done")
        turn_done = ph.sem("turn_done")
        evac = [ph.sem(f"evac{j}") for j in range(2)]
        pv_done = ph.sem("pv_done")
        pc_done = ph.sem("pc_done")
        rden_done = ph.sem("rden_done")
        laid_out = ph.sem("laid_out")
        rows_copied = ph.sem("rows_copied")
        y_done = ph.sem("y_done")
        x_added = ph.sem("x_added")
        row_added = ph.sem("row_added")

        def chunks(i):
            return -(-(i + 1) // CHUNK)

        def look(i):
            return U // chunks(i)

        def slot(i, u):
            return (u % look(i)) * chunks(i) * BLK

        turned_before = [0]
        uses = [1]
        for i in range(TILES):
            turned_before.append(turned_before[-1] + NH * chunks(i))
            uses.append(uses[-1] + NH * chunks(i) // 2)

        def use(i, it, u):
            return uses[i] + ((it * U + u) if chunks(i) == 2 else (it * (U // 2) + u // 2))

        def turns(i, it, u, c):
            return turned_before[i] + (it * U + u) * chunks(i) + c + 1

        def head(i, it, u):
            return it * U + (NH * i + u)

        def pair_of(i, it, u):
            return it * (U // 2) + (NH // 2 * i + u // 2)

        def scored(i, it, u, last):
            if last and i + 1 < TILES and look(i + 1) < look(i):
                u -= look(i) - look(i + 1)
                return (i + 1, u, NH * (i + 1) + u) if u >= 0 else None
            to = u + look(i)
            if last and to >= U:
                return (i + 1, to - U, NH * (i + 1) + to - U) if i + 1 < TILES else None
            return i, to % U, head(i, it, to)

        def for_turns(eng, step, end):
            for i in range(TILES):
                with eng.Fori(0, TURNS - 1) as it:
                    for u in range(U):
                        step(i, it, u, False)
                for u in range(U):
                    step(i, TURNS - 1, u, True)
                end(i)

        with ph.block() as block:
            @block.gpsimd
            def _(pool):
                nc.gpsimd.memset(identb[:], 0.0).then_inc(const, 1)
                nc.gpsimd.memset(future[:], 0.0).then_inc(const, 1)
                pool.wait_ge(const, 2)
                nc.gpsimd.affine_select(out=identb[:], in_=identb[:], compare_op=ALU.not_equal, fill=1.0,
                                        base=0, pattern=[[-1, P]], channel_multiplier=1).then_inc(const, 1)
                nc.gpsimd.affine_select(out=future[:], in_=future[:], compare_op=ALU.is_ge, fill=BIG,
                                        base=0, pattern=[[-1, P]], channel_multiplier=1).then_inc(const, 1)

                def step(i, it, u, last):
                    n = head(i, it, u)
                    if last and i + 1 == TILES:
                        return
                    if last:
                        src = Q.q[:, u // 2, u % 2, (i + 1) * P:(i + 2) * P]
                    else:
                        src = Q.q[:, bass.ds(it * (U // 2) + (U + u) // 2, 1), u % 2, i * P:(i + 1) * P].rearrange("p a t -> p (a t)")
                    hold_apart(pool, score_done, n + 1, apart)
                    nc.gpsimd.tensor_copy(qs[:, u], src).then_inc(qs_ready, 1)

                for u in range(U):
                    nc.gpsimd.tensor_copy(qs[:, u], Q.q[:, u // 2, u % 2, 0:P]).then_inc(qs_ready, 1)
                for_turns(pool, step, lambda i: None)

            @block.tensor
            def _(pe):
                pe.sem_inc(pv_done, 1)
                pe.wait_ge(const, 4)

                def scores(i, u, n):
                    pe.wait_ge(qs_ready, n + 1)
                    if not isinstance(n, int) or n >= look(i):
                        pe.wait_ge(exp_done, n - look(i) + 1)
                    keys = (W.kA, W.kB)[u % 2]
                    at, width = slot(i, u), (i + 1) * P
                    for c in range(chunks(i)):
                        lo, hi = c * BLK, min(width, (c + 1) * BLK)
                        nc.tensor.matmul(score[:, at + lo:at + hi], qs[:, u], keys[:, b, lo:hi], start=True,
                                         stop=(hi < width), skip_group_check=True)
                    nc.tensor.matmul(score[:, at + width - P:at + width], identb[:], future[:], start=False, stop=True,
                                     skip_group_check=True).then_inc(score_done, 1)

                def step(i, it, u, last):
                    n = head(i, it, u)
                    pe.wait_ge(exp_done, n + 1)
                    for c in range(chunks(i)):
                        bank = (u + c) % 2
                        pe.wait_ge(evac[bank], use(i, it, u))
                        for j in range(c * CHUNK, min(i + 1, (c + 1) * CHUNK)):
                            ins = nc.tensor.transpose(turned[bank][:, (j % CHUNK) * P:(j % CHUNK + 1) * P],
                                                      probs[:, slot(i, u) + j * P:slot(i, u) + (j + 1) * P], G.ident[:])
                        ins.then_inc(turn_done, 1)
                    to = scored(i, it, u, last)
                    if to:
                        scores(*to)
                    pe.wait_ge(pc_done, pair_of(i, it, u) + 1)
                    if i:
                        pe.wait_ge(x_added, i)
                    k = u % 2
                    pe.wait_ge(rden_done, n + 1)
                    nc.tensor.matmul(pv[k * KVL:(k + 1) * KVL, u // 2, 1], spread(rden[:, u:u + 1], [P, KVL]),
                                     G.ident[:], start=True, stop=True, skip_group_check=True).then_inc(laid_out, 1)
                    if u % 2:
                        for bank in range(2):
                            pe.wait_ge(evac[bank], use(i, it, u) + 1)
                        for j in range(i + 1):
                            for k in range(2):
                                ins = nc.tensor.matmul(pv[k * KVL:(k + 1) * KVL, u // 2, 0], W.c[:, b, j], probsT[:, k, j],
                                                       start=(j == 0), stop=(j == i), skip_group_check=True)
                        ins.then_inc(pv_done, 1)

                def end(i):
                    for p in range(PAIRS):
                        if p in (0, PAIRS - 1):
                            p_read = max(p, PAIRS - 2)
                            pe.wait_ge(pc_done, 2 + PAIRS * i + p_read + 1)
                        ins = nc.tensor.matmul(y, pcT[:, i % 2, p], W.m[:, p], start=(p == 0), stop=(p == PAIRS - 1))
                    ins.then_inc(y_done, 1)

                for u in range(look(0)):
                    scores(0, u, u)
                for_turns(pe, step, end)

            def empty(eng, bank, i, it, u):
                copy = nc.scalar.copy if bank == 0 else nc.vector.tensor_copy
                for c in range(chunks(i)):
                    if (u + c) % 2 == bank:
                        tiles = min(i + 1, (c + 1) * CHUNK) - c * CHUNK
                        eng.wait_ge(turn_done, turns(i, it, u, c))
                        eng.wait_ge(pv_done, pair_of(i, it, u) + 1)
                        copy(probsT[:, u % 2, c * CHUNK:c * CHUNK + tiles].rearrange("p j t -> p (j t)"),
                             turned[bank][:, 0:tiles * P]).then_inc(evac[bank], 1)

            @block.scalar
            def _(act):
                act.sem_inc(evac[0], 1)

                def softmax(i, u, n):
                    at, width = slot(i, u), (i + 1) * P
                    act.wait_ge(shift_ready, n + 1)
                    if not isinstance(n, int) or n >= U:
                        act.wait_ge(laid_out, n - U + 1)
                    nc.scalar.activation(probs[:, at:at + width], score[:, at:at + width], ACT.Exp, bias=shift[:, u:u + 1],
                                         scale=SCALE, accum_out=row_sum[:, u:u + 1]).then_inc(exp_done, 1)

                def step(i, it, u, last):
                    empty(act, 0, i, it, u)
                    for v in (u - 1, u) if u % 2 else ():
                        to = scored(i, it, v, last)
                        if to:
                            act.wait_ge(turn_done, turns(i, it, v, chunks(i) - 1))
                            softmax(*to)

                for u in range(look(0)):
                    softmax(0, u, u)
                for_turns(act, step, lambda i: None)

            @block.vector
            def _(dve):
                dve.sem_inc(pc_done, 2)
                dve.sem_inc(evac[1], 1)

                def maximum(i, u, n):
                    at = slot(i, u)
                    dve.wait_ge(score_done, n + 1)
                    nc.vector.tensor_reduce(neg_max[:, u:u + 1], score[:, at:at + (i + 1) * P], AX.X, ALU.max, negate=True)\
                        .then_inc(max_done, 1)
                    dve.wait_ge(max_done, n + 1)
                    if not isinstance(n, int) or n >= U:
                        dve.wait_ge(exp_done, n - U + 1)
                    nc.vector.tensor_scalar(shift[:, u:u + 1], neg_max[:, u:u + 1], SCALE, None, ALU.mult)\
                        .then_inc(shift_ready, 1)

                def invert(u, n):
                    dve.wait_ge(exp_done, n + 1)
                    nc.vector.reciprocal(rden[:, u:u + 1], row_sum[:, u:u + 1]).then_inc(rden_done, 1)

                def step(i, it, u, last):
                    empty(dve, 1, i, it, u)
                    to = scored(i, it, u, last)
                    if to:
                        maximum(*to)
                        invert((to[1] - 1) % U, to[2] - 1)
                    elif i + 1 == TILES and u == look(i):
                        invert(U - 1, NH * TILES - 1)
                    if u % 2:
                        dve.wait_ge(pv_done, pair_of(i, it, u) + 2)
                        dst = pcT[:, i % 2, 2 * it + u // 2] if last else \
                            pcT[:, i % 2, bass.ds(it * 2 + u // 2, 1)].rearrange("p a t -> p (a t)")
                        nc.vector.tensor_copy(rden_rows[:], pv[:, u // 2, 1]).then_inc(rows_copied, 1)
                        dve.wait_ge(rows_copied, pair_of(i, it, u) + 1)
                        nc.vector.tensor_tensor(dst, pv[:, u // 2, 0], rden_rows[:], ALU.mult).then_inc(pc_done, 1)

                def end(i):
                    nc.vector.tensor_tensor(G.x[:, b, i], G.x[:, b, i], W.row[:, b], ALU.add).then_inc(row_added, 1)
                    dve.wait_ge(row_added, i + 1)
                    dve.wait_ge(y_done, i + 1)
                    nc.vector.tensor_tensor(G.x[:, b, i], y, G.x[:, b, i], ALU.add).then_inc(x_added, 1)

                for u in range(look(0)):
                    maximum(0, u, u)
                    if u:
                        invert(u - 1, u - 1)
                for_turns(dve, step, end)


E1, R1, F1 = 8, 8, 1024
FM = F1 // P
SCALING = 16.0 / 8.0


def route(nc, dve, steps, apart, logits, top, index, index_f, hot, iota8):
    hold_apart(dve, steps.sem, now(steps.it, steps.per, steps.n), apart)
    for j in range(TPB):
        n = steps.mark(nc.vector.max(top[:, j], logits[:, j]))
    hold_apart(dve, steps.sem, now(steps.it, steps.per, n), apart)
    for j in range(TPB):
        n = steps.mark(nc.vector.max_index(index[:, j], top[:, j], logits[:, j]))
    steps.hold(n)
    steps.then(nc.vector.tensor_copy(index_f[:], index[:, :, 0:2]))
    for k in range(2):
        n = steps.mark(nc.vector.tensor_tensor(hot[:, :, k], spread(iota8[:].unsqueeze(1), [P, TPB, 8]),
                                               spread(index_f[:, :, k:k + 1], [P, TPB, 8]), ALU.is_equal))
    steps.hold(n)
ROUTE_STEPS = 2 * TPB + 3


def l1_ffn(nc, G):
    with Phase(nc, "f1w") as W:
        shapes = {"ra": ([P, KC, E1 + E1 * R1], G.dram["f1_ra"].rearrange("(k p) n -> p k n", p=P)),
                  "w1": ([P, KC, F1], G.dram["f1_w1"].rearrange("(k p) n -> p k n", p=P)),
                  "b1": ([P, FM], G.dram["f1_b1"]), "B1": ([P, F1], G.dram["f1_B1"]),
                  "A2": ([P, FM, E1 * R1], G.dram["f1_A2"].rearrange("(m p) n -> p m n", p=P)),
                  "w2": ([P, FM, D], G.dram["f1_w2"].rearrange("(m p) n -> p m n", p=P)),
                  "B2": ([P, D], G.dram["f1_B2"]),
                  "b2": ([P, D], G.dram["L1_ffn_b2"].partition_broadcast(P)),
                  "br": ([P, E1], G.dram["L1_ffn_b_r"].partition_broadcast(P)),
                  "iota8": ([P, E1], G.dram["iota8"].partition_broadcast(P))}
        w_in = W.sem("w_in")
        for name, (shape, _) in shapes.items():
            W.sb(name, shape)

        def load(sp):
            for name, (_, src) in shapes.items():
                sp.dma_start(W[name][:], src).then_inc(w_in, 16)
        norm_phase(nc, G, "f1n", load=load)
        l1_ffn_blocks(nc, G, W, w_in, 16 * len(shapes))


def l1_ffn_blocks(nc, G, W, w_in, LOADS):
    with Phase(nc, "f1b") as ph:
        xs = ph.sb("xs", [P, KC, BLK])
        logits = ph.sb("logits", [P, TPB, E1])
        top = ph.sb("top", [P, TPB, 8])
        index = ph.sb("index", [P, TPB, 8], U32)
        index_f = ph.sb("index_f", [P, TPB, 2])
        hot = ph.sb("hot", [P, TPB, 2, E1])
        slot = ph.sb("slot", [P, TPB, 2, E1])
        hot_w = ph.sb("hot_w", [P, TPB, 2, E1])
        expo = ph.sb("expo", [P, TPB, 8])
        total = ph.sb("total", [P, TPB])
        w = ph.sb("w", [P, TPB, 2])
        w_sum = ph.sb("w_sum", [P, TPB])
        z = ph.sb("z", [P, TPB, 2, E1, R1])
        wide = ph.sb("wide", [P, TPB, 2 * E1, R1])
        zT = ph.sb("zT", [P, BLK])
        wideT = ph.sb("wideT", [P, BLK])
        wb = ph.sb("wb", [P, 2, BLK])
        h = ph.sb("h", [P, 2, 2, BLK])
        h_w = ph.sb("h_w", [P, 2, 2, BLK])
        h_sum = ph.sb("h_sum", [P, FM, BLK])
        z2T = ph.sb("z2T", [P, BLK])
        HB = 3
        hid = [ph.ps(f"hid{j}", [P, BLK]) for j in range(HB)]
        first = ph.ps("first", [P, TPB, E1 + E1 * R1])
        turned = [ph.ps(f"turned{j}", [P, BLK]) for j in range(2)]
        u2 = ph.ps("u2", [P, BLK])
        y = ph.ps("y", [P, 2, D])
        xs_ready = ph.sem("xs_ready")
        first_done = ph.sem("first_done")
        top_ready = ph.sem("top_ready")
        expo_done = ph.sem("expo_done")
        z_ready = ph.sem("z_ready")
        turn_done = ph.sem("turn_done")
        turn_out = ph.sem("turn_out")
        hid_done = ph.sem("hid_done")
        h_done = ph.sem("h_done")
        u2_done = ph.sem("u2_done")
        hw_dve = ph.sem("hw_dve")
        hw_pool = ph.sem("hw_pool")
        sum_done = ph.sem("sum_done")
        z2_ready = ph.sem("z2_ready")
        y_done = ph.sem("y_done")
        x_added = ph.sem("x_added")
        dve_steps = ph.sem("dve_steps")
        apart, apart_pool = ph.sem("apart"), ph.sem("apart_pool")
        xnT = G.xnT[:].rearrange("p k b t -> p k (b t)")
        x_flat = G.x[:].rearrange("p b i d -> p (b i) d")
        ER = E1 * R1
        with ph.block() as block:
            @block.gpsimd
            def _(pool):
                pool.sem_inc(hw_pool, FM)
                with pool.Fori(0, BLOCKS) as it:
                    hold_apart(pool, u2_done, before(it, FM, FM), apart_pool)
                    nc.gpsimd.tensor_copy(xs[:], xnT[:, :, bass.ds(it * BLK, BLK)]).then_inc(xs_ready, 1)
                    pool.wait_ge(turn_out, now(it, 4, 4, credit=True))
                    for m in range(FM):
                        pool.wait_ge(h_done, now(it, 2 * FM, 2 * m + 2, credit=True))
                        if m >= 2:
                            pool.wait_ge(sum_done, now(it, FM, m - 1, credit=True))
                        nc.gpsimd.tensor_tensor(h_w[:, m % 2, 1], h[:, m % 2, 1], wb[:, 1], ALU.mult).then_inc(hw_pool, 1)

            @block.tensor
            def _(pe):
                pe.sem_inc(u2_done, FM)
                pe.sem_inc(y_done, 2)
                pe.wait_ge(w_in, LOADS)
                with pe.Fori(0, BLOCKS) as it:
                    pe.wait_ge(xs_ready, now(it, 1, 1))
                    for j in range(TPB):
                        for k in range(KC):
                            ins = nc.tensor.matmul(first[:, j], xs[:, k, j * P:(j + 1) * P], W["ra"][:, k],
                                                   start=(k == 0), stop=(k == KC - 1))
                    ins.then_inc(first_done, 1)

                    def base(m):
                        if m >= HB:
                            pe.wait_ge(h_done, now(it, 2 * FM, 2 * (m - HB) + 2, credit=True))
                        else:
                            pe.wait_ge(h_done, before(it, 2 * FM, 2 * FM))
                        for k in range(KC):
                            nc.tensor.matmul(hid[m % HB][:], W["w1"][:, k, m * P:(m + 1) * P], xs[:, k],
                                             start=(k == 0), stop=False, skip_group_check=True)

                    def rank0(m):
                        nc.tensor.matmul(hid[m % HB][:], W["B1"][0:ER, m * P:(m + 1) * P], zT[0:ER], start=False, stop=True,
                                         skip_group_check=True).then_inc(hid_done, 1)

                    def rank1(m):
                        pe.wait_ge(h_done, now(it, 2 * FM, 2 * m + 1, credit=True))
                        nc.tensor.matmul(hid[m % HB][:], W["B1"][ER:2 * ER, m * P:(m + 1) * P], zT[ER:2 * ER], start=False,
                                         stop=True, skip_group_check=True).then_inc(hid_done, 1)

                    def adapter2(m):
                        pe.wait_ge(h_done, now(it, 2 * FM, 2 * m + 2, credit=True))
                        for k in range(2):
                            ins = nc.tensor.matmul(u2[k * ER:(k + 1) * ER], W["A2"][:, m], h[:, m % 2, k],
                                                   start=(m == 0), stop=(m == FM - 1))
                        ins.then_inc(u2_done, 1)

                    base(0)
                    base(1)
                    pe.wait_ge(z_ready, now(it, 1, 1))
                    for bank in range(4):
                        if bank >= 2:
                            pe.wait_ge(turn_out, now(it, 4, bank - 1, credit=True))
                        else:
                            pe.wait_ge(turn_out, before(it, 4, 3 + bank))
                        for j in range(TPB):
                            out = turned[bank % 2][:, j * P:(j + 1) * P]
                            if bank == 0:
                                ins = nc.tensor.transpose(out, z[:, j].rearrange("p k e r -> p (k e r)"), G.ident[:])
                            elif bank == 1:
                                ins = nc.tensor.transpose(out, wide[:, j].rearrange("p k r -> p (k r)"), G.ident[:])
                            else:
                                ins = nc.tensor.matmul(out, spread(w[:, j, bank - 2:bank - 1], [P, P]), G.ident[:],
                                                       start=True, stop=True)
                        ins.then_inc(turn_done, 1)
                    pe.wait_ge(turn_out, now(it, 4, 1, credit=True))
                    rank0(0)
                    rank0(1)
                    for m in range(FM):
                        if m + 2 < FM:
                            base(m + 2)
                            rank0(m + 2)
                        rank1(m)
                        if m >= 1:
                            adapter2(m - 1)
                    adapter2(FM - 1)
                    for c in range(2):
                        pe.wait_ge(x_added, before(it, 2, 2) if c == 0 else now(it, 2, 1, credit=True))
                        pe.wait_ge(sum_done, now(it, FM, FM, credit=True))
                        pe.wait_ge(z2_ready, now(it, 1, 1))
                        for j in range(2):
                            cols = slice((2 * c + j) * P, (2 * c + j + 1) * P)
                            for m in range(FM):
                                nc.tensor.matmul(y[:, j], h_sum[:, m, cols], W["w2"][:, m], start=(m == 0), stop=False)
                            ins = nc.tensor.matmul(y[:, j], z2T[:, cols], W["B2"][:], start=False, stop=True)
                        ins.then_inc(y_done, 1)

            @block.scalar
            def _(act):
                act.sem_inc(h_done, 2 * FM)
                act.sem_inc(turn_out, 4)
                act.wait_ge(w_in, LOADS)
                with act.Fori(0, BLOCKS) as it:
                    act.wait_ge(top_ready, now(it, 1, 1))
                    nc.scalar.activation(expo[:], expo[:], ACT.Exp).then_inc(expo_done, 1)
                    for bank, dst in enumerate((zT[:], wideT[:], wb[:, 0], wb[:, 1])):
                        act.wait_ge(turn_done, now(it, 4, bank + 1))
                        if bank == 2:
                            act.wait_ge(sum_done, before(it, FM, FM))
                        nc.scalar.copy(dst, turned[bank % 2][:]).then_inc(turn_out, 1)

                    def hidden(m, k):
                        act.wait_ge(hid_done, now(it, 2 * FM, hid_order.index((m, k)) + 1))
                        if m >= 2:
                            act.wait_ge(u2_done, now(it, FM, m - 1, credit=True))
                            act.wait_ge(hw_pool, now(it, FM, m - 1, credit=True))
                            act.wait_ge(hw_dve, now(it, FM, m - 1))
                        nc.scalar.activation(h[:, m % 2, k], hid[m % HB][:], ACT.Gelu_apprx_tanh, bias=W["b1"][:, m:m + 1])\
                            .then_inc(h_done, 1)
                    hid_order = [(0, 0), (1, 0)]
                    for m in range(FM):
                        if m + 2 < FM:
                            hid_order.append((m + 2, 0))
                        hid_order.append((m, 1))
                    for m in range(FM):
                        hidden(m, 0)
                        hidden(m, 1)

            @block.vector
            def _(dve):
                dve.sem_inc(sum_done, FM)
                dve.sem_inc(x_added, 2)
                dve.wait_ge(w_in, LOADS)
                with dve.Fori(0, BLOCKS) as it:
                    steps = Steps(dve, dve_steps, it, ROUTE_STEPS + 14)
                    dve.wait_ge(first_done, now(it, 1, 1))
                    steps.mark(nc.vector.tensor_tensor(logits[:], first[:, :, 0:E1], spread(W["br"][:].unsqueeze(1), [P, TPB, E1]), ALU.add))
                    route(nc, dve, steps, apart, logits, top, index, index_f, hot, W["iota8"])
                    nc.vector.tensor_tensor(expo[:], top[:], spread(top[:, :, 0:1], [P, TPB, 8]), ALU.subtract).then_inc(top_ready, 1)
                    steps.then(nc.vector.tensor_scalar(hot[:], hot[:], SCALING, None, ALU.mult))
                    nc.vector.tensor_copy(slot[:, :, 0], hot[:, :, 0])
                    steps.then(nc.vector.tensor_tensor(slot[:, :, 1], hot[:, :, 1], hot[:, :, 0], ALU.subtract))
                    for k in range(2):
                        n = steps.mark(nc.vector.tensor_tensor(
                            z[:, :, k], first[:, :, E1:].rearrange("p j (e r) -> p j e r", r=R1),
                            spread(slot[:, :, k].unsqueeze(3), [P, TPB, E1, R1]), ALU.mult))
                    dve.wait_ge(expo_done, now(it, 1, 1))
                    steps.then(nc.vector.tensor_reduce(total[:], expo[:], AX.X, ALU.add))
                    steps.then(nc.vector.reciprocal(total[:], total[:]))
                    steps.then(nc.vector.tensor_tensor(w[:], expo[:, :, 0:2], spread(total[:].unsqueeze(2), [P, TPB, 2]), ALU.mult))
                    steps.then(nc.vector.tensor_reduce(w_sum[:], w[:], AX.X, ALU.add))
                    steps.then(nc.vector.tensor_tensor(hot_w[:], hot[:], spread(w[:].unsqueeze(3), [P, TPB, 2, E1]), ALU.mult))
                    nc.vector.tensor_copy(wide[:], spread(hot_w[:].rearrange("p j k e -> p j (k e)").unsqueeze(3), [P, TPB, 2 * E1, R1]))\
                        .then_inc(z_ready, 1)
                    for j in range(TPB):
                        x_tile = x_flat[:, bass.ds(it * TPB + j, 1), :].rearrange("p a d -> p (a d)")
                        n = steps.mark(nc.vector.scalar_tensor_tensor(x_tile, W["b2"][:], w_sum[:, j:j + 1], x_tile, ALU.mult, ALU.add))
                    steps.hold(n)
                    dve.wait_ge(turn_out, now(it, 4, 4, credit=True))
                    for m in range(FM):
                        dve.wait_ge(h_done, now(it, 2 * FM, 2 * m + 1, credit=True))
                        nc.vector.tensor_tensor(h_w[:, m % 2, 0], h[:, m % 2, 0], wb[:, 0], ALU.mult).then_inc(hw_dve, 1)
                        dve.wait_ge(hw_dve, now(it, FM, m + 1))
                        dve.wait_ge(hw_pool, now(it, FM, m + 1, credit=True))
                        if m == 0:
                            dve.wait_ge(y_done, before(it, 2, 2))
                        nc.vector.tensor_tensor(h_sum[:, m], h_w[:, m % 2, 0], h_w[:, m % 2, 1], ALU.add).then_inc(sum_done, 1)
                    dve.wait_ge(u2_done, now(it, FM, FM, credit=True))
                    nc.vector.tensor_tensor(z2T[:], u2[:], wideT[:], ALU.mult).then_inc(z2_ready, 1)
                    for c in range(2):
                        dve.wait_ge(y_done, now(it, 2, c + 1, credit=True))
                        x_tiles = x_flat[:, bass.ds(it * TPB + 2 * c, 2), :]
                        nc.vector.tensor_tensor(x_tiles, y[:], x_tiles, ALU.add).then_inc(x_added, 1)
                    steps.close()


LH, LD = 16, 16
HPC = P // LD


def linear_attn(nc, G, tag, gated):
    with Phase(nc, tag + "w") as W:
        pre = "L3_attn_" if gated else "L2_attn_"
        wide = [P, 3 * D]
        loads = {"w": ([P, KC, 3 * D], G.dram[tag + "_w"].rearrange("(k p) n -> p k n", p=P)),
                 "b": (wide, G.dram[tag + "_b"].partition_broadcast(P)),
                 "wo": ([P, KC, D], G.dram[tag + "_wo"].rearrange("(k p) n -> p k n", p=P)),
                 "bo": ([P, D], G.dram[pre + "bo"].partition_broadcast(P)),
                 "same_head": ([P, P], G.dram["same_head"]), "head_of": ([P, HPC], G.dram["head_of"])}
        if gated:
            loads["ln_g"] = ([P, D], G.dram["L3_attn_ln_g"].partition_broadcast(P))
            loads["ln_b"] = ([P, D], G.dram["L3_attn_ln_b"].partition_broadcast(P))
        for name, (shape, _) in loads.items():
            W.sb(name, shape)
        W.w_in = W.sem("w_in")
        W.loads = 16 * len(loads)
        W.k = W.sb("k_all", [P, NB, TILES, D])
        W.v = W.sb("v_all", [P, NB, TILES, KC, P + 1])
        W.u = W.sb("u_all", [P, NB, TILES, D]) if gated else None
        W.qT = W.sb("qT", [P, KC, NB, SEQ])
        W.kv = W.sb("kv", [P, NB, KC, P + HPC])

        def load(sp):
            for name, (_, src) in loads.items():
                sp.dma_start(W[name][:], src).then_inc(W.w_in, 16)
        norm_phase(nc, G, tag + "n", load=load)
        linear_project(nc, G, W, tag + "p", gated)
        linear_state(nc, G, W, tag + "s")
        linear_output(nc, G, W, tag + "o", gated)


def linear_project(nc, G, W, tag, gated):
    with Phase(nc, tag) as ph:
        xs = ph.sb("xs", [P, KC, NB, P])
        s = ph.sb("s", [P, NB, 3 * D])
        expo = ph.sb("expo", [P, NB, 2 * D])
        low = ph.sb("low", [P, NB, 2 * D])
        relu = ph.sb("relu", [P, NB, 2 * D])
        q = ph.sb("q", [P, NB, D])
        half = ph.sb("half", [P, NB, 2 * D]) if gated else None
        tanh = ph.sb("tanh", [P, NB, 2 * D]) if gated else None
        prod = [ph.ps(f"prod{b}", [P, 2 * BLK]) for b in range(NB)]
        turned = [ph.ps(f"turned{b}", [P, KC, P]) for b in range(NB)]
        QK = D if gated else 2 * D
        xs_ready = ph.sem("xs_ready")
        prod_done = ph.sem("prod_done")
        s_ready = ph.sem("s_ready")
        expo_done = ph.sem("expo_done")
        stored = ph.sem("stored")
        turn_done = ph.sem("turn_done")
        turn_out = ph.sem("turn_out")
        dve_steps = ph.sem("dve_steps")
        apart = ph.sem("apart")
        with ph.block() as block:
            @block.gpsimd
            def _(pool):
                nc.gpsimd.memset(W.v[:, :, :, :, P:P + 1], 1.0)
                with pool.Fori(0, TILES) as it:
                    for b in range(NB):
                        hold_apart(pool, prod_done, before(it, NB, b + 1), apart)
                        nc.gpsimd.tensor_copy(xs[:, :, b], G.xnT[:, :, b, bass.ds(it * P, P)]).then_inc(xs_ready, 1)

            @block.tensor
            def _(pe):
                pe.sem_inc(prod_done, NB)
                pe.sem_inc(turn_done, NB)
                pe.wait_ge(W.w_in, W.loads)

                def product(i, b):
                    pe.wait_ge(xs_ready, now(i, NB, b + 1))
                    pe.wait_ge(s_ready, before(i, NB, b + 1))
                    for lo, hi in ((0, BLK), (BLK, 3 * D)):
                        for k in range(KC):
                            ins = nc.tensor.matmul(prod[b][:, lo:hi], xs[:, k, b], W["w"][:, k, lo:hi],
                                                   start=(k == 0), stop=(k == KC - 1))
                    ins.then_inc(prod_done, 1)

                def turn(i, b):
                    pe.wait_ge(stored, now(i, NB, b + 1, credit=True))
                    pe.wait_ge(turn_out, before(i, NB, b + 1))
                    for k in range(KC):
                        ins = nc.tensor.transpose(turned[b][:, k], q[:, b, k * P:(k + 1) * P], G.ident[:])
                    ins.then_inc(turn_done, 1)

                for b in range(NB):
                    product(0, b)
                with pe.Fori(0, TILES - 1) as it:
                    for b in range(NB):
                        product(it + 1, b)
                        turn(it, b)
                for b in range(NB):
                    turn(TILES - 1, b)

            @block.scalar
            def _(act):
                act.sem_inc(turn_out, NB)

                def functions(i, b):
                    act.wait_ge(s_ready, now(i, NB, b + 1, credit=True))
                    act.wait_ge(stored, before(i, NB, b + 1))
                    if gated:
                        nc.scalar.activation(tanh[:, b], s[:, b, D:3 * D], ACT.Tanh, scale=0.5)
                        nc.scalar.activation(half[:, b], s[:, b, D:3 * D], ACT.Copy, scale=0.5)
                    nc.scalar.activation(expo[:, b, 0:QK], low[:, b, 0:QK], ACT.Exp).then_inc(expo_done, 1)

                def empty(i, b):
                    act.wait_ge(turn_done, now(i, NB, b + 1, credit=True))
                    nc.scalar.copy(W.qT[:, :, b, bass.ds(i * P, P)], turned[b][:]).then_inc(turn_out, 1)

                for b in range(NB):
                    functions(0, b)
                with act.Fori(0, TILES - 1) as it:
                    for b in range(NB):
                        empty(it, b)
                        functions(it + 1, b)
                for b in range(NB):
                    empty(TILES - 1, b)

            @block.vector
            def _(dve):
                dve.sem_inc(s_ready, NB)
                dve.sem_inc(stored, NB)
                dve.wait_ge(W.w_in, W.loads)
                with dve.Fori(0, TILES) as it:
                    steps = Steps(dve, dve_steps, it, 3 * NB)
                    for b in range(NB):
                        dve.wait_ge(prod_done, now(it, NB, b + 1, credit=True))
                        steps.then(nc.vector.tensor_tensor(s[:, b], prod[b][:, 0:3 * D], W["b"][:], ALU.add))
                        nc.vector.tensor_scalar(low[:, b, 0:QK], s[:, b, 0:QK], 0.0, None, ALU.min).then_inc(s_ready, 1)
                    for b in range(NB):
                        steps.then(nc.vector.tensor_scalar(relu[:, b, 0:QK], s[:, b, 0:QK], 0.0, -1.0 if gated else 0.0, ALU.max, ALU.add))
                        dve.wait_ge(expo_done, now(it, NB, b + 1))
                        dve.wait_ge(turn_done, before(it, NB, b + 1))
                        steps.then(nc.vector.tensor_tensor(q[:, b], expo[:, b, 0:D], relu[:, b, 0:D], ALU.add))
                        k_dst = W.k[:, b, bass.ds(it, 1)].rearrange("p a d -> p (a d)")
                        v_dst = W.v[:, b, bass.ds(it, 1), :, 0:P].rearrange("p a k d -> p (a k) d")
                        if gated:
                            nc.vector.tensor_copy(k_dst, q[:, b])
                            u_dst = W.u[:, b, bass.ds(it, 1)].rearrange("p a d -> p (a d)")
                            nc.vector.scalar_tensor_tensor(u_dst, tanh[:, b, D:2 * D], 1.0, half[:, b, D:2 * D], ALU.add, ALU.mult)
                            nc.vector.scalar_tensor_tensor(v_dst, tanh[:, b, 0:D].rearrange("p (k d) -> p k d", k=KC), 1.0,
                                                           half[:, b, 0:D].rearrange("p (k d) -> p k d", k=KC), ALU.add, ALU.mult)\
                                .then_inc(stored, 1)
                        else:
                            nc.vector.tensor_tensor(k_dst, expo[:, b, D:2 * D], relu[:, b, D:2 * D], ALU.add)
                            nc.vector.tensor_copy(v_dst, s[:, b, 2 * D:3 * D].rearrange("p (k d) -> p k d", k=KC)).then_inc(stored, 1)
                    steps.close()


def linear_state(nc, G, W, tag):
    with Phase(nc, tag) as ph:
        acc = [ph.ps(f"acc{b}", [P, KC, P + 1]) for b in range(NB)]
        acc_done = ph.sem("acc_done")
        with ph.block() as block:
            @block.tensor
            def _(pe):
                for b in range(NB):
                    for k in range(KC):
                        for i in range(TILES):
                            ins = nc.tensor.matmul(acc[b][:, k], W.k[:, b, i, k * P:(k + 1) * P], W.v[:, b, i, k],
                                                   start=(i == 0), stop=(i == TILES - 1))
                    ins.then_inc(acc_done, 1)

            @block.vector
            def _(dve):
                for b in range(NB):
                    dve.wait_ge(acc_done, b + 1)
                    nc.vector.tensor_tensor(W.kv[:, b, :, 0:P], acc[b][:, :, 0:P], spread(W["same_head"][:].unsqueeze(1), [P, KC, P]), ALU.mult)
                    nc.vector.tensor_tensor(W.kv[:, b, :, P:P + HPC], spread(acc[b][:, :, P:P + 1], [P, KC, HPC]),
                                            spread(W["head_of"][:].unsqueeze(1), [P, KC, HPC]), ALU.mult)


def linear_output(nc, G, W, tag, gated):
    with Phase(nc, tag) as ph:
        qs = ph.sb("qs", [P, KC, NB, P])
        den = ph.sb("den", [P, NB, KC, HPC])
        out = ph.sb("out", [P, NB, D])
        outT = ph.sb("outT", [P, NB, KC, P])
        stats = ph.sb("stats", [P, NB, 6])
        mv = ph.sb("mv", [P, NB, 2])
        veps = ph.sb("veps", [P, NB])
        rstd = ph.sb("rstd", [P, NB])
        prod = [ph.ps(f"prod{b}", [P, KC, P + HPC]) for b in range(NB)]
        turned = [ph.ps(f"turned{b}", [P, KC, P]) for b in range(NB)]
        y = ph.ps("y", [P, NB, D])
        qs_ready = ph.sem("qs_ready")
        prod_done = ph.sem("prod_done")
        var_ready, rstd_ready = ph.sem("var_ready"), ph.sem("rstd_ready")
        out_ready = ph.sem("out_ready")
        turn_done = ph.sem("turn_done")
        turn_out = ph.sem("turn_out")
        y_done = ph.sem("y_done")
        x_added = ph.sem("x_added")
        dve_steps = ph.sem("dve_steps")
        apart, apart_pool = ph.sem("apart"), ph.sem("apart_pool")
        N = P if gated else P + HPC
        with ph.block() as block:
            @block.gpsimd
            def _(pool):
                with pool.Fori(0, TILES) as it:
                    for b in range(NB):
                        hold_apart(pool, prod_done, before(it, NB, b + 1), apart_pool)
                        nc.gpsimd.tensor_copy(qs[:, :, b], W.qT[:, :, b, bass.ds(it * P, P)]).then_inc(qs_ready, 1)
                    if gated:
                        pool.wait_ge(var_ready, now(it, 1, 1))
                        nc.gpsimd.tensor_tensor(rstd[:], veps[:], G.minus_half[:, 0:NB], ALU.pow).then_inc(rstd_ready, 1)

            @block.tensor
            def _(pe):
                pe.sem_inc(prod_done, NB)
                pe.sem_inc(turn_done, NB)
                pe.sem_inc(y_done, 1)

                def product(i, b):
                    pe.wait_ge(qs_ready, now(i, NB, b + 1))
                    pe.wait_ge(out_ready, before(i, NB, b + 1))
                    for k in range(KC):
                        ins = nc.tensor.matmul(prod[b][:, k, 0:N], qs[:, k, b], W.kv[:, b, k, 0:N], start=True, stop=True)
                    ins.then_inc(prod_done, 1)

                def turn(i, b):
                    pe.wait_ge(out_ready, now(i, NB, b + 1, credit=True))
                    pe.wait_ge(turn_out, before(i, NB, b + 1))
                    for k in range(KC):
                        ins = nc.tensor.transpose(turned[b][:, k], out[:, b, k * P:(k + 1) * P], G.ident[:])
                    ins.then_inc(turn_done, 1)

                def output(i):
                    pe.wait_ge(x_added, before(i, 1, 1))
                    for b in range(NB):
                        pe.wait_ge(turn_out, now(i, NB, b + 1, credit=True))
                        for k in range(KC):
                            ins = nc.tensor.matmul(y[:, b], outT[:, b, k], W["wo"][:, k], start=(k == 0), stop=(k == KC - 1))
                    ins.then_inc(y_done, 1)

                for b in range(NB):
                    product(0, b)
                with pe.Fori(0, TILES - 1) as it:
                    for b in range(NB):
                        product(it + 1, b)
                        turn(it, b)
                    output(it)
                for b in range(NB):
                    turn(TILES - 1, b)
                output(TILES - 1)

            @block.scalar
            def _(act):
                act.sem_inc(turn_out, NB)
                with act.Fori(0, TILES) as it:
                    for b in range(NB):
                        act.wait_ge(turn_done, now(it, NB, b + 1, credit=True))
                        if b == 0:
                            act.wait_ge(y_done, before(it, 1, 1))
                        nc.scalar.copy(outT[:, b], turned[b][:]).then_inc(turn_out, 1)

            @block.vector
            def _(dve):
                dve.sem_inc(out_ready, NB)
                dve.sem_inc(x_added, 1)

                def x_tile(i):
                    return G.x[:, :, bass.ds(i, 1), :].rearrange("p b i d -> p b (i d)")

                def add_output(i):
                    dve.wait_ge(y_done, now(i, 1, 1, credit=True))
                    nc.vector.tensor_tensor(x_tile(i), y[:], x_tile(i), ALU.add).then_inc(x_added, 1)

                def turn(i, first):
                    steps = Steps(dve, dve_steps, i, 5 * NB + 1 if gated else 2 * NB + 1)
                    add_bias = lambda: steps.mark(nc.vector.tensor_tensor(x_tile(i), x_tile(i), spread(W["bo"][:].unsqueeze(1), [P, NB, D]), ALU.add))
                    if gated:
                        for b in range(NB):
                            dve.wait_ge(prod_done, now(i, NB, b + 1, credit=True))
                            n = steps.mark(nc.vector.bn_stats(stats[:, b], prod[b][:, :, 0:P]))
                        hold_apart(dve, dve_steps, now(i, steps.per, n), apart)
                        for b in range(NB):
                            n = steps.mark(nc.vector.bn_aggr(mv[:, b], stats[:, b]))
                        steps.hold(n)
                        nc.vector.tensor_scalar(veps[:], mv[:, :, 1], EPS, None, ALU.add).then_inc(var_ready, 1)
                        add_bias()
                        dve.wait_ge(rstd_ready, now(i, 1, 1))
                        for b in range(NB):
                            dve.wait_ge(turn_done, before(i, NB, b + 1))
                            o = out[:, b].rearrange("p (k d) -> p k d", k=KC)
                            u_src = W.u[:, b, bass.ds(i, 1)].rearrange("p a d -> p (a d)")
                            steps.then(nc.vector.tensor_scalar(o, prod[b][:, :, 0:P], mv[:, b, 0:1], rstd[:, b:b + 1], ALU.subtract, ALU.mult))
                            steps.then(nc.vector.tensor_tensor(out[:, b], out[:, b], W["ln_g"][:], ALU.mult))
                            steps.then(nc.vector.tensor_tensor(out[:, b], out[:, b], W["ln_b"][:], ALU.add))
                            nc.vector.tensor_tensor(out[:, b], out[:, b], u_src, ALU.mult).then_inc(out_ready, 1)
                            if b == 0 and not first:
                                add_output(i - 1)
                    else:
                        add_bias()
                        for b in range(NB):
                            dve.wait_ge(prod_done, now(i, NB, b + 1, credit=True))
                            steps.then(nc.vector.tensor_scalar(den[:, b], prod[b][:, :, P:P + HPC], 1e-8, None, ALU.add))
                            steps.then(nc.vector.reciprocal(den[:, b], den[:, b]))
                            dve.wait_ge(turn_done, before(i, NB, b + 1))
                            nc.vector.tensor_tensor(out[:, b].rearrange("p (k h d) -> p k h d", k=KC, h=HPC),
                                                    prod[b][:, :, 0:P].rearrange("p k (h d) -> p k h d", h=HPC),
                                                    spread(den[:, b].unsqueeze(3), [P, KC, HPC, LD]), ALU.mult).then_inc(out_ready, 1)
                        if not first:
                            add_output(i - 1)
                    steps.close()

                turn(0, True)
                with dve.Fori(1, TILES) as it:
                    turn(it, False)
                add_output(TILES - 1)


def l2_attn(nc, G):
    linear_attn(nc, G, "l2", False)


def l3_attn(nc, G):
    linear_attn(nc, G, "l3", True)


E2, SH = 8, 256
HC = E2 + SH // P


def l2_ffn(nc, G):
    with Phase(nc, "f2w") as W:
        loads = {"gate": ([P, KC, E2], G.dram["L2_ffn_gate_w"].rearrange("(k p) n -> p k n", p=P)),
                 "w1": ([P, KC, HC * P], G.dram["f2_w1"].rearrange("(k p) n -> p k n", p=P)),
                 "b1": ([P, HC], G.dram["f2_b1"]),
                 "w2": ([P, HC, D], G.dram["f2_w2"].rearrange("(c p) n -> p c n", p=P)),
                 "b2": ([E2, D], G.dram["L2_ffn_b2"]),
                 "sb2": ([P, D], G.dram["L2_ffn_shared_b2"].partition_broadcast(P)),
                 "iota8": ([P, E2], G.dram["iota8"].partition_broadcast(P))}
        for name, (shape, _) in loads.items():
            W.sb(name, shape)
        w_in = W.sem("w_in")

        def load(sp):
            for name, (_, src) in loads.items():
                sp.dma_start(W[name][:], src).then_inc(w_in, 16)
        norm_phase(nc, G, "f2n", load=load)
        l2_ffn_blocks(nc, G, W, w_in, 16 * len(loads))


def l2_ffn_blocks(nc, G, W, w_in, LOADS):
    with Phase(nc, "f2b") as ph:
        xs = ph.sb("xs", [P, KC, BLK])
        logits = ph.sb("logits", [P, TPB, E2])
        top = ph.sb("top", [P, TPB, 8])
        index = ph.sb("index", [P, TPB, 8], U32)
        index_f = ph.sb("index_f", [P, TPB, 2])
        hot = ph.sb("hot", [P, TPB, 2, E2])
        expo = ph.sb("expo", [P, TPB])
        g = ph.sb("g", [P, TPB, 2])
        hot_g = ph.sb("hot_g", [P, TPB, 2, E2])
        gates = ph.sb("gates", [P, TPB, E2])
        gatesT = ph.sb("gatesT", [E2, TPB, P])
        h = ph.sb("h", [P, HC, BLK])
        OB = 3
        first = ph.ps("first", [P, TPB, E2])
        turned = ph.ps("turned", [E2, TPB, P])
        hid = [ph.ps(f"hid{j}", [P, BLK]) for j in range(2)]
        shared = ph.ps("shared", [P, D])
        out = [ph.ps(f"out{j}", [P, 2, D]) for j in range(OB)]
        xs_ready = ph.sem("xs_ready")
        first_done = ph.sem("first_done")
        gap_ready = ph.sem("gap_ready")
        expo_done = ph.sem("expo_done")
        gates_ready = ph.sem("gates_ready")
        turn_done = ph.sem("turn_done")
        turn_out = ph.sem("turn_out")
        hid_done = ph.sem("hid_done")
        h_done = ph.sem("h_done")
        shared_done = ph.sem("shared_done")
        out_done = ph.sem("out_done")
        shared_read = ph.sem("shared_read")
        out_read = ph.sem("out_read")
        dve_steps = ph.sem("dve_steps")
        apart, apart_pool = ph.sem("apart"), ph.sem("apart_pool")
        OUTS = TPB * E2 // 2
        xnT = G.xnT[:].rearrange("p k b t -> p k (b t)")
        x_flat = G.x[:].rearrange("p b i d -> p (b i) d")
        with ph.block() as block:
            @block.gpsimd
            def _(pool):
                with pool.Fori(0, BLOCKS) as it:
                    hold_apart(pool, hid_done, before(it, HC, HC), apart_pool)
                    nc.gpsimd.tensor_copy(xs[:], xnT[:, :, bass.ds(it * BLK, BLK)]).then_inc(xs_ready, 1)

            @block.tensor
            def _(pe):
                pe.sem_inc(hid_done, HC)
                pe.sem_inc(out_done, OUTS)
                pe.wait_ge(w_in, LOADS)
                with pe.Fori(0, BLOCKS) as it:
                    pe.wait_ge(xs_ready, now(it, 1, 1))
                    for j in range(TPB):
                        for k in range(KC):
                            ins = nc.tensor.matmul(first[:, j], xs[:, k, j * P:(j + 1) * P], W["gate"][:, k],
                                                   start=(k == 0), stop=(k == KC - 1))
                    ins.then_inc(first_done, 1)
                    for c in range(HC):
                        pe.wait_ge(h_done, now(it, HC, c - 1, credit=True) if c >= 2 else before(it, HC, HC - 1 + c))
                        for k in range(KC):
                            ins = nc.tensor.matmul(hid[c % 2][:], W["w1"][:, k, c * P:(c + 1) * P], xs[:, k],
                                                   start=(k == 0), stop=(k == KC - 1))
                        ins.then_inc(hid_done, 1)
                    pe.wait_ge(gates_ready, now(it, 1, 1))
                    for j in range(TPB):
                        ins = nc.tensor.transpose(turned[:, j], gates[:, j], G.ident[:])
                    ins.then_inc(turn_done, 1)
                    pe.wait_ge(turn_out, now(it, 1, 1))
                    pe.wait_ge(h_done, now(it, HC, HC, credit=True))
                    for j in range(TPB):
                        cols = slice(j * P, (j + 1) * P)
                        pe.wait_ge(shared_read, it * TPB + j + 1)
                        nc.tensor.matmul(shared[:], gatesT[:, j], W["b2"][:], start=True, stop=False)
                        for c in range(E2, HC):
                            ins = nc.tensor.matmul(shared[:], h[:, c, cols], W["w2"][:, c], start=False, stop=(c == HC - 1))
                        ins.then_inc(shared_done, 1)
                        for e in range(0, E2, 2):
                            n = j * (E2 // 2) + e // 2
                            pe.wait_ge(out_read, now(it, OUTS, n - OB + 1, credit=True))
                            for d in range(2):
                                ins = nc.tensor.matmul(out[n % OB][:, d], h[:, e + d, cols], W["w2"][:, e + d], start=True, stop=True)
                            ins.then_inc(out_done, 1)

            @block.scalar
            def _(act):
                act.sem_inc(h_done, HC)
                act.wait_ge(w_in, LOADS)
                with act.Fori(0, BLOCKS) as it:
                    act.wait_ge(gap_ready, now(it, 1, 1))
                    nc.scalar.activation(expo[:], expo[:], ACT.Exp).then_inc(expo_done, 1)
                    act.wait_ge(out_done, before(it, OUTS, OUTS))
                    for c in range(HC):
                        act.wait_ge(hid_done, now(it, HC, c + 1, credit=True))
                        nc.scalar.activation(h[:, c], hid[c % 2][:], ACT.Gelu, bias=W["b1"][:, c:c + 1]).then_inc(h_done, 1)
                    act.wait_ge(turn_done, now(it, 1, 1))
                    nc.scalar.copy(gatesT[:], turned[:]).then_inc(turn_out, 1)

            @block.vector
            def _(dve):
                dve.sem_inc(shared_read, 1)
                dve.sem_inc(out_read, OUTS)
                dve.wait_ge(w_in, LOADS)
                with dve.Fori(0, BLOCKS) as it:
                    steps = Steps(dve, dve_steps, it, ROUTE_STEPS + 5 + TPB * (1 + E2))
                    dve.wait_ge(first_done, now(it, 1, 1))
                    steps.mark(nc.vector.tensor_copy(logits[:], first[:]))
                    route(nc, dve, steps, apart, logits, top, index, index_f, hot, W["iota8"])
                    nc.vector.tensor_tensor(expo[:], top[:, :, 1], top[:, :, 0], ALU.subtract).then_inc(gap_ready, 1)
                    dve.wait_ge(expo_done, now(it, 1, 1))
                    steps.then(nc.vector.tensor_scalar(g[:, :, 0], expo[:], 1.0, None, ALU.add))
                    steps.then(nc.vector.reciprocal(g[:, :, 0], g[:, :, 0]))
                    steps.then(nc.vector.tensor_tensor(g[:, :, 1], expo[:], g[:, :, 0], ALU.mult))
                    steps.then(nc.vector.tensor_tensor(hot_g[:], hot[:], spread(g[:].unsqueeze(3), [P, TPB, 2, E2]), ALU.mult))
                    nc.vector.tensor_tensor(gates[:], hot_g[:, :, 0], hot_g[:, :, 1], ALU.add).then_inc(gates_ready, 1)
                    dve.wait_ge(gates_ready, now(it, 1, 1))
                    for j in range(TPB):
                        x_tile = x_flat[:, bass.ds(it * TPB + j, 1), :].rearrange("p a d -> p (a d)")
                        steps.then(nc.vector.tensor_tensor(x_tile, x_tile, W["sb2"][:], ALU.add))
                        dve.wait_ge(shared_done, now(it, TPB, j + 1))
                        nc.vector.tensor_tensor(x_tile, shared[:], x_tile, ALU.add).then_inc(shared_read, 1)
                        dve.wait_ge(shared_read, it * TPB + j + 2)
                        for e in range(E2):
                            n = j * (E2 // 2) + e // 2
                            dve.wait_ge(out_done, now(it, OUTS, n + 1, credit=True))
                            ins = nc.vector.scalar_tensor_tensor(x_tile, out[n % OB][:, e % 2], gates[:, j, e:e + 1], x_tile, ALU.mult, ALU.add)
                            steps.then(ins)
                            if e % 2:
                                dve.sem_inc(out_read, 1)
                    steps.close()



def l3_ffn(nc, G):
    with Phase(nc, "f3w") as W:
        w = W.sb("w", [P, KC, D])
        variation = W.sb("variation", [P, KC, D])
        low = W.sb("low", [P, KC, D])
        wT = W.sb("wT", [P, KC, D])
        w_in, steps_sem = W.sem("w_in"), W.sem("steps")
        TH_X, SC_X, TH_W, SC_W = 0.33, 0.5, 0.2, 0.6

        def load(sp):
            sp.dma_start(w[:], G.dram["f3_w"].rearrange("(k p) n -> p k n", p=P)).then_inc(w_in, 16)
            sp.dma_start(variation[:], G.dram["f3_v"].rearrange("(k p) n -> p k n", p=P)).then_inc(w_in, 16)
        norm_phase(nc, G, "f3n", load=load, ternary=(TH_X, SC_X))
        with nc.Block() as block:
            @block.vector
            def _(dve):
                steps = Steps(dve, steps_sem)
                dve.wait_ge(w_in, 2 * 16)
                nc.vector.tensor_scalar(low[:], w[:], -TH_W, SC_W, ALU.is_lt, ALU.mult)
                steps.then(nc.vector.tensor_scalar(wT[:], w[:], TH_W, SC_W, ALU.is_gt, ALU.mult))
                steps.then(nc.vector.tensor_tensor(wT[:], wT[:], low[:], ALU.subtract))
                nc.vector.tensor_tensor(wT[:], wT[:], variation[:], ALU.add)
        staged_linear(nc, G, "f3l", wT, None)


BRANCHES = [l0_attn, l0_ffn, l1_attn, l1_ffn, l2_attn, l2_ffn, l3_attn, l3_ffn]


SEMS_OF_A_BRANCH = 80


def program(nc, dram, out):
    RETIRED.clear()
    with Phase(nc, "g") as G:
        G.dram = dram
        G.x = G.sb("x", [P, NB, TILES, D])
        G.xnT = G.sb("xnT", [P, KC, NB, SEQ])
        G.ident = G.sb("ident", [P, P])
        G.minus_half = G.sb("minus_half", [P, TPB])
        x_in, const = G.sem("x_in"), G.sem("const")
        stored = G.sem("stored")
        with nc.Block() as block:
            @block.sync
            def _(sp):
                for b in range(NB):
                    sp.dma_start(G.x[:, b], dram["L0_attn_x"][b].rearrange("(i p) d -> p i d", p=P)).then_inc(x_in, 16)
                sp.wait_ge(x_in, 16 * NB)

            @block.gpsimd
            def _(pool):
                nc.gpsimd.memset(G.minus_half[:], -0.5)
                nc.gpsimd.memset(G.ident[:], 0.0).then_inc(const, 1)
                pool.wait_ge(const, 1)
                nc.gpsimd.affine_select(out=G.ident[:], in_=G.ident[:], compare_op=ALU.not_equal, fill=1.0,
                                        base=0, pattern=[[-1, P]], channel_multiplier=1)
        for n in LAYERS:
            BRANCHES[n](nc, G)
            if nc.free_len() < SEMS_OF_A_BRANCH:
                recycle_semaphores(nc)
        with nc.Block() as block:
            @block.sync
            def _(sp):
                for b in range(NB):
                    sp.dma_start(out[b].rearrange("(i p) d -> p i d", p=P), G.x[:, b]).then_inc(stored, 16)
                sp.wait_ge(stored, 16 * NB)


def rope_tables():
    fraction = np.arange(0, HD, 2, dtype=np.float32) / np.float32(HD)
    inv = (np.float32(1.0) / np.power(np.float32(10000.0), fraction)).astype(np.float32)
    angle = np.outer(np.arange(SEQ, dtype=np.float32), inv).astype(np.float32)
    cos, sin = np.cos(angle).T, np.sin(angle).T
    return np.concatenate([cos, cos]), np.concatenate([sin, -sin])


def l1_layouts(i):
    places = np.concatenate([np.arange(0, DR, 2), np.arange(1, DR, 2)])
    swapped = np.concatenate([np.arange(1, DR, 2), np.arange(0, DR, 2)])
    by_head = lambda w, d: w.reshape(w.shape[0], NH, d).transpose(2, 1, 0)
    qr = i["L1_attn_W_qr"].reshape(QL, PAIRS, 2, DR)
    kr = i["L1_attn_W_kr"]
    inv = 1.0 / 10000.0 ** (np.arange(0, DR, 2)[:DR // 2].astype(np.float32) / DR)
    angle = np.outer(np.arange(SEQ, dtype=np.float32), inv)
    cos, sin = np.cos(angle).T.astype(np.float32), np.sin(angle).T.astype(np.float32)
    rows = np.arange(P)
    order = rows // TOPK
    return {
        "l1_qcT": by_head(i["L1_attn_W_qc"], DK), "l1_kcT": by_head(i["L1_attn_W_kc"], DK),
        "l1_vT": by_head(i["L1_attn_W_v"], DV), "L1_attn_W_o": i["L1_attn_W_o"],
        "l1_qr": qr[..., places].reshape(QL, PAIRS, P),
        "l1_k": np.concatenate([kr[:, places], i["L1_attn_W_c"], kr[:, swapped]], axis=1),
        **{n: i[n] for n in ("L1_attn_W_cp", "L1_attn_W_gate", "L1_attn_W_idx", "L1_attn_W_sq",
                             "L1_attn_W_sk", "L1_attn_W_sv", "L1_attn_W_iout")},
        "l1_cos": np.concatenate([cos] * 4), "l1_sin": np.concatenate([-sin, sin] * 2),
        "l1_iota": (rows[:, None] + P * np.arange(TILES)).astype(np.float32),
        "l1_same": np.where(order[:, None] == order, 0.0, BIG).astype(np.float32),
        "l1_mean": ((order[:, None] == np.arange(NB * IH)) / TOPK).astype(np.float32),
    }


def ffn_layouts(i):
    B1 = i["L1_ffn_B1"].transpose(0, 2, 1).reshape(E1 * R1, F1)
    B2 = i["L1_ffn_B2"].transpose(0, 2, 1).reshape(E1 * R1, D)
    return {
        "f1_ra": np.concatenate([i["L1_ffn_W_r"].T, i["L1_ffn_A1"].reshape(E1 * R1, D).T], axis=1),
        "f1_w1": i["L1_ffn_W1"].T, "f1_b1": i["L1_ffn_b1"].reshape(FM, P).T, "f1_B1": np.concatenate([B1, B1]),
        "f1_A2": i["L1_ffn_A2"].reshape(E1 * R1, F1).T, "f1_w2": i["L1_ffn_W2"].T, "f1_B2": np.concatenate([B2, B2]),
        "L1_ffn_b2": i["L1_ffn_b2"], "L1_ffn_b_r": i["L1_ffn_b_r"],
        "iota8": np.arange(8, dtype=np.float32),
        "L2_ffn_gate_w": i["L2_ffn_gate_w"], "L2_ffn_b2": i["L2_ffn_b2"], "L2_ffn_shared_b2": i["L2_ffn_shared_b2"],
        "f2_w1": np.concatenate([i["L2_ffn_w1"].transpose(1, 0, 2).reshape(D, E2 * P), i["L2_ffn_shared_w1"]], axis=1),
        "f2_b1": np.concatenate([i["L2_ffn_b1"], i["L2_ffn_shared_b1"].reshape(SH // P, P)]).T,
        "f2_w2": np.concatenate([i["L2_ffn_w2"].reshape(E2 * P, D), i["L2_ffn_shared_w2"]]),
        "f3_w": i["L3_ffn_weight"].T, "f3_v": i["L3_ffn_rram_variation"].T,
    }


def linear_layouts(i):
    two, three = (lambda n: i["L2_attn_" + n]), (lambda n: i["L3_attn_" + n])
    head = np.arange(P) // LD
    return {
        "l2_w": np.concatenate([two(n).T for n in ("wq", "wk", "wv")], axis=1),
        "l2_b": np.concatenate([two(n) for n in ("bq", "bk", "bv")]),
        "l2_wo": two("wo").T, "L2_attn_bo": two("bo"),
        "l3_w": np.concatenate([three(n) for n in ("Wqk", "Wv", "Wu")], axis=1),
        "l3_b": np.concatenate([three(n) for n in ("bqk", "bv", "bu")]),
        "l3_wo": three("Wo"), "L3_attn_bo": three("bo"), "L3_attn_ln_g": three("ln_g"), "L3_attn_ln_b": three("ln_b"),
        "same_head": (head[:, None] == head).astype(np.float32),
        "head_of": (head[:, None] == np.arange(HPC)).astype(np.float32),
    }


def layouts(i):
    cos, sin = rope_tables()
    return {
        "L0_attn_x": i["L0_attn_x"],
        "L0_attn_q_kernel": i["L0_attn_q_kernel"], "L0_attn_k_kernel": i["L0_attn_k_kernel"],
        "L0_attn_v_kernel": i["L0_attn_v_kernel"], "L0_attn_out_kernel": i["L0_attn_out_kernel"],
        "l0_cos": cos, "l0_sin": sin,
        "L0_ffn_weight": i["L0_ffn_weight"], "L0_ffn_bias": i["L0_ffn_bias"],
        **l1_layouts(i), **ffn_layouts(i), **linear_layouts(i),
    }


def kernel(**inputs):
    import numpy as _np
    import concourse.bacc as _bacc
    from concourse import mybir as _mybir
    from concourse.bass_utils import run_bass_kernel_spmd as _run

    nc = _bacc.Bacc("TRN2", target_bir_lowering=False, num_devices=1)
    arrays, dram = {}, {}
    for name, a in layouts({k: _np.asarray(v) for k, v in inputs.items()}).items():
        arrays[f"in_{name}"] = a = _np.ascontiguousarray(a)
        dram[name] = nc.dram_tensor(f"in_{name}", a.shape, _mybir.dt.from_np(a.dtype), kind="ExternalInput").ap()
    out = nc.dram_tensor("out_0_dram", (NB, SEQ, D), F32, kind="ExternalOutput").ap()
    program(nc, dram, out)
    r = _run(nc, [arrays], core_ids=[0])
    return r.results[0]["out_0_dram"]
```

```python
from contextlib import ExitStack

import numpy as np

import concourse.bass as bass
from concourse import mybir

F32 = mybir.dt.float32
BF16 = mybir.dt.bfloat16
U32 = mybir.dt.uint32
ACT = mybir.ActivationFunctionType
ALU = mybir.AluOpType
AX = mybir.AxisListType

P = 128
NB, SEQ, D = 2, 1024, 256
TILES = SEQ // P
KC = D // P
BLK = 512
TPB = BLK // P
BLOCKS = NB * SEQ // BLK
BPB = SEQ // BLK
EPS = 1e-5

LAYERS = range(8)


def before(it, per, n):
    assert n >= 1
    return it * per + n


def now(it, per, n, credit=False):
    assert n + (per if credit else 0) >= 1
    return it * per + n + (per if credit else 0)


class Steps:

    def __init__(self, eng, sem, it=0, per=0):
        self.eng, self.sem, self.it, self.per, self.n = eng, sem, it, per, 0

    def mark(self, ins):
        self.n += 1
        ins.then_inc(self.sem, 1)
        return self.n

    def hold(self, n):
        self.eng.wait_ge(self.sem, now(self.it, self.per, n))

    def then(self, ins):
        self.hold(self.mark(ins))

    def close(self):
        assert self.per in (0, self.n), (self.per, self.n)


def hold_apart(eng, sem, value, apart):
    eng.wait_ge(sem, value)
    eng.sem_inc(apart, 1)


def spread(ap, shape):
    return ap.to_broadcast(shape)


RETIRED = []


def recycle_semaphores(nc):
    nc.clear_and_free_semaphores(RETIRED)
    RETIRED.clear()
    nc.all_engine_barrier()


class Phase:

    def __init__(self, nc, tag):
        self.nc, self.tag, self.stack, self.sems, self.named = nc, tag, ExitStack(), [], {}

    def __enter__(self):
        self.stack.__enter__()
        return self

    def __exit__(self, *what):
        RETIRED.extend(self.sems)
        return self.stack.__exit__(*what)

    def sb(self, name, shape, dt=F32):
        self.named[name] = self.stack.enter_context(self.nc.sbuf_tensor(f"{self.tag}_{name}", shape, dt))
        return self.named[name]

    def __getitem__(self, name):
        return self.named[name]

    def ps(self, name, shape, dt=F32):
        return self.stack.enter_context(self.nc.psum_tensor(f"{self.tag}_{name}", shape, dt))

    def sem(self, name):
        self.sems.append(self.nc.alloc_semaphore(f"{self.tag}_{name}"))
        return self.sems[-1]

    def block(self):
        return self.nc.Block()


def norm_phase(nc, G, tag, load=None, keep=None, ternary=None):
    with Phase(nc, tag) as ph:
        stats = ph.sb("stats", [P, 2, TPB, 6])
        mv = ph.sb("mv", [P, BLOCKS * TPB, 2])
        veps = ph.sb("veps", [P, BLOCKS * TPB])
        neg_mean = ph.sb("neg_mean", [P, BLOCKS * TPB])
        rstd = ph.sb("rstd", [P, BLOCKS * TPB])
        shift = ph.sb("shift", [P, BLOCKS * TPB])
        xn = None if keep is not None else ph.sb("xn", [P, 2, TPB, D])
        low = ph.sb("low", [P, TPB, D]) if ternary else None
        turned = [ph.ps(f"turned{j}", [P, KC, BLK]) for j in range(2)]
        agg_done = ph.sem("agg_done")
        var_ready = ph.sem("var_ready")
        rstd_ready = ph.sem("rstd_ready")
        xn_ready = ph.sem("xn_ready")
        last_ready = ph.sem("last_ready")
        tern_ready = ph.sem("tern_ready")
        turn_done = ph.sem("turn_done")
        out_act = ph.sem("out_act")
        out_dve = ph.sem("out_dve")
        dve_steps = ph.sem("dve_steps")
        x_flat = G.x[:].rearrange("p b i d -> p (b i) d")
        xnT_flat = G.xnT[:].rearrange("p k b t -> p k (b t)")
        keep_flat = keep[:].rearrange("p b i d -> p (b i) d") if keep is not None else None
        threshold, scale = ternary if ternary else (0.0, 1.0)
        from_dve = KC // 2

        first, G.loading = G.loading, False

        def rows(n):
            return slice(n * TPB, (n + 1) * TPB)

        def normal(n, j):
            return keep_flat[:, n * TPB + j] if keep is not None else xn[:, n % 2, j]

        with ph.block() as block:
            if load:
                @block.sync
                def _(sp):
                    load(sp)

            @block.gpsimd
            def _(pool):
                for n in range(BLOCKS):
                    pool.wait_ge(var_ready, 2 * n + 2)
                    nc.gpsimd.tensor_tensor(rstd[:, rows(n)], veps[:, rows(n)], G.minus_half[:], ALU.pow)\
                        .then_inc(rstd_ready, 1)
                    pool.wait_ge(rstd_ready, 2 * n + 1)
                    nc.gpsimd.tensor_tensor(shift[:, rows(n)], neg_mean[:, rows(n)], rstd[:, rows(n)], ALU.mult)\
                        .then_inc(rstd_ready, 1)

            @block.vector
            def _(dve):
                steps = Steps(dve, dve_steps)

                def empty(n):
                    dve.wait_ge(turn_done, n + 1)
                    for k in range(from_dve, KC):
                        ins = nc.vector.tensor_scalar(xnT_flat[:, k, n * BLK:(n + 1) * BLK], turned[n % 2][:, k], scale, None, ALU.mult)
                    ins.then_inc(out_dve, 1)

                def normalise(n):
                    at = n * TPB + TPB - 1
                    dve.wait_ge(rstd_ready, 2 * n + 1)
                    if n >= 2:
                        dve.wait_ge(turn_done, n - 1)
                    nc.vector.tensor_scalar(normal(n, TPB - 1), x_flat[:, at], mv[:, at, 0:1], rstd[:, at:at + 1],
                                            ALU.subtract, ALU.mult).then_inc(last_ready, 1)

                for n in range(BLOCKS):
                    if first:
                        dve.wait_ge(G.x_in[n], 16)
                    for j in range(TPB):
                        s = steps.mark(nc.vector.bn_stats(stats[:, n % 2, j], x_flat[:, n * TPB + j]))
                    steps.hold(s)
                    for j in range(TPB):
                        nc.vector.bn_aggr(mv[:, n * TPB + j], stats[:, n % 2, j]).then_inc(agg_done, 1)
                    dve.wait_ge(agg_done, (n + 1) * TPB)
                    nc.vector.tensor_scalar(veps[:, rows(n)], mv[:, rows(n), 1], EPS, None, ALU.add).then_inc(var_ready, 1)
                    nc.vector.tensor_scalar(neg_mean[:, rows(n)], mv[:, rows(n), 0], -1.0, None, ALU.mult).then_inc(var_ready, 1)
                    if n in (1, 2) and not ternary:
                        normalise(n - 1)

                def quantise(n):
                    part = xn[:, n % 2]
                    dve.wait_ge(xn_ready, n + 1)
                    if n:
                        dve.wait_ge(tern_ready, n)
                    steps.then(nc.vector.tensor_scalar(low[:], part, -threshold, None, ALU.is_lt))
                    nc.vector.scalar_tensor_tensor(part, part, threshold, low[:], ALU.is_gt, ALU.subtract).then_inc(tern_ready, 1)

                if ternary:
                    quantise(0)
                for n in range(BLOCKS):
                    if ternary and n + 1 < BLOCKS:
                        quantise(n + 1)
                    empty(n)
                    if not ternary and n + 2 < BLOCKS:
                        normalise(n + 2)

            @block.tensor
            def _(pe):
                for n in range(BLOCKS):
                    pe.wait_ge(tern_ready if ternary else xn_ready, n + 1)
                    if not ternary:
                        pe.wait_ge(last_ready, n + 1)
                    if n >= 2:
                        pe.wait_ge(out_act, n - 1)
                        pe.wait_ge(out_dve, n - 1)
                    for k in range(KC):
                        for j in range(TPB):
                            ins = nc.tensor.transpose(turned[n % 2][:, k, j * P:(j + 1) * P],
                                                      normal(n, j)[:, k * P:(k + 1) * P], G.ident[:])
                    ins.then_inc(turn_done, 1)

            @block.scalar
            def _(act):
                def empty(n):
                    act.wait_ge(turn_done, n + 1)
                    for k in range(from_dve):
                        ins = nc.scalar.activation(xnT_flat[:, k, n * BLK:(n + 1) * BLK], turned[n % 2][:, k], ACT.Copy, scale=scale)
                    ins.then_inc(out_act, 1)

                for n in range(BLOCKS):
                    act.wait_ge(rstd_ready, 2 * n + 2)
                    if n >= 2:
                        act.wait_ge(turn_done, n - 1)
                    for j in range(TPB if ternary else TPB - 1):
                        at = slice(n * TPB + j, n * TPB + j + 1)
                        ins = nc.scalar.activation(normal(n, j), x_flat[:, n * TPB + j], ACT.Identity,
                                                   bias=shift[:, at], scale=rstd[:, at])
                    ins.then_inc(xn_ready, 1)
                    if n:
                        empty(n - 1)
                empty(BLOCKS - 1)


NH, NKV, HD = 16, 4, 128
GROUP = NH // NKV
CAP = 50.0


def load_l0_attn(nc, G, W, sem):
    def load(sp):
        I = G.dram
        for dst, src in ((W.q[:], I["L0_attn_q_kernel"].rearrange("(k p) n -> p k n", p=P)),
                         (W.k[:], I["L0_attn_k_kernel"].rearrange("(k p) n -> p k n", p=P)),
                         (W.v[:], I["L0_attn_v_kernel"].rearrange("(k p) n -> p k n", p=P)),
                         (W.o[:], I["L0_attn_out_kernel"].rearrange("(h p) n -> p h n", p=P)),
                         (W.cos[:], I["l0_cos"]), (W.sin[:], I["l0_sin"])):
            sp.dma_start(dst, src).then_inc(sem, 16)
    return load


def l0_attn(nc, G):
    with Phase(nc, "l0w") as W:
        W.q = W.sb("q", [P, KC, NH * HD])
        W.k = W.sb("k", [P, KC, NKV * HD])
        W.v = W.sb("v", [P, KC, NKV * HD])
        W.o = W.sb("o", [P, NH, D])
        W.cos = W.sb("cos", [P, SEQ])
        W.sin = W.sb("sin", [P, SEQ])
        w_in = W.sem("w_in")
        LOADS = 6 * 16
        norm_phase(nc, G, "l0n", load=load_l0_attn(nc, G, W, w_in))
        l0_attn_tiles(nc, G, W, w_in, LOADS)


def l0_attn_tiles(nc, G, W, w_in, LOADS):
    with Phase(nc, "l0a") as ph:
        xs = ph.sb("xs", [P, KC, NB, P])
        qT = ph.sb("qT", [P, NH, NB, P])
        kT = ph.sb("kT", [P, 2, NKV, NB, P])
        v = ph.sb("v", [P, 2, NB, NKV, HD + 1])
        rope_a = ph.sb("rope_a", [P, 2, BLK])
        rope_b = ph.sb("rope_b", [P, 2, BLK])
        capped = ph.sb("capped", [P, 2, BLK])
        probs = ph.sb("probs", [P, 2, 2, BLK])
        rden = ph.sb("rden", [P, GROUP])
        enc = ph.sb("enc", [P, 2, GROUP, HD])
        encT = ph.sb("encT", [P, NB, NH, P])
        proj = ph.ps("proj", [P, 2, BLK])
        score = ph.ps("score", [P, 2, BLK])
        pv = ph.ps("pv", [P, 2, BLK])
        turned = ph.ps("turned", [P, BLK])
        y = ph.ps("y", [P, NB, D])

        UNITS = NKV * NB
        KB, QB = NKV // 2, NH // 2
        ROPES = KB + QB
        SCALE = float(HD) ** -0.5 / CAP

        xs_ready = ph.sem("xs_ready")
        proj_done = ph.sem("proj_done")
        roped = ph.sem("roped")
        rotated = ph.sem("rotated")
        v_ready = ph.sem("v_ready")
        score_done = ph.sem("score_done")
        tanh_done = ph.sem("tanh_done")
        exp_done = ph.sem("exp_done")
        masked = ph.sem("masked")
        pv_done = ph.sem("pv_done")
        enc_done = ph.sem("enc_done")
        turn_done = ph.sem("turn_done")
        encT_done = ph.sem("encT_done")
        y_done = ph.sem("y_done")
        x_added = ph.sem("x_added")
        dve_steps = ph.sem("dve_steps")
        apart = ph.sem("apart")
        cleared = ph.sem("cleared")
        BANKS = KB + NB + QB
        n_rope = {**{("k", j): j + 1 for j in range(KB)}, **{("q", j): KB + j + 1 for j in range(QB)}}

        def q_banks(u):
            g = u // NB + 1
            return (2 * g, 2 * g + 1) if u % NB == 0 and g < NKV else ()

        def turns(eng, begin, body):
            begin(0, 0)
            with eng.Fori(0, TILES // 2 - 1) as it:
                for par in range(2):
                    body(it * 2 + par, par, it * 2 + par + 1)
            body(TILES - 2, 0, TILES - 1)
            body(TILES - 1, 1, None)

        with ph.block() as block:
            @block.gpsimd
            def _(pool):
                nc.gpsimd.memset(kT[:], 0.0).then_inc(cleared, 1)
                nc.gpsimd.memset(v[:], 0.0).then_inc(cleared, 1)

                def stage(t):
                    hold_apart(pool, proj_done, before(t, BANKS, BANKS), apart)
                    nc.gpsimd.tensor_copy(xs[:], G.xnT[:, :, :, bass.ds(t * P, P)]).then_inc(xs_ready, 1)

                def begin(t, par):
                    hold_apart(pool, pv_done, before(t, UNITS, UNITS), apart)
                    nc.gpsimd.memset(v[:, par, :, :, HD:HD + 1], 1.0)

                def mask(t, u):
                    for c in range(2):
                        hold_apart(pool, exp_done, now(t, 2 * UNITS, 2 * u + c + 1), apart)
                        part = probs[:, u % 2, c].rearrange("p (h t) -> p h t", h=GROUP)
                        sign = 1 if c == 0 else -1
                        nc.gpsimd.affine_select(out=part, in_=part, compare_op=ALU.is_ge, fill=0.0,
                                                base=0, pattern=[[0, GROUP], [sign, P]],
                                                channel_multiplier=-sign).then_inc(masked, 1)

                def body(t, par, nxt):
                    for u in range(UNITS):
                        mask(t, u)
                        if u == UNITS - 3 and nxt is not None:
                            stage(nxt)
                    if nxt is not None:
                        begin(nxt, 1 - par)

                pool.wait_ge(cleared, 2)
                stage(0)
                turns(pool, begin, body)

            @block.tensor
            def _(pe):
                pe.sem_inc(proj_done, BANKS)
                pe.sem_inc(pv_done, UNITS)
                pe.sem_inc(turn_done, UNITS)
                pe.sem_inc(y_done, 1)
                pe.wait_ge(w_in, LOADS)

                def free_bank(t, n):
                    n -= 2
                    back = n < 0
                    n %= BANKS
                    at = before if back else (lambda i, per, m: now(i, per, m, credit=True))
                    if KB <= n < KB + NB:
                        pe.wait_ge(v_ready, at(t, NB, n - KB + 1))
                    else:
                        pe.wait_ge(roped, at(t, ROPES, (n if n < KB else n - NB) + 1))

                def project(t, w, n, j):
                    free_bank(t, n)
                    for h in range(2):
                        for k in range(KC):
                            ins = nc.tensor.matmul(proj[:, n % 2, h * NB * P:(h + 1) * NB * P],
                                                   w[:, k, (2 * j + h) * HD:(2 * j + h + 1) * HD],
                                                   xs[:, k].rearrange("p b t -> p (b t)"),
                                                   start=(k == 0), stop=(k == KC - 1))
                    ins.then_inc(proj_done, 1)

                def project_keys(t):
                    pe.wait_ge(xs_ready, now(t, 1, 1))
                    for j in range(KB):
                        project(t, W.k, j, j)

                def project_rest(t):
                    for b in range(NB):
                        n = KB + b
                        free_bank(t, n)
                        for k in range(KC):
                            ins = nc.tensor.matmul(proj[:, n % 2], xs[:, k, b], W.v[:, k, :],
                                                   start=(k == 0), stop=(k == KC - 1))
                        ins.then_inc(proj_done, 1)
                    for j in range(2):
                        project(t, W.q, KB + NB + j, j)

                def scores(t, par, u):
                    g, b = u // NB, u % NB
                    pe.wait_ge(rotated, now(t, ROPES, n_rope["q", 2 * g + 1], credit=True))
                    for c in range(2):
                        if u:
                            pe.wait_ge(tanh_done, now(t, 2 * UNITS, 2 * (u - 1) + c + 1, credit=True))
                        else:
                            pe.wait_ge(tanh_done, before(t, 2 * UNITS, 2 * (UNITS - 1) + c + 1))
                        nc.tensor.matmul(score[:, c], kT[:, par ^ c, g, b],
                                         qT[:, g * GROUP:(g + 1) * GROUP, b, :],
                                         start=True, stop=True).then_inc(score_done, 1)

                def weigh(t, par, u):
                    g, b = u // NB, u % NB
                    pe.wait_ge(masked, now(t, 2 * UNITS, 2 * u + 2))
                    if u == 0:
                        pe.wait_ge(v_ready, now(t, NB, NB, credit=True))
                    if u:
                        pe.wait_ge(enc_done, now(t, UNITS, u, credit=True))
                    else:
                        pe.wait_ge(enc_done, before(t, UNITS, UNITS))
                    for h in range(GROUP):
                        at = (h % 2) * (HD + 1)
                        for c in range(2):
                            ins = nc.tensor.matmul(pv[:, h // 2, at:at + HD + 1],
                                                   probs[:, u % 2, c, h * P:(h + 1) * P],
                                                   v[:, par ^ c, b, g, :], start=(c == 0), stop=(c == 1))
                    ins.then_inc(pv_done, 1)

                def turn(t, u):
                    pe.wait_ge(enc_done, now(t, UNITS, u + 1, credit=True))
                    if u:
                        pe.wait_ge(encT_done, now(t, UNITS, u, credit=True))
                    else:
                        pe.wait_ge(encT_done, before(t, UNITS, UNITS))
                    for h in range(GROUP):
                        ins = nc.tensor.transpose(turned[:, h * P:(h + 1) * P], enc[:, u % 2, h], G.ident[:])
                    ins.then_inc(turn_done, 1)

                def begin(t, par):
                    project_keys(t)
                    project_rest(t)

                def body(t, par, nxt):
                    for u in range(UNITS):
                        scores(t, par, u)
                        for j in q_banks(u):
                            project(t, W.q, KB + NB + j, j)
                        if u >= 1:
                            weigh(t, par, u - 1)
                        if u >= 2:
                            turn(t, u - 2)
                    if nxt is not None:
                        project_keys(nxt)
                    weigh(t, par, UNITS - 1)
                    turn(t, UNITS - 2)
                    if nxt is not None:
                        project_rest(nxt)
                    turn(t, UNITS - 1)
                    pe.wait_ge(x_added, before(t, 1, 1))
                    for b in range(NB):
                        pe.wait_ge(encT_done, now(t, UNITS, UNITS - NB + 1 + b, credit=True))
                        for h in range(NH):
                            ins = nc.tensor.matmul(y[:, b], encT[:, b, h], W.o[:, h], start=(h == 0), stop=(h == NH - 1))
                    ins.then_inc(y_done, 1)

                turns(pe, begin, body)

            @block.scalar
            def _(act):
                act.sem_inc(v_ready, NB)
                act.sem_inc(tanh_done, 2 * UNITS)
                act.sem_inc(encT_done, UNITS)
                act.wait_ge(cleared, 2)

                def begin(t, par):
                    for b in range(NB):
                        act.wait_ge(proj_done, now(t, BANKS, KB + b + 1, credit=True))
                        nc.scalar.copy(v[:, par, b, :, 0:HD], proj[:, (KB + b) % 2].rearrange("p (g d) -> p g d", g=NKV))\
                            .then_inc(v_ready, 1)

                def softmax_part(t, u):
                    for c in range(2):
                        act.wait_ge(score_done, now(t, 2 * UNITS, 2 * u + c + 1))
                        if u:
                            act.wait_ge(exp_done, now(t, 2 * UNITS, 2 * (u - 1) + c + 1))
                        nc.scalar.activation(capped[:, c], score[:, c], ACT.Tanh, scale=SCALE).then_inc(tanh_done, 1)
                    for c in range(2):
                        act.wait_ge(tanh_done, now(t, 2 * UNITS, 2 * u + c + 1, credit=True))
                        if c == 0:
                            act.wait_ge(pv_done, now(t, UNITS, u - 1, credit=True))
                        nc.scalar.activation(probs[:, u % 2, c], capped[:, c], ACT.Exp, scale=CAP)\
                            .then_inc(exp_done, 1)

                def evacuate(t, u):
                    g, b = u // NB, u % NB
                    act.wait_ge(turn_done, now(t, UNITS, u + 1, credit=True))
                    if u == 0:
                        act.wait_ge(y_done, before(t, 1, 1))
                    nc.scalar.copy(encT[:, b, g * GROUP:(g + 1) * GROUP].rearrange("p h t -> p (h t)"), turned[:])\
                        .then_inc(encT_done, 1)

                def body(t, par, nxt):
                    for u in range(UNITS):
                        softmax_part(t, u)
                        if u >= 2:
                            evacuate(t, u - 2)
                    evacuate(t, UNITS - 2)
                    if nxt is not None:
                        begin(nxt, 1 - par)
                    evacuate(t, UNITS - 1)

                turns(act, begin, body)

            @block.vector
            def _(dve):
                dve.sem_inc(roped, ROPES)
                dve.sem_inc(rotated, ROPES)
                dve.sem_inc(enc_done, UNITS)
                dve.sem_inc(x_added, 1)
                dve.wait_ge(w_in, LOADS)
                dve.wait_ge(cleared, 2)
                H = HD // 2

                def rope(t, par, kind, j):
                    cos = spread(W.cos[:, bass.ds(t * P, P)].unsqueeze(1), [P, 4, P])
                    sin = W.sin[:, bass.ds(t * P, P)].unsqueeze(1)
                    n = n_rope[kind, j]
                    bank = (j if kind == "k" else KB + NB + j)
                    dve.wait_ge(proj_done, now(t, BANKS, bank + 1, credit=True))
                    src = proj[:, bank % 2].rearrange("p (r t) -> p r t", t=P)
                    a = rope_a[:, n % 2].rearrange("p (r t) -> p r t", t=P)
                    b = rope_b[:, n % 2].rearrange("p (r t) -> p r t", t=P)
                    nc.vector.tensor_tensor(a, src, cos, ALU.mult)
                    nc.vector.tensor_tensor(b[0:H], src[H:HD], spread(sin[H:HD], [H, 4, P]), ALU.mult)
                    nc.vector.tensor_tensor(b[H:HD], src[0:H], spread(sin[0:H], [H, 4, P]), ALU.mult)\
                        .then_inc(roped, 1)
                    dve.wait_ge(roped, now(t, ROPES, n, credit=True))
                    dst = kT[:, par, 2 * j:2 * j + 2] if kind == "k" else qT[:, 2 * j:2 * j + 2]
                    nc.vector.tensor_tensor(dst.rearrange("p h b t -> p (h b t)"), rope_a[:, n % 2], rope_b[:, n % 2], ALU.add)\
                        .then_inc(rotated, 1)

                def begin(t, par):
                    for j in range(KB):
                        rope(t, par, "k", j)
                    for j in range(2):
                        rope(t, par, "q", j)

                def body(t, par, nxt):
                    steps = Steps(dve, dve_steps, t, UNITS)

                    def normalise(u):
                        dve.wait_ge(pv_done, now(t, UNITS, u + 1, credit=True))
                        dve.wait_ge(turn_done, now(t, UNITS, u - 1, credit=True))
                        rows = pv[:, :, 0:2 * (HD + 1)].rearrange("p a (h d) -> p a h d", h=2)
                        r = rden[:].rearrange("p (a h d) -> p a h d", a=2, h=2)
                        steps.then(nc.vector.reciprocal(r, rows[:, :, :, HD:HD + 1]))
                        nc.vector.tensor_tensor(enc[:, u % 2].rearrange("p (a h) d -> p a h d", a=2),
                                                rows[:, :, :, 0:HD], spread(r, [P, 2, 2, HD]), ALU.mult)\
                            .then_inc(enc_done, 1)

                    for u in range(UNITS):
                        for j in q_banks(u):
                            rope(t, par, "q", j)
                        if u >= 1:
                            normalise(u - 1)
                    if nxt is not None:
                        for j in range(KB):
                            rope(nxt, 1 - par, "k", j)
                    normalise(UNITS - 1)
                    if nxt is not None:
                        for j in range(2):
                            rope(nxt, 1 - par, "q", j)
                    dve.wait_ge(y_done, now(t, 1, 1, credit=True))
                    x_tile = G.x[:, :, bass.ds(t, 1), :].rearrange("p b i d -> p b (i d)")
                    nc.vector.tensor_tensor(x_tile, y[:], x_tile, ALU.add).then_inc(x_added, 1)
                    steps.close()

                turns(dve, begin, body)



def staged_linear(nc, G, tag, wT, bias, w_in=None, loads=0, store=False):
    PAIRS = 2
    with Phase(nc, tag) as ph:
        xs = ph.sb("xs", [P, PAIRS, KC, NB, P])
        y = [ph.ps(f"y{j}", [P, NB, D]) for j in range(PAIRS)]
        xs_ready = [ph.sem(f"xs_ready{b}") for b in range(NB)]
        y_done = ph.sem("y_done")
        x_added = ph.sem("x_added")
        dve_steps = ph.sem("dve_steps")
        apart = ph.sem("apart")
        with ph.block() as block:
            if store:
                @block.sync
                def _(sp):
                    for turn in range(TILES // PAIRS):
                        tiles = slice(turn * PAIRS, (turn + 1) * PAIRS)
                        sp.wait_ge(x_added, (turn + 2) * PAIRS)
                        for b in range(NB):
                            sp.dma_start(G.out[b].rearrange("(i p) d -> p i d", p=P)[:, tiles], G.x[:, b, tiles])\
                                .then_inc(G.stored, 16)
                    sp.wait_ge(G.stored, 16 * NB * (TILES // PAIRS))

            @block.gpsimd
            def _(pool):
                with pool.Fori(0, TILES // PAIRS) as it:
                    for j in range(PAIRS):
                        hold_apart(pool, y_done, before(it, PAIRS, j + 1), apart)
                        nc.gpsimd.tensor_copy(xs[:, j, :, 0], G.xnT[:, :, 0, bass.ds((it * PAIRS + j) * P, P)])\
                            .then_inc(xs_ready[0], 1)

            @block.scalar
            def _(act):
                with act.Fori(0, TILES // PAIRS) as it:
                    for j in range(PAIRS):
                        act.wait_ge(y_done, before(it, PAIRS, j + 1))
                        nc.scalar.copy(xs[:, j, :, 1], G.xnT[:, :, 1, bass.ds((it * PAIRS + j) * P, P)])\
                            .then_inc(xs_ready[1], 1)

            @block.tensor
            def _(pe):
                pe.sem_inc(y_done, PAIRS)
                if w_in is not None:
                    pe.wait_ge(w_in, loads)
                with pe.Fori(0, TILES // PAIRS) as it:
                    for j in range(PAIRS):
                        pe.wait_ge(x_added, before(it, PAIRS, j + 1))
                        for b in range(NB):
                            pe.wait_ge(xs_ready[b], now(it, PAIRS, j + 1))
                            for k in range(KC):
                                ins = nc.tensor.matmul(y[j][:, b], xs[:, j, k, b], wT[:, k], start=(k == 0), stop=(k == KC - 1))
                        ins.then_inc(y_done, 1)

            @block.vector
            def _(dve):
                dve.sem_inc(x_added, PAIRS)
                if w_in is not None:
                    dve.wait_ge(w_in, loads)
                with dve.Fori(0, TILES // PAIRS) as it:
                    steps = Steps(dve, dve_steps, it, PAIRS if bias is not None else 0)
                    for j in range(PAIRS):
                        dve.wait_ge(y_done, now(it, PAIRS, j + 1, credit=True))
                        x_tile = G.x[:, :, bass.ds(it * PAIRS + j, 1), :].rearrange("p b i d -> p b (i d)")
                        if bias is not None:
                            steps.then(nc.vector.tensor_tensor(x_tile, x_tile, spread(bias[:].unsqueeze(1), [P, NB, D]), ALU.add))
                        nc.vector.tensor_tensor(x_tile, y[j][:], x_tile, ALU.add).then_inc(x_added, 1)
                    steps.close()


def l0_ffn(nc, G, load_ahead=None):
    with Phase(nc, "f0w") as W:
        w = W.sb("w", [P, KC, D])
        bias = W.sb("bias", [P, D])
        wT = W.sb("wT", [P, KC, D])
        w_in = W.sem("w_in")

        def load(sp):
            sp.dma_start(w[:], G.dram["L0_ffn_weight"].rearrange("(k p) n -> p k n", p=P)).then_inc(w_in, 16)
            sp.dma_start(bias[:], G.dram["L0_ffn_bias"].partition_broadcast(P)).then_inc(w_in, 16)
            if load_ahead:
                load_ahead(sp)
        norm_phase(nc, G, "f0n", load=load)
        with Phase(nc, "f0b") as ph:
            alpha = ph.sb("alpha", [P, KC])
            bw = ph.sb("bw", [P, KC, D])
            turned = ph.ps("turned", [P, KC, D])
            steps_sem, bw_ready, turn_done = ph.sem("steps"), ph.sem("bw_ready"), ph.sem("turn_done")
            with ph.block() as block:
                @block.vector
                def _(dve):
                    steps = Steps(dve, steps_sem)
                    dve.wait_ge(w_in, 2 * 16)
                    nc.vector.tensor_reduce(alpha[:], w[:], AX.X, ALU.add, apply_absolute_value=True)
                    steps.then(nc.vector.tensor_scalar(bw[:], w[:], 0.0, 2.0, ALU.is_ge, ALU.mult))
                    steps.then(nc.vector.tensor_scalar(alpha[:], alpha[:], 1.0 / D, None, ALU.mult))
                    for k in range(KC):
                        n = steps.mark(nc.vector.tensor_scalar(bw[:, k], bw[:, k], -1.0, alpha[:, k:k + 1], ALU.add, ALU.mult))
                    steps.hold(n)
                    steps.then(nc.vector.tensor_tensor(bw[:], bw[:], w[:], ALU.subtract))
                    nc.vector.tensor_tensor(bw[:], bw[:], w[:], ALU.add).then_inc(bw_ready, 1)
                    dve.wait_ge(turn_done, 1)
                    nc.vector.tensor_copy(wT[:], turned[:])

                @block.tensor
                def _(pe):
                    pe.wait_ge(bw_ready, 1)
                    for k in range(KC):
                        for o in range(KC):
                            ins = nc.tensor.transpose(turned[:, k, o * P:(o + 1) * P], bw[:, o, k * P:(k + 1) * P], G.ident[:])
                    ins.then_inc(turn_done, 1)
        staged_linear(nc, G, "f0l", wT, bias)


QL, KVL, DR, DK, DV = 192, 64, 64, 128, 128
PAIRS = NH // 2
QREST = QL - P
IH, ID, TOPK = 8, 128, 8
SEL = IH * TOPK
BIG = -1e30


def load_l1_attn(nc, G, W, sem):
    def load(sp):
        I = G.dram
        for dst, src in ((W.early["qcT"][:], I["l1_qcT"]), (W.early["kcT"][:], I["l1_kcT"]), (W.early["vT"][:], I["l1_vT"]),
                         (W.early["o"][:], I["L1_attn_W_o"].rearrange("(h p) n -> p h n", p=P)),
                         (W.q0[:, :, 0:P], I["l1_qr"][0:P]), (W.q1[:, :, 0:P], I["l1_qr"][P:QL]),
                         (W.early["k"][:], I["l1_k"].rearrange("(k p) n -> p k n", p=P)),
                         (W.early["cp"][:], I["L1_attn_W_cp"].rearrange("(k p) n -> p k n", p=P)),
                         (W.early["gate"][:], I["L1_attn_W_gate"].rearrange("(k p) n -> p k n", p=P)),
                         (W.early["idx"][:], I["L1_attn_W_idx"].rearrange("(k p) n -> p k n", p=P)),
                         (W.early["sq"][:], I["L1_attn_W_sq"]), (W.early["sk"][:], I["L1_attn_W_sk"]), (W.early["sv"][:], I["L1_attn_W_sv"]),
                         (W.early["iout"][:], I["L1_attn_W_iout"][:, 0:DV]),
                         (W.cos[:], I["l1_cos"]), (W.sin[:], I["l1_sin"]),
                         (W.early["iota"][:], I["l1_iota"]), (W.early["same"][:], I["l1_same"]), (W.early["mean"][:], I["l1_mean"])):
            sp.dma_start(dst, src).then_inc(sem, 16)
            W.loads += 16
    return load


def l1_attn(nc, G, before=None):
    with Phase(nc, "l1w") as W:
        W.loads = 0
        W.q0 = W.sb("q0", [P, PAIRS, 2 * P])
        W.q1 = W.sb("q1", [QREST, PAIRS, 2 * P])
        W.m = W.sb("m", [P, PAIRS, D])
        W.cos = W.sb("cos", [P, SEQ])
        W.sin = W.sb("sin", [P, SEQ])
        W.kA = W.sb("kA", [P, NB, SEQ])
        W.kB = W.sb("kB", [P, NB, SEQ])
        W.cp0 = W.sb("cp0", [P, NB, SEQ])
        W.cp1 = W.sb("cp1", [QREST, NB, SEQ])
        W.c = W.sb("c", [P, NB, TILES, KVL])
        W.row = W.sb("row", [P, NB, D])
        W.identb = W.sb("identb", [P, P], BF16)
        W.future = W.sb("future", [P, P], BF16)
        W.w_in = W.sem("w_in")
        with Phase(nc, "l1v") as V:
            for name, shape in (("qcT", [P, NH, QL]), ("kcT", [P, NH, KVL]), ("vT", [P, NH, KVL]), ("o", [P, NH, D]),
                                ("k", [P, KC, 3 * DR]), ("cp", [P, KC, QL]), ("gate", [P, KC, IH]),
                                ("idx", [P, KC, IH * ID]), ("sq", [ID, ID]), ("sk", [ID, ID]), ("sv", [ID, ID]),
                                ("iout", [ID, DV]), ("iota", [P, TILES]), ("same", [P, P]), ("mean", [P, NB * IH]),
                                ("xn", [P, NB, TILES, D]), ("gateT", [IH, NB, SEQ])):
                V.sb(name, shape)
            W.early = V
            load = load_l1_attn(nc, G, W, W.w_in)
            if before:
                before(nc, G, load_ahead=load)
                load = None
            norm_phase(nc, G, "l1n", load=load, keep=W.early["xn"])
            l1_weights(nc, G, W)
            l1_latents(nc, G, W)
            l1_sparse(nc, G, W)
        for b in range(NB):
            with Phase(nc, f"l1q{b}") as Q:
                Q.q = Q.sb("q", [P, PAIRS, 2, SEQ])
                l1_queries(nc, G, W, Q, b)
                l1_attend(nc, G, W, Q, b)


def l1_weights(nc, G, W):
    with Phase(nc, "l1p") as ph:
        ab = ph.ps("ab", [P, 2, BLK])
        rest = ph.ps("rest", [QREST, 2, BLK])
        m = ph.ps("m", [P, PAIRS // 2, 2, D])
        made = ph.sem("made")
        cleared = ph.sem("cleared")
        with ph.block() as block:
            @block.gpsimd
            def _(pool):
                nc.gpsimd.memset(W.identb[:], 0.0).then_inc(cleared, 1)
                nc.gpsimd.memset(W.future[:], 0.0).then_inc(cleared, 1)
                pool.wait_ge(cleared, 2)
                nc.gpsimd.affine_select(out=W.identb[:], in_=W.identb[:], compare_op=ALU.not_equal, fill=1.0,
                                        base=0, pattern=[[-1, P]], channel_multiplier=1)
                nc.gpsimd.affine_select(out=W.future[:], in_=W.future[:], compare_op=ALU.is_ge, fill=BIG,
                                        base=0, pattern=[[-1, P]], channel_multiplier=1)

            @block.tensor
            def _(pe):
                pe.wait_ge(W.w_in, W.loads)
                for h in range(NH):
                    pair, odd = h // 2, h % 2
                    at = (pair % 4) * P + (0 if odd else KVL)
                    nc.tensor.matmul(ab[:, pair // 4, at:at + KVL], W.early["qcT"][:, h, 0:P], W.early["kcT"][:, h], start=True, stop=True)
                    nc.tensor.matmul(rest[:, pair // 4, at:at + KVL], W.early["qcT"][:, h, P:QL], W.early["kcT"][:, h], start=True, stop=True)
                    ins = nc.tensor.matmul(m[odd * KVL:(odd + 1) * KVL, pair // 2, pair % 2], W.early["vT"][:, h], W.early["o"][:, h],
                                           start=True, stop=True)
                ins.then_inc(made, 1)

            @block.scalar
            def _(act):
                act.wait_ge(made, 1)
                nc.scalar.copy(W.m[:], m[:].rearrange("p a b n -> p (a b) n"))

            @block.vector
            def _(dve):
                dve.wait_ge(W.w_in, W.loads)
                dve.wait_ge(made, 1)
                nc.vector.tensor_copy(W.q0[:, :, P:2 * P], ab[:].rearrange("p a (b n) -> p (a b) n", n=P))
                nc.vector.tensor_copy(W.q1[:, :, P:2 * P], rest[:].rearrange("p a (b n) -> p (a b) n", n=P))


def l1_latents(nc, G, W):
    with Phase(nc, "l1l") as ph:
        xs = ph.sb("xs", [P, KC, BLK])
        rope_a = ph.sb("rope_a", [DR, BLK])
        rope_b = ph.sb("rope_b", [DR, BLK])
        key = ph.ps("key", [P, BLK])
        swapped = ph.ps("swapped", [DR, BLK])
        cp0, cp1 = ph.ps("cp0", [P, BLK]), ph.ps("cp1", [QREST, BLK])
        gate = ph.ps("gate", [IH, BLK])
        ctok = ph.ps("ctok", [P, TPB, KVL])
        xs_ready = ph.sem("xs_ready")
        key_done = ph.sem("key_done")
        all_done = ph.sem("all_done")
        key_read = ph.sem("key_read")
        act_done = ph.sem("act_done")
        dve_done = ph.sem("dve_done")
        dve_steps = ph.sem("dve_steps")
        apart = ph.sem("apart")
        flat = lambda t: t[:].rearrange("p b t -> p (b t)")
        xnT = G.xnT[:].rearrange("p k b t -> p k (b t)")
        c_flat = W.c[:].rearrange("p b i d -> p (b i) d")
        with ph.block() as block:
            @block.gpsimd
            def _(pool):
                with pool.Fori(0, BLOCKS) as it:
                    hold_apart(pool, all_done, before(it, 1, 1), apart)
                    nc.gpsimd.tensor_copy(xs[:], xnT[:, :, bass.ds(it * BLK, BLK)]).then_inc(xs_ready, 1)

            @block.tensor
            def _(pe):
                pe.sem_inc(all_done, 1)
                pe.wait_ge(W.w_in, W.loads)
                with pe.Fori(0, BLOCKS) as it:
                    def product(out, w):
                        for k in range(KC):
                            ins = nc.tensor.matmul(out, w(k), xnT[:, k, bass.ds(it * BLK, BLK)], start=(k == 0), stop=(k == KC - 1))
                        return ins
                    pe.wait_ge(key_read, before(it, 1, 1))
                    pe.wait_ge(dve_done, before(it, 1, 1))
                    product(key[:], lambda k: W.early["k"][:, k, 0:P])
                    product(swapped[:], lambda k: W.early["k"][:, k, P:P + DR]).then_inc(key_done, 1)
                    pe.wait_ge(act_done, before(it, 1, 1))
                    product(cp0[:], lambda k: W.early["cp"][:, k, 0:P])
                    product(cp1[:], lambda k: W.early["cp"][:, k, P:QL])
                    product(gate[:], lambda k: W.early["gate"][:, k])
                    pe.wait_ge(xs_ready, now(it, 1, 1))
                    for j in range(TPB):
                        for k in range(KC):
                            ins = nc.tensor.matmul(ctok[:, j], xs[:, k, j * P:(j + 1) * P], W.early["k"][:, k, DR:P],
                                                   start=(k == 0), stop=(k == KC - 1))
                    ins.then_inc(all_done, 1)

            @block.scalar
            def _(act):
                act.sem_inc(act_done, 1)
                act.sem_inc(key_read, 1)
                with act.Fori(0, BLOCKS) as it:
                    cols = bass.ds(it * BLK, BLK)
                    act.wait_ge(key_done, now(it, 1, 1))
                    nc.scalar.copy(flat(W.kA)[DR:P, cols], key[DR:P])
                    nc.scalar.copy(flat(W.kB)[0:KVL, cols], key[DR:P]).then_inc(key_read, 1)
                    act.wait_ge(all_done, now(it, 1, 1, credit=True))
                    nc.scalar.copy(flat(W.cp0)[:, cols], cp0[:])
                    nc.scalar.copy(flat(W.cp1)[:, cols], cp1[:])
                    nc.scalar.copy(flat(W.early["gateT"])[:, cols], gate[:])
                    nc.scalar.copy(c_flat[:, bass.ds(it * TPB, TPB), 0:KVL], ctok[:]).then_inc(act_done, 1)

            @block.vector
            def _(dve):
                dve.sem_inc(dve_done, 1)
                dve.wait_ge(W.w_in, W.loads)
                with dve.Fori(0, BLOCKS) as it:
                    steps = Steps(dve, dve_steps, it, 1)
                    cols = bass.ds(it * BLK, BLK)
                    pos = bass.ds((it % BPB) * BLK, BLK)
                    dve.wait_ge(key_done, now(it, 1, 1))
                    nc.vector.tensor_tensor(rope_a[:], key[0:DR], W.cos[0:DR, pos], ALU.mult)
                    steps.then(nc.vector.tensor_tensor(rope_b[:], swapped[:], W.sin[0:DR, pos], ALU.mult))
                    nc.vector.tensor_tensor(flat(W.kA)[0:DR, cols], rope_a[:], rope_b[:], ALU.add)
                    nc.vector.tensor_tensor(flat(W.kB)[DR:P, cols], rope_a[:], rope_b[:], ALU.add).then_inc(dve_done, 1)
                    steps.close()


def l1_sparse(nc, G, W):
    with Phase(nc, "l1s") as ph:
        top = ph.sb("top", [IH, NB, TOPK])
        index = ph.sb("index", [IH, NB, TOPK], U32)
        index_f = ph.sb("index_f", [IH, NB, TOPK])
        own = ph.sb("own", [IH, NB, IH, TOPK])
        ones = ph.sb("ones", [IH, P])
        pick = ph.sb("pick", [P, NB, TILES, SEL])
        selx = ph.sb("selx", [P, KC, NB, SEL])
        selT = ph.sb("selT", [ID, IH, NB * TOPK])
        sqT, skT, sv = (ph.sb(n, [P, P]) for n in ("sqT", "skT", "sv"))
        logits = ph.sb("logits", [P, P])
        top1 = ph.sb("top1", [P, 1])
        total = ph.sb("total", [P, 1])
        probs = ph.sb("probs", [P, P])
        weight = ph.sb("weight", [P, NB * IH])
        outT = ph.sb("outT", [P, NB * IH])
        ioT = ph.sb("ioT", [P, NB * IH])
        o_sum = ph.sb("o_sum", [DV, IH, D])
        rows = ph.sb("rows", [NB, D])
        rows_p = ph.ps("rows_p", [NB, D])
        index_p = ph.ps("index_p", [P, NB, SEL])
        selx_p = ph.ps("selx_p", [P, KC, NB, SEL])
        selT_p = ph.ps("selT_p", [ID, IH, NB * TOPK])
        work = ph.ps("work", [P, 4, P])
        row_p = ph.ps("row_p", [P, NB, D])
        dve_sem, pe_sem = ph.sem("dve"), ph.sem("pe")
        exp_done = ph.sem("exp_done")
        o_summed = ph.sem("o_summed")
        marks = {}
        with ph.block() as block:
            @block.gpsimd
            def _(pool):
                o = W.early["o"][:].rearrange("p (g k) n -> p g k n", k=NH // IH)
                nc.gpsimd.tensor_tensor(o_sum[:], o[:, :, 0], o[:, :, 1], ALU.add).then_inc(o_summed, 1)

            @block.vector
            def _(dve):
                steps = Steps(dve, dve_sem)
                nc.vector.memset(ones[:], 1.0)
                for b in range(NB):
                    steps.then(nc.vector.max(top[:, b], W.early["gateT"][:, b]))
                    steps.then(nc.vector.max_index(index[:, b], top[:, b], W.early["gateT"][:, b]))
                steps.then(nc.vector.tensor_copy(index_f[:], index[:]))
                for b in range(NB):
                    n = steps.mark(nc.vector.tensor_tensor(
                        own[:, b], spread(index_f[:, b].unsqueeze(1), [IH, IH, TOPK]),
                        spread(G.ident[0:IH, 0:IH].unsqueeze(2), [IH, IH, TOPK]), ALU.mult))
                marks["own"] = n
                dve.wait_ge(pe_sem, 1)
                for i in range(TILES):
                    n = steps.mark(nc.vector.tensor_scalar(pick[:, :, i], index_p[:], W.early["iota"][:, i:i + 1], None, ALU.is_equal))
                marks["pick"] = n

                def copy(name, dst, src, after):
                    dve.wait_ge(pe_sem, after)
                    marks[name] = steps.mark(nc.vector.tensor_copy(dst, src))
                copy("selx", selx[:], selx_p[:], 2)
                copy("selT", selT[:], selT_p[:], 3)
                dve.wait_ge(pe_sem, 4)
                nc.vector.tensor_copy(sqT[:], work[:, 0])
                nc.vector.tensor_copy(skT[:], work[:, 1])
                copy("sqkv", sv[:], work[:, 2], 4)
                dve.wait_ge(pe_sem, 5)
                steps.then(nc.vector.scalar_tensor_tensor(logits[:], work[:, 3], float(ID) ** -0.5, W.early["same"][:], ALU.mult, ALU.add))
                steps.then(nc.vector.tensor_reduce(top1[:], logits[:], AX.X, ALU.max, negate=True))
                marks["top1"] = steps.n
                dve.wait_ge(exp_done, 1)
                steps.then(nc.vector.reciprocal(total[:], total[:]))
                marks["probs"] = steps.mark(nc.vector.tensor_scalar(probs[:], probs[:], total[:], None, ALU.mult))
                copy("weight", weight[:], work[:, 0, 0:NB * IH], 6)
                copy("outT", outT[:], work[:, 1, 0:NB * IH], 7)
                copy("ioT", ioT[:], work[:, 2, 0:NB * IH], 8)
                copy("rows", rows[:], rows_p[:], 9)
                dve.wait_ge(pe_sem, 10)
                nc.vector.tensor_copy(W.row[:], row_p[:])

            @block.scalar
            def _(act):
                act.wait_ge(dve_sem, marks["top1"])
                nc.scalar.activation(probs[:], logits[:], ACT.Exp, bias=top1[:], accum_out=total[:]).then_inc(exp_done, 1)

            @block.tensor
            def _(pe):
                pe.wait_ge(dve_sem, marks["own"])
                for b in range(NB):
                    ins = nc.tensor.matmul(index_p[:, b], ones[:], own[:, b].rearrange("p h k -> p (h k)"), start=True, stop=True)
                ins.then_inc(pe_sem, 1)
                pe.wait_ge(dve_sem, marks["pick"])
                for b in range(NB):
                    for k in range(KC):
                        for i in range(TILES):
                            ins = nc.tensor.matmul(selx_p[:, k, b], W.early["xn"][:, b, i, k * P:(k + 1) * P], pick[:, b, i],
                                                   start=(i == 0), stop=(i == TILES - 1))
                ins.then_inc(pe_sem, 1)
                pe.wait_ge(dve_sem, marks["selx"])
                for h in range(IH):
                    for k in range(KC):
                        ins = nc.tensor.matmul(selT_p[:, h], W.early["idx"][:, k, h * ID:(h + 1) * ID],
                                               selx[:, k, :, h * TOPK:(h + 1) * TOPK], start=(k == 0), stop=(k == KC - 1))
                ins.then_inc(pe_sem, 1)
                pe.wait_ge(dve_sem, marks["selT"])
                sel = selT[:].rearrange("p h r -> p (h r)")
                nc.tensor.matmul(work[:, 0], W.early["sq"][:], sel, start=True, stop=True)
                nc.tensor.matmul(work[:, 1], W.early["sk"][:], sel, start=True, stop=True)
                nc.tensor.matmul(work[:, 2], sel, W.early["sv"][:], start=True, stop=True).then_inc(pe_sem, 1)
                pe.wait_ge(dve_sem, marks["sqkv"])
                nc.tensor.matmul(work[:, 3], sqT[:], skT[:], start=True, stop=True).then_inc(pe_sem, 1)
                pe.wait_ge(dve_sem, marks["probs"])
                nc.tensor.matmul(work[:, 0, 0:NB * IH], probs[:], W.early["mean"][:], start=True, stop=True).then_inc(pe_sem, 1)
                pe.wait_ge(dve_sem, marks["weight"])
                nc.tensor.matmul(work[:, 1, 0:NB * IH], sv[:], weight[:], start=True, stop=True).then_inc(pe_sem, 1)
                pe.wait_ge(dve_sem, marks["outT"])
                nc.tensor.matmul(work[:, 2, 0:NB * IH], W.early["iout"][:], outT[:], start=True, stop=True).then_inc(pe_sem, 1)
                pe.wait_ge(dve_sem, marks["ioT"])
                pe.wait_ge(o_summed, 1)
                for g in range(IH):
                    ins = nc.tensor.matmul(rows_p[:], ioT[:, g * NB:(g + 1) * NB], o_sum[:, g], start=(g == 0), stop=(g == IH - 1))
                ins.then_inc(pe_sem, 1)
                pe.wait_ge(dve_sem, marks["rows"])
                for b in range(NB):
                    ins = nc.tensor.matmul(row_p[:, b], spread(G.ident[0:NB, b:b + 1], [NB, P]), rows[:], start=True, stop=True)
                ins.then_inc(pe_sem, 1)


def l1_queries(nc, G, W, Q, b):
    with Phase(nc, f"l1r{b}") as ph:
        rope_a = ph.sb("rope_a", [P, 2, BLK])
        rope_b = ph.sb("rope_b", [P, 2, BLK])
        swapped = ph.sb("swapped", [P, 2, BLK])
        rotary = [ph.ps(f"rotary{j}", [P, BLK]) for j in range(2)]
        latent = [ph.ps(f"latent{j}", [P, BLK]) for j in range(2)]
        rotary_in = ph.sem("rotary_in")
        latent_in = ph.sem("latent_in")
        cos_done = ph.sem("cos_done")
        swap_done = ph.sem("swap_done")
        roped = ph.sem("roped")
        added = ph.sem("added")
        copied = ph.sem("copied")
        with ph.block() as block:
            @block.tensor
            def _(pe):
                with pe.Fori(0, BPB) as it:
                    for p in range(PAIRS):
                        def product(out, part):
                            nc.tensor.matmul(out[:], W.q0[:, p, part * P:(part + 1) * P],
                                             W.cp0[:, b, bass.ds(it * BLK, BLK)], start=True, stop=False)
                            return nc.tensor.matmul(out[:], W.q1[:, p, part * P:(part + 1) * P],
                                                    W.cp1[:, b, bass.ds(it * BLK, BLK)], start=False, stop=True)
                        pe.wait_ge(swap_done, it * PAIRS + p + 1)
                        product(rotary[p % 2], 0).then_inc(rotary_in, 1)
                        pe.wait_ge(copied, it * PAIRS + p + 1)
                        product(latent[p % 2], 1).then_inc(latent_in, 1)

            @block.vector
            def _(dve):
                dve.sem_inc(roped, 2)
                with dve.Fori(0, BPB) as it:
                    pos = bass.ds(it * BLK, BLK)

                    def times_sin(p):
                        dve.wait_ge(swap_done, it * PAIRS + p + 3)
                        nc.vector.tensor_tensor(rope_b[:, p % 2], swapped[:, p % 2], W.sin[:, pos], ALU.mult).then_inc(roped, 1)

                    for p in range(PAIRS):
                        dve.wait_ge(rotary_in, now(it, PAIRS, p + 1))
                        dve.wait_ge(added, it * PAIRS + p + 1)
                        nc.vector.tensor_tensor(rope_a[:, p % 2], rotary[p % 2][:], W.cos[:, pos], ALU.mult).then_inc(cos_done, 1)
                        if p:
                            times_sin(p - 1)
                    times_sin(PAIRS - 1)

            @block.gpsimd
            def _(pool):
                pool.sem_inc(added, 2)
                with pool.Fori(0, BPB) as it:
                    for p in range(PAIRS):
                        pool.wait_ge(roped, it * PAIRS + p + 3)
                        for odd in range(2):
                            half = slice(odd * DR, (odd + 1) * DR)
                            ins = nc.gpsimd.tensor_tensor(Q.q[half, p, odd, bass.ds(it * BLK, BLK)],
                                                          rope_a[half, p % 2], rope_b[half, p % 2], ALU.add)
                        ins.then_inc(added, 1)

            @block.scalar
            def _(act):
                act.sem_inc(copied, 2)
                act.sem_inc(swap_done, 2)
                H = DR // 2
                with act.Fori(0, BPB) as it:
                    for p in range(PAIRS):
                        act.wait_ge(cos_done, now(it, PAIRS, p + 1))
                        act.wait_ge(roped, it * PAIRS + p + 1)
                        for half in range(4):
                            other = half ^ 1
                            ins = nc.scalar.copy(swapped[half * H:(half + 1) * H, p % 2], rotary[p % 2][other * H:(other + 1) * H])
                        ins.then_inc(swap_done, 1)
                        act.wait_ge(latent_in, now(it, PAIRS, p + 1))
                        nc.scalar.copy(Q.q[KVL:P, p, 0, bass.ds(it * BLK, BLK)], latent[p % 2][KVL:P])
                        nc.scalar.copy(Q.q[0:KVL, p, 1, bass.ds(it * BLK, BLK)], latent[p % 2][0:KVL]).then_inc(copied, 1)


def l1_attend(nc, G, W, Q, b):
    with Phase(nc, f"l1a{b}") as ph:
        U = 4
        TURNS = NH // U
        CHUNK = BLK // P
        SCALE = 1.0 / float(np.sqrt(DK + DR))
        qs = ph.sb("qs", [P, U, P])
        neg_max = ph.sb("neg_max", [P, U])
        shift = ph.sb("shift", [P, U])
        row_sum = ph.sb("row_sum", [P, U])
        rden = ph.sb("rden", [P, U])
        rden_rows = ph.sb("rden_rows", [P, P])
        probs = ph.sb("probs", [P, U * BLK])
        probsT = ph.sb("probsT", [P, 2, TILES, P])
        pcT = ph.sb("pcT", [P, 2, PAIRS, P])
        score = ph.ps("score", [P, U * BLK])
        turned = [ph.ps(f"turned{j}", [P, BLK]) for j in range(2)]
        pv = ph.ps("pv", [P, 2, BLK // P, P])
        y = pv[:, 0, 2:4].rearrange("p a t -> p (a t)")
        apart = ph.sem("apart")
        qs_ready = ph.sem("qs_ready")
        score_done = ph.sem("score_done")
        max_done = ph.sem("max_done")
        shift_ready = ph.sem("shift_ready")
        exp_done = ph.sem("exp_done")
        turn_done = ph.sem("turn_done")
        evac = [ph.sem(f"evac{j}") for j in range(2)]
        pv_done = ph.sem("pv_done")
        pc_done = ph.sem("pc_done")
        rden_done = ph.sem("rden_done")
        laid_out = ph.sem("laid_out")
        rows_copied = ph.sem("rows_copied")
        y_done = ph.sem("y_done")
        x_added = ph.sem("x_added")
        row_added = ph.sem("row_added")

        def chunks(i):
            return -(-(i + 1) // CHUNK)

        def look(i):
            return U // chunks(i)

        def slot(i, u):
            return (u % look(i)) * chunks(i) * BLK

        turned_before = [0]
        uses = [1]
        for i in range(TILES):
            turned_before.append(turned_before[-1] + NH * chunks(i))
            uses.append(uses[-1] + NH * chunks(i) // 2)

        def use(i, it, u):
            return uses[i] + ((it * U + u) if chunks(i) == 2 else (it * (U // 2) + u // 2))

        def turns(i, it, u, c):
            return turned_before[i] + (it * U + u) * chunks(i) + c + 1

        def head(i, it, u):
            return it * U + (NH * i + u)

        def pair_of(i, it, u):
            return it * (U // 2) + (NH // 2 * i + u // 2)

        def scored(i, it, u, last):
            if last and i + 1 < TILES and look(i + 1) < look(i):
                u -= look(i) - look(i + 1)
                return (i + 1, u, NH * (i + 1) + u) if u >= 0 else None
            to = u + look(i)
            if last and to >= U:
                return (i + 1, to - U, NH * (i + 1) + to - U) if i + 1 < TILES else None
            return i, to % U, head(i, it, to)

        def for_turns(eng, step, end):
            for i in range(TILES):
                with eng.Fori(0, TURNS - 1) as it:
                    for u in range(U):
                        step(i, it, u, False)
                for u in range(U):
                    step(i, TURNS - 1, u, True)
                end(i)

        with ph.block() as block:
            @block.gpsimd
            def _(pool):
                def step(i, it, u, last):
                    n = head(i, it, u)
                    if last and i + 1 == TILES:
                        return
                    if last:
                        src = Q.q[:, u // 2, u % 2, (i + 1) * P:(i + 2) * P]
                    else:
                        src = Q.q[:, bass.ds(it * (U // 2) + (U + u) // 2, 1), u % 2, i * P:(i + 1) * P].rearrange("p a t -> p (a t)")
                    hold_apart(pool, score_done, n + 1, apart)
                    nc.gpsimd.tensor_copy(qs[:, u], src).then_inc(qs_ready, 1)

                for u in range(U):
                    nc.gpsimd.tensor_copy(qs[:, u], Q.q[:, u // 2, u % 2, 0:P]).then_inc(qs_ready, 1)
                for_turns(pool, step, lambda i: None)

            @block.tensor
            def _(pe):
                pe.sem_inc(pv_done, 1)

                def scores(i, u, n):
                    pe.wait_ge(qs_ready, n + 1)
                    if not isinstance(n, int) or n >= look(i):
                        pe.wait_ge(exp_done, n - look(i) + 1)
                    keys = (W.kA, W.kB)[u % 2]
                    at, width = slot(i, u), (i + 1) * P
                    for c in range(chunks(i)):
                        lo, hi = c * BLK, min(width, (c + 1) * BLK)
                        nc.tensor.matmul(score[:, at + lo:at + hi], qs[:, u], keys[:, b, lo:hi], start=True,
                                         stop=(hi < width), skip_group_check=True)
                    nc.tensor.matmul(score[:, at + width - P:at + width], W.identb[:], W.future[:], start=False, stop=True,
                                     skip_group_check=True).then_inc(score_done, 1)

                def step(i, it, u, last):
                    n = head(i, it, u)
                    pe.wait_ge(exp_done, n + 1)
                    for c in range(chunks(i)):
                        bank = (u + c) % 2
                        pe.wait_ge(evac[bank], use(i, it, u))
                        for j in range(c * CHUNK, min(i + 1, (c + 1) * CHUNK)):
                            ins = nc.tensor.transpose(turned[bank][:, (j % CHUNK) * P:(j % CHUNK + 1) * P],
                                                      probs[:, slot(i, u) + j * P:slot(i, u) + (j + 1) * P], G.ident[:])
                        ins.then_inc(turn_done, 1)
                    to = scored(i, it, u, last)
                    if to:
                        scores(*to)
                    pe.wait_ge(pc_done, pair_of(i, it, u) + 1)
                    if i:
                        pe.wait_ge(x_added, i)
                    k = u % 2
                    pe.wait_ge(rden_done, n + 1)
                    nc.tensor.matmul(pv[k * KVL:(k + 1) * KVL, u // 2, 1], spread(rden[:, u:u + 1], [P, KVL]),
                                     G.ident[:], start=True, stop=True, skip_group_check=True).then_inc(laid_out, 1)
                    if u % 2:
                        for bank in range(2):
                            pe.wait_ge(evac[bank], use(i, it, u) + 1)
                        for j in range(i + 1):
                            for k in range(2):
                                ins = nc.tensor.matmul(pv[k * KVL:(k + 1) * KVL, u // 2, 0], W.c[:, b, j], probsT[:, k, j],
                                                       start=(j == 0), stop=(j == i), skip_group_check=True)
                        ins.then_inc(pv_done, 1)

                def end(i):
                    for p in range(PAIRS):
                        if p in (0, PAIRS - 1):
                            p_read = max(p, PAIRS - 2)
                            pe.wait_ge(pc_done, 2 + PAIRS * i + p_read + 1)
                        ins = nc.tensor.matmul(y, pcT[:, i % 2, p], W.m[:, p], start=(p == 0), stop=(p == PAIRS - 1))
                    ins.then_inc(y_done, 1)

                for u in range(look(0)):
                    scores(0, u, u)
                for_turns(pe, step, end)

            def empty(eng, bank, i, it, u):
                copy = nc.scalar.copy if bank == 0 else nc.vector.tensor_copy
                for c in range(chunks(i)):
                    if (u + c) % 2 == bank:
                        tiles = min(i + 1, (c + 1) * CHUNK) - c * CHUNK
                        eng.wait_ge(turn_done, turns(i, it, u, c))
                        eng.wait_ge(pv_done, pair_of(i, it, u) + 1)
                        copy(probsT[:, u % 2, c * CHUNK:c * CHUNK + tiles].rearrange("p j t -> p (j t)"),
                             turned[bank][:, 0:tiles * P]).then_inc(evac[bank], 1)

            @block.scalar
            def _(act):
                act.sem_inc(evac[0], 1)

                def softmax(i, u, n):
                    at, width = slot(i, u), (i + 1) * P
                    act.wait_ge(shift_ready, n + 1)
                    if not isinstance(n, int) or n >= U:
                        act.wait_ge(laid_out, n - U + 1)
                    nc.scalar.activation(probs[:, at:at + width], score[:, at:at + width], ACT.Exp, bias=shift[:, u:u + 1],
                                         scale=SCALE, accum_out=row_sum[:, u:u + 1]).then_inc(exp_done, 1)

                def step(i, it, u, last):
                    empty(act, 0, i, it, u)
                    for v in (u - 1, u) if u % 2 else ():
                        to = scored(i, it, v, last)
                        if to:
                            act.wait_ge(turn_done, turns(i, it, v, chunks(i) - 1))
                            softmax(*to)

                for u in range(look(0)):
                    softmax(0, u, u)
                for_turns(act, step, lambda i: None)

            @block.vector
            def _(dve):
                dve.sem_inc(pc_done, 2)
                dve.sem_inc(evac[1], 1)

                def shifts(i, u, n, heads):
                    first = u - heads + 1
                    for k in range(first, u + 1):
                        at = slot(i, k)
                        dve.wait_ge(score_done, n - u + k + 1)
                        nc.vector.tensor_reduce(neg_max[:, k:k + 1], score[:, at:at + (i + 1) * P], AX.X, ALU.max, negate=True)\
                            .then_inc(max_done, 1)
                    dve.wait_ge(max_done, n + 1)
                    if not isinstance(n, int) or n >= U:
                        dve.wait_ge(exp_done, n - U + 1)
                    nc.vector.tensor_scalar(shift[:, first:u + 1], neg_max[:, first:u + 1], SCALE, None, ALU.mult)\
                        .then_inc(shift_ready, heads)

                def invert(u, n, heads):
                    dve.wait_ge(exp_done, n + 1)
                    nc.vector.reciprocal(rden[:, u - heads + 1:u + 1], row_sum[:, u - heads + 1:u + 1]).then_inc(rden_done, heads)

                def step(i, it, u, last):
                    empty(dve, 1, i, it, u)
                    to = scored(i, it, u, last)
                    if to and look(to[0]) == U:
                        if u % 2:
                            shifts(*to, 2)
                            invert((to[1] - 2) % U, to[2] - 2, 2)
                    elif to:
                        shifts(*to, 1)
                        begins = last and i + 1 < TILES and look(i) == U and to[1] == 0
                        invert((to[1] - 1) % U, to[2] - 1, 2 if begins else 1)
                    elif i + 1 == TILES and u == look(i):
                        invert(U - 1, NH * TILES - 1, 1)
                    if u % 2:
                        dve.wait_ge(pv_done, pair_of(i, it, u) + 2)
                        dst = pcT[:, i % 2, 2 * it + u // 2] if last else \
                            pcT[:, i % 2, bass.ds(it * 2 + u // 2, 1)].rearrange("p a t -> p (a t)")
                        nc.vector.tensor_copy(rden_rows[:], pv[:, u // 2, 1]).then_inc(rows_copied, 1)
                        dve.wait_ge(rows_copied, pair_of(i, it, u) + 1)
                        nc.vector.tensor_tensor(dst, pv[:, u // 2, 0], rden_rows[:], ALU.mult).then_inc(pc_done, 1)

                def end(i):
                    nc.vector.tensor_tensor(G.x[:, b, i], G.x[:, b, i], W.row[:, b], ALU.add).then_inc(row_added, 1)
                    dve.wait_ge(row_added, i + 1)
                    dve.wait_ge(y_done, i + 1)
                    nc.vector.tensor_tensor(G.x[:, b, i], y, G.x[:, b, i], ALU.add).then_inc(x_added, 1)

                for u in range(look(0)):
                    if u % 2:
                        shifts(0, u, u, 2)
                        if u > 1:
                            invert(u - 2, u - 2, 2)
                for_turns(dve, step, end)


E1, R1, F1 = 8, 8, 1024
FM = F1 // P
SCALING = 16.0 / 8.0


def route(nc, dve, steps, apart, logits, top, index, index_f, hot, iota8):
    for j in range(TPB):
        n = steps.mark(nc.vector.max(top[:, j], logits[:, j]))
    hold_apart(dve, steps.sem, now(steps.it, steps.per, n), apart)
    for j in range(TPB):
        n = steps.mark(nc.vector.max_index(index[:, j], top[:, j], logits[:, j]))
    steps.hold(n)
    steps.then(nc.vector.tensor_copy(index_f[:], index[:, :, 0:2]))
    for k in range(2):
        n = steps.mark(nc.vector.tensor_tensor(hot[:, :, k], spread(iota8[:].unsqueeze(1), [P, TPB, 8]),
                                               spread(index_f[:, :, k:k + 1], [P, TPB, 8]), ALU.is_equal))
    steps.hold(n)
ROUTE_STEPS = 2 * TPB + 3


def l1_ffn(nc, G):
    with Phase(nc, "f1w") as W:
        shapes = {"ra": ([P, KC, E1 + E1 * R1], G.dram["f1_ra"].rearrange("(k p) n -> p k n", p=P)),
                  "w1": ([P, KC, F1], G.dram["f1_w1"].rearrange("(k p) n -> p k n", p=P)),
                  "b1": ([P, FM], G.dram["f1_b1"]), "B1": ([P, F1], G.dram["f1_B1"]),
                  "A2": ([P, FM, E1 * R1], G.dram["f1_A2"].rearrange("(m p) n -> p m n", p=P)),
                  "w2": ([P, FM, D], G.dram["f1_w2"].rearrange("(m p) n -> p m n", p=P)),
                  "B2": ([P, D], G.dram["f1_B2"]),
                  "b2": ([P, D], G.dram["L1_ffn_b2"].partition_broadcast(P)),
                  "br": ([P, E1], G.dram["L1_ffn_b_r"].partition_broadcast(P)),
                  "iota8": ([P, E1], G.dram["iota8"].partition_broadcast(P))}
        w_in = W.sem("w_in")
        for name, (shape, _) in shapes.items():
            W.sb(name, shape)

        def load(sp):
            for name, (_, src) in shapes.items():
                sp.dma_start(W[name][:], src).then_inc(w_in, 16)
        norm_phase(nc, G, "f1n", load=load)
        l1_ffn_blocks(nc, G, W, w_in, 16 * len(shapes))


def l1_ffn_blocks(nc, G, W, w_in, LOADS):
    with Phase(nc, "f1b") as ph:
        xs = ph.sb("xs", [P, KC, BLK])
        logits = ph.sb("logits", [P, TPB, E1])
        top = ph.sb("top", [P, TPB, 8])
        index = ph.sb("index", [P, TPB, 8], U32)
        index_f = ph.sb("index_f", [P, TPB, 2])
        hot = ph.sb("hot", [P, TPB, 2, E1])
        slot = ph.sb("slot", [P, TPB, 2, E1])
        hot_w = ph.sb("hot_w", [P, TPB, 2, E1])
        expo = ph.sb("expo", [P, TPB, 8])
        total = ph.sb("total", [P, TPB])
        w = ph.sb("w", [P, TPB, 2])
        w_sum = ph.sb("w_sum", [P, TPB])
        z = ph.sb("z", [P, TPB, 2, E1, R1])
        wide = ph.sb("wide", [P, TPB, 2 * E1, R1])
        zT = ph.sb("zT", [P, BLK])
        wideT = ph.sb("wideT", [P, BLK])
        wb = ph.sb("wb", [P, 2, BLK])
        h = ph.sb("h", [P, 2, 2, BLK])
        h_w = ph.sb("h_w", [P, 2, 2, BLK])
        h_sum = ph.sb("h_sum", [P, FM, BLK])
        z2T = ph.sb("z2T", [P, BLK])
        HB = 3
        hid = [ph.ps(f"hid{j}", [P, BLK]) for j in range(HB)]
        first = ph.ps("first", [P, TPB, E1 + E1 * R1])
        turned = [ph.ps(f"turned{j}", [P, BLK]) for j in range(2)]
        u2 = ph.ps("u2", [P, BLK])
        y = [ph.ps("y", [P, 2, D]), u2[:].rearrange("p (a d) -> p a d", a=2)]
        xs_ready = ph.sem("xs_ready")
        first_done = ph.sem("first_done")
        top_ready = ph.sem("top_ready")
        expo_done = ph.sem("expo_done")
        z_ready = ph.sem("z_ready")
        turn_done = ph.sem("turn_done")
        turn_out = ph.sem("turn_out")
        hid_done = ph.sem("hid_done")
        h_done = ph.sem("h_done")
        u2_done = ph.sem("u2_done")
        hw_dve = ph.sem("hw_dve")
        hw_pool = ph.sem("hw_pool")
        sum_done = ph.sem("sum_done")
        z2_ready = ph.sem("z2_ready")
        y_done = ph.sem("y_done")
        x_added = ph.sem("x_added")
        dve_steps = ph.sem("dve_steps")
        apart, apart_pool = ph.sem("apart"), ph.sem("apart_pool")
        xnT = G.xnT[:].rearrange("p k b t -> p k (b t)")
        x_flat = G.x[:].rearrange("p b i d -> p (b i) d")
        ER = E1 * R1
        with ph.block() as block:
            @block.gpsimd
            def _(pool):
                pool.sem_inc(hw_pool, FM)

                def stage(t):
                    hold_apart(pool, first_done, before(t, 1, 1), apart_pool)
                    nc.gpsimd.tensor_copy(xs[:], xnT[:, :, bass.ds(t * BLK, BLK)]).then_inc(xs_ready, 1)

                def body(it, nxt):
                    if nxt is not None:
                        stage(nxt)
                    pool.wait_ge(turn_out, now(it, 4, 4, credit=True))
                    for m in range(FM):
                        pool.wait_ge(h_done, now(it, 2 * FM, 2 * m + 2, credit=True))
                        if m >= 2:
                            pool.wait_ge(sum_done, now(it, FM, m - 1, credit=True))
                        nc.gpsimd.tensor_tensor(h_w[:, m % 2, 1], h[:, m % 2, 1], wb[:, 1], ALU.mult).then_inc(hw_pool, 1)

                stage(0)
                with pool.Fori(0, BLOCKS - 1) as it:
                    body(it, it + 1)
                body(BLOCKS - 1, None)

            @block.tensor
            def _(pe):
                pe.sem_inc(first_done, 1)
                pe.sem_inc(u2_done, FM)
                pe.sem_inc(y_done, 2)
                pe.wait_ge(w_in, LOADS)

                def router(t):
                    pe.wait_ge(xs_ready, now(t, 1, 1))
                    for j in range(TPB):
                        for k in range(KC):
                            ins = nc.tensor.matmul(first[:, j], xs[:, k, j * P:(j + 1) * P], W["ra"][:, k],
                                                   start=(k == 0), stop=(k == KC - 1))
                    ins.then_inc(first_done, 1)

                def body(it, nxt):

                    def base(m):
                        if m >= HB:
                            pe.wait_ge(h_done, now(it, 2 * FM, 2 * (m - HB) + 2, credit=True))
                        else:
                            pe.wait_ge(h_done, before(it, 2 * FM, 2 * FM))
                        for k in range(KC):
                            nc.tensor.matmul(hid[m % HB][:], W["w1"][:, k, m * P:(m + 1) * P], xnT[:, k, bass.ds(it * BLK, BLK)],
                                             start=(k == 0), stop=False, skip_group_check=True)

                    def rank0(m):
                        nc.tensor.matmul(hid[m % HB][:], W["B1"][0:ER, m * P:(m + 1) * P], zT[0:ER], start=False, stop=True,
                                         skip_group_check=True).then_inc(hid_done, 1)

                    def rank1(m):
                        pe.wait_ge(h_done, now(it, 2 * FM, 2 * m + 1, credit=True))
                        nc.tensor.matmul(hid[m % HB][:], W["B1"][ER:2 * ER, m * P:(m + 1) * P], zT[ER:2 * ER], start=False,
                                         stop=True, skip_group_check=True).then_inc(hid_done, 1)

                    def adapter2(m):
                        pe.wait_ge(h_done, now(it, 2 * FM, 2 * m + 2, credit=True))
                        if m == 0:
                            pe.wait_ge(x_added, before(it, 2, 2))
                        for k in range(2):
                            ins = nc.tensor.matmul(u2[k * ER:(k + 1) * ER], W["A2"][:, m], h[:, m % 2, k],
                                                   start=(m == 0), stop=(m == FM - 1))
                        ins.then_inc(u2_done, 1)

                    base(0)
                    base(1)
                    pe.wait_ge(z_ready, now(it, 1, 1))
                    for bank in range(4):
                        if bank >= 2:
                            pe.wait_ge(turn_out, now(it, 4, bank - 1, credit=True))
                        else:
                            pe.wait_ge(turn_out, before(it, 4, 3 + bank))
                        for j in range(TPB):
                            out = turned[bank % 2][:, j * P:(j + 1) * P]
                            if bank == 0:
                                ins = nc.tensor.transpose(out, z[:, j].rearrange("p k e r -> p (k e r)"), G.ident[:])
                            elif bank == 1:
                                ins = nc.tensor.transpose(out, wide[:, j].rearrange("p k r -> p (k r)"), G.ident[:])
                            else:
                                ins = nc.tensor.matmul(out, spread(w[:, j, bank - 2:bank - 1], [P, P]), G.ident[:],
                                                       start=True, stop=True)
                        ins.then_inc(turn_done, 1)
                    pe.wait_ge(turn_out, now(it, 4, 1, credit=True))
                    rank0(0)
                    rank0(1)
                    for m in range(FM):
                        if m + 2 < FM:
                            base(m + 2)
                            rank0(m + 2)
                        rank1(m)
                        if m >= 1:
                            adapter2(m - 1)
                    adapter2(FM - 1)
                    if nxt is not None:
                        router(nxt)
                    for c in range(2):
                        if c == 0:
                            pe.wait_ge(x_added, before(it, 2, 1))
                        pe.wait_ge(sum_done, now(it, FM, FM, credit=True))
                        pe.wait_ge(z2_ready, now(it, 1, 1))
                        for j in range(2):
                            cols = slice((2 * c + j) * P, (2 * c + j + 1) * P)
                            for m in range(FM):
                                nc.tensor.matmul(y[c][:, j], h_sum[:, m, cols], W["w2"][:, m], start=(m == 0), stop=False)
                            ins = nc.tensor.matmul(y[c][:, j], z2T[:, cols], W["B2"][:], start=False, stop=True)
                        ins.then_inc(y_done, 1)

                router(0)
                with pe.Fori(0, BLOCKS - 1) as it:
                    body(it, it + 1)
                body(BLOCKS - 1, None)

            @block.scalar
            def _(act):
                act.sem_inc(h_done, 2 * FM)
                act.sem_inc(turn_out, 4)
                act.wait_ge(w_in, LOADS)

                def exponential(t):
                    act.wait_ge(top_ready, now(t, 1, 1))
                    nc.scalar.activation(expo[:], expo[:], ACT.Exp).then_inc(expo_done, 1)

                def body(it, nxt):
                    for bank, dst in enumerate((zT[:], wideT[:], wb[:, 0], wb[:, 1])):
                        act.wait_ge(turn_done, now(it, 4, bank + 1))
                        if bank == 2:
                            act.wait_ge(sum_done, before(it, FM, FM))
                        nc.scalar.copy(dst, turned[bank % 2][:]).then_inc(turn_out, 1)

                    def hidden(m, k):
                        act.wait_ge(hid_done, now(it, 2 * FM, hid_order.index((m, k)) + 1))
                        if m >= 2:
                            act.wait_ge(u2_done, now(it, FM, m - 1, credit=True))
                            act.wait_ge(hw_pool, now(it, FM, m - 1, credit=True))
                            act.wait_ge(hw_dve, now(it, FM, m - 1))
                        nc.scalar.activation(h[:, m % 2, k], hid[m % HB][:], ACT.Gelu_apprx_tanh, bias=W["b1"][:, m:m + 1])\
                            .then_inc(h_done, 1)
                    hid_order = [(0, 0), (1, 0)]
                    for m in range(FM):
                        if m + 2 < FM:
                            hid_order.append((m + 2, 0))
                        hid_order.append((m, 1))
                    for m in range(FM):
                        hidden(m, 0)
                        hidden(m, 1)
                    if nxt is not None:
                        exponential(nxt)

                exponential(0)
                with act.Fori(0, BLOCKS - 1) as it:
                    body(it, it + 1)
                body(BLOCKS - 1, None)

            @block.vector
            def _(dve):
                dve.sem_inc(sum_done, FM)
                dve.sem_inc(x_added, 2)
                dve.wait_ge(w_in, LOADS)

                def router(it):
                    steps = Steps(dve, dve_steps, it, ROUTE_STEPS + 14)
                    dve.wait_ge(first_done, now(it, 1, 1, credit=True))
                    steps.mark(nc.vector.tensor_tensor(logits[:], first[:, :, 0:E1], spread(W["br"][:].unsqueeze(1), [P, TPB, E1]), ALU.add))
                    hold_apart(dve, dve_steps, now(it, steps.per, steps.n), apart)
                    route(nc, dve, steps, apart, logits, top, index, index_f, hot, W["iota8"])
                    nc.vector.tensor_tensor(expo[:], top[:], spread(top[:, :, 0:1], [P, TPB, 8]), ALU.subtract).then_inc(top_ready, 1)
                    steps.then(nc.vector.tensor_scalar(hot[:], hot[:], SCALING, None, ALU.mult))
                    nc.vector.tensor_copy(slot[:, :, 0], hot[:, :, 0])
                    steps.then(nc.vector.tensor_tensor(slot[:, :, 1], hot[:, :, 1], hot[:, :, 0], ALU.subtract))
                    for k in range(2):
                        n = steps.mark(nc.vector.tensor_tensor(
                            z[:, :, k], first[:, :, E1:].rearrange("p j (e r) -> p j e r", r=R1),
                            spread(slot[:, :, k].unsqueeze(3), [P, TPB, E1, R1]), ALU.mult))
                    dve.wait_ge(expo_done, now(it, 1, 1))
                    steps.then(nc.vector.tensor_reduce(total[:], expo[:], AX.X, ALU.add))
                    steps.then(nc.vector.reciprocal(total[:], total[:]))
                    steps.then(nc.vector.tensor_tensor(w[:], expo[:, :, 0:2], spread(total[:].unsqueeze(2), [P, TPB, 2]), ALU.mult))
                    steps.then(nc.vector.tensor_reduce(w_sum[:], w[:], AX.X, ALU.add))
                    steps.then(nc.vector.tensor_tensor(hot_w[:], hot[:], spread(w[:].unsqueeze(3), [P, TPB, 2, E1]), ALU.mult))
                    nc.vector.tensor_copy(wide[:], spread(hot_w[:].rearrange("p j k e -> p j (k e)").unsqueeze(3), [P, TPB, 2 * E1, R1]))\
                        .then_inc(z_ready, 1)
                    for j in range(TPB):
                        x_tile = x_flat[:, bass.ds(it * TPB + j, 1), :].rearrange("p a d -> p (a d)")
                        n = steps.mark(nc.vector.scalar_tensor_tensor(x_tile, W["b2"][:], w_sum[:, j:j + 1], x_tile, ALU.mult, ALU.add))
                    steps.hold(n)
                    steps.close()

                def body(it, nxt):
                    dve.wait_ge(turn_out, now(it, 4, 4, credit=True))
                    for m in range(FM):
                        dve.wait_ge(h_done, now(it, 2 * FM, 2 * m + 1, credit=True))
                        nc.vector.tensor_tensor(h_w[:, m % 2, 0], h[:, m % 2, 0], wb[:, 0], ALU.mult).then_inc(hw_dve, 1)
                        dve.wait_ge(hw_dve, now(it, FM, m + 1))
                        dve.wait_ge(hw_pool, now(it, FM, m + 1, credit=True))
                        if m == 0:
                            dve.wait_ge(y_done, before(it, 2, 2))
                        nc.vector.tensor_tensor(h_sum[:, m], h_w[:, m % 2, 0], h_w[:, m % 2, 1], ALU.add).then_inc(sum_done, 1)
                    dve.wait_ge(u2_done, now(it, FM, FM, credit=True))
                    nc.vector.tensor_tensor(z2T[:], u2[:], wideT[:], ALU.mult).then_inc(z2_ready, 1)
                    if nxt is not None:
                        router(nxt)
                    for c in range(2):
                        dve.wait_ge(y_done, now(it, 2, c + 1, credit=True))
                        x_tiles = x_flat[:, bass.ds(it * TPB + 2 * c, 2), :]
                        nc.vector.tensor_tensor(x_tiles, y[c][:], x_tiles, ALU.add).then_inc(x_added, 1)

                router(0)
                with dve.Fori(0, BLOCKS - 1) as it:
                    body(it, it + 1)
                body(BLOCKS - 1, None)


LH, LD = 16, 16
HPC = P // LD


def linear_attn(nc, G, tag, gated):
    with Phase(nc, tag + "w") as W:
        pre = "L3_attn_" if gated else "L2_attn_"
        wide = [P, 3 * D]
        loads = {"w": ([P, KC, 3 * D], G.dram[tag + "_w"].rearrange("(k p) n -> p k n", p=P)),
                 "b": (wide, G.dram[tag + "_b"].partition_broadcast(P)),
                 "wo": ([P, KC, D], G.dram[tag + "_wo"].rearrange("(k p) n -> p k n", p=P)),
                 "bo": ([P, D], G.dram[pre + "bo"].partition_broadcast(P)),
                 "same_head": ([P, P], G.dram["same_head"]), "head_of": ([P, HPC], G.dram["head_of"])}
        if gated:
            loads["ln_g"] = ([P, D], G.dram["L3_attn_ln_g"].partition_broadcast(P))
            loads["ln_b"] = ([P, D], G.dram["L3_attn_ln_b"].partition_broadcast(P))
        for name, (shape, _) in loads.items():
            W.sb(name, shape)
        W.w_in = W.sem("w_in")
        W.loads = 16 * len(loads)
        W.k = W.sb("k_all", [P, NB, TILES, D])
        W.v = W.sb("v_all", [P, NB, TILES, KC, P + 1])
        W.u = W.sb("u_all", [P, NB, TILES, D]) if gated else None
        W.ug = W.sb("ug_all", [P, NB, TILES, D]) if gated else None
        W.qT = W.sb("qT", [P, KC, NB, SEQ])
        W.kv = W.sb("kv", [P, NB, KC, P + HPC])

        def load(sp):
            for name, (_, src) in loads.items():
                sp.dma_start(W[name][:], src).then_inc(W.w_in, 16)
        norm_phase(nc, G, tag + "n", load=load)
        linear_project(nc, G, W, tag + "p", gated)
        linear_state(nc, G, W, tag + "s")
        linear_output(nc, G, W, tag + "o", gated)


def linear_project(nc, G, W, tag, gated):
    with Phase(nc, tag) as ph:
        xs = ph.sb("xs", [P, KC, NB, P])
        s = ph.sb("s", [P, NB, 3 * D])
        expo = ph.sb("expo", [P, NB, 2 * D])
        low = ph.sb("low", [P, NB, 2 * D])
        relu = ph.sb("relu", [P, NB, 2 * D])
        q = ph.sb("q", [P, NB, D])
        half = ph.sb("half", [P, NB, 2 * D]) if gated else None
        tanh = ph.sb("tanh", [P, NB, 2 * D]) if gated else None
        prod = [ph.ps(f"prod{b}", [P, 2 * BLK]) for b in range(NB)]
        turned = [ph.ps(f"turned{b}", [P, KC, P]) for b in range(NB)]
        QK = D if gated else 2 * D
        xs_ready = ph.sem("xs_ready")
        prod_done = ph.sem("prod_done")
        s_ready = ph.sem("s_ready")
        expo_done = ph.sem("expo_done")
        q_ready = ph.sem("q_ready")
        stored = ph.sem("stored")
        turn_done = ph.sem("turn_done")
        turn_out = ph.sem("turn_out")
        dve_steps = ph.sem("dve_steps")
        apart = ph.sem("apart")
        with ph.block() as block:
            @block.gpsimd
            def _(pool):
                nc.gpsimd.memset(W.v[:, :, :, :, P:P + 1], 1.0)

                def stage(i):
                    for b in range(NB):
                        hold_apart(pool, prod_done, before(i, NB, b + 1), apart)
                        nc.gpsimd.tensor_copy(xs[:, :, b], G.xnT[:, :, b, bass.ds(i * P, P)]).then_inc(xs_ready, 1)

                def weigh_gate(i):
                    for b in range(NB):
                        u, ug = (t[:, b, bass.ds(i, 1)].rearrange("p a d -> p (a d)") for t in (W.u, W.ug))
                        pool.wait_ge(stored, now(i, NB, b + 1, credit=True))
                        nc.gpsimd.tensor_tensor(ug, u, W["ln_g"][:], ALU.mult)
                        nc.gpsimd.tensor_tensor(u, u, W["ln_b"][:], ALU.mult)

                stage(0)
                with pool.Fori(1, TILES) as it:
                    stage(it)
                    if gated:
                        weigh_gate(it - 1)
                if gated:
                    weigh_gate(TILES - 1)

            @block.tensor
            def _(pe):
                pe.sem_inc(prod_done, NB)
                pe.sem_inc(turn_done, NB)
                pe.wait_ge(W.w_in, W.loads)

                def product(i, b):
                    pe.wait_ge(xs_ready, now(i, NB, b + 1))
                    pe.wait_ge(s_ready, before(i, NB, b + 1))
                    for lo, hi in ((0, BLK), (BLK, 3 * D)):
                        for k in range(KC):
                            ins = nc.tensor.matmul(prod[b][:, lo:hi], xs[:, k, b], W["w"][:, k, lo:hi],
                                                   start=(k == 0), stop=(k == KC - 1))
                    ins.then_inc(prod_done, 1)

                def turn(i, b):
                    pe.wait_ge(q_ready, now(i, NB, b + 1))
                    pe.wait_ge(turn_out, before(i, NB, b + 1))
                    for k in range(KC):
                        ins = nc.tensor.transpose(turned[b][:, k], q[:, b, k * P:(k + 1) * P], G.ident[:])
                    ins.then_inc(turn_done, 1)

                for b in range(NB):
                    product(0, b)
                with pe.Fori(0, TILES - 1) as it:
                    for b in range(NB):
                        product(it + 1, b)
                        turn(it, b)
                for b in range(NB):
                    turn(TILES - 1, b)

            @block.scalar
            def _(act):
                act.sem_inc(turn_out, NB)

                def functions(i, b):
                    act.wait_ge(s_ready, now(i, NB, b + 1, credit=True))
                    act.wait_ge(stored, before(i, NB, b + 1))
                    if gated:
                        nc.scalar.activation(tanh[:, b], s[:, b, D:3 * D], ACT.Tanh, scale=0.5)
                        nc.scalar.activation(half[:, b], s[:, b, D:3 * D], ACT.Copy, scale=0.5)
                    nc.scalar.activation(expo[:, b, 0:QK], low[:, b, 0:QK], ACT.Exp).then_inc(expo_done, 1)

                def empty(i, b):
                    act.wait_ge(turn_done, now(i, NB, b + 1, credit=True))
                    nc.scalar.copy(W.qT[:, :, b, bass.ds(i * P, P)], turned[b][:]).then_inc(turn_out, 1)

                for b in range(NB):
                    functions(0, b)
                with act.Fori(0, TILES - 1) as it:
                    for b in range(NB):
                        empty(it, b)
                        functions(it + 1, b)
                for b in range(NB):
                    empty(TILES - 1, b)

            @block.vector
            def _(dve):
                dve.sem_inc(s_ready, NB)
                dve.sem_inc(stored, NB)
                dve.wait_ge(W.w_in, W.loads)
                with dve.Fori(0, TILES) as it:
                    steps = Steps(dve, dve_steps, it, 2 * NB)
                    for b in range(NB):
                        dve.wait_ge(prod_done, now(it, NB, b + 1, credit=True))
                        steps.then(nc.vector.tensor_tensor(s[:, b], prod[b][:, 0:3 * D], W["b"][:], ALU.add))
                        nc.vector.tensor_scalar(low[:, b, 0:QK], s[:, b, 0:QK], 0.0, None, ALU.min).then_inc(s_ready, 1)
                    for b in range(NB):
                        steps.then(nc.vector.tensor_scalar(relu[:, b, 0:QK], s[:, b, 0:QK], 0.0, -1.0 if gated else 0.0, ALU.max, ALU.add))
                        dve.wait_ge(expo_done, now(it, NB, b + 1))
                        dve.wait_ge(turn_done, before(it, NB, b + 1))
                        nc.vector.tensor_tensor(q[:, b], expo[:, b, 0:D], relu[:, b, 0:D], ALU.add).then_inc(q_ready, 1)
                        k_dst = W.k[:, b, bass.ds(it, 1)].rearrange("p a d -> p (a d)")
                        v_dst = W.v[:, b, bass.ds(it, 1), :, 0:P].rearrange("p a k d -> p (a k) d")
                        if gated:
                            dve.wait_ge(q_ready, now(it, NB, b + 1))
                            nc.vector.tensor_copy(k_dst, q[:, b])
                            u_dst = W.u[:, b, bass.ds(it, 1)].rearrange("p a d -> p (a d)")
                            nc.vector.scalar_tensor_tensor(u_dst, tanh[:, b, D:2 * D], 1.0, half[:, b, D:2 * D], ALU.add, ALU.mult)
                            nc.vector.scalar_tensor_tensor(v_dst, tanh[:, b, 0:D].rearrange("p (k d) -> p k d", k=KC), 1.0,
                                                           half[:, b, 0:D].rearrange("p (k d) -> p k d", k=KC), ALU.add, ALU.mult)\
                                .then_inc(stored, 1)
                        else:
                            nc.vector.tensor_tensor(k_dst, expo[:, b, D:2 * D], relu[:, b, D:2 * D], ALU.add)
                            nc.vector.tensor_copy(v_dst, s[:, b, 2 * D:3 * D].rearrange("p (k d) -> p k d", k=KC)).then_inc(stored, 1)
                    steps.close()


def linear_state(nc, G, W, tag):
    with Phase(nc, tag) as ph:
        acc = [ph.ps(f"acc{b}", [P, KC, P + 1]) for b in range(NB)]
        acc_done = ph.sem("acc_done")
        with ph.block() as block:
            @block.tensor
            def _(pe):
                for b in range(NB):
                    for k in range(KC):
                        for i in range(TILES):
                            ins = nc.tensor.matmul(acc[b][:, k], W.k[:, b, i, k * P:(k + 1) * P], W.v[:, b, i, k],
                                                   start=(i == 0), stop=(i == TILES - 1))
                    ins.then_inc(acc_done, 1)

            @block.vector
            def _(dve):
                for b in range(NB):
                    dve.wait_ge(acc_done, b + 1)
                    nc.vector.tensor_tensor(W.kv[:, b, :, 0:P], acc[b][:, :, 0:P], spread(W["same_head"][:].unsqueeze(1), [P, KC, P]), ALU.mult)
                    nc.vector.tensor_tensor(W.kv[:, b, :, P:P + HPC], spread(acc[b][:, :, P:P + 1], [P, KC, HPC]),
                                            spread(W["head_of"][:].unsqueeze(1), [P, KC, HPC]), ALU.mult)


def linear_output(nc, G, W, tag, gated):
    with Phase(nc, tag) as ph:
        qs = ph.sb("qs", [P, KC, NB, P])
        den = ph.sb("den", [P, NB, KC, HPC])
        out = ph.sb("out", [P, NB, D])
        outT = ph.sb("outT", [P, NB, KC, P])
        stats = ph.sb("stats", [P, NB, 6])
        mv = ph.sb("mv", [P, NB, 2])
        veps = ph.sb("veps", [P, NB])
        rstd = ph.sb("rstd", [P, NB])
        prod = [ph.ps(f"prod{b}", [P, KC, P + HPC]) for b in range(NB)]
        turned = [ph.ps(f"turned{b}", [P, KC, P]) for b in range(NB)]
        y = ph.ps("y", [P, NB, D])
        qs_ready = ph.sem("qs_ready")
        prod_done = ph.sem("prod_done")
        var_ready, rstd_ready = ph.sem("var_ready"), ph.sem("rstd_ready")
        out_ready = ph.sem("out_ready")
        turn_done = ph.sem("turn_done")
        turn_out = ph.sem("turn_out")
        y_done = ph.sem("y_done")
        x_added = ph.sem("x_added")
        dve_steps = ph.sem("dve_steps")
        apart, apart_pool = ph.sem("apart"), ph.sem("apart_pool")
        N = P if gated else P + HPC
        with ph.block() as block:
            @block.gpsimd
            def _(pool):
                with pool.Fori(0, TILES) as it:
                    for b in range(NB):
                        hold_apart(pool, prod_done, before(it, NB, b + 1), apart_pool)
                        nc.gpsimd.tensor_copy(qs[:, :, b], W.qT[:, :, b, bass.ds(it * P, P)]).then_inc(qs_ready, 1)
                    if gated:
                        pool.wait_ge(var_ready, now(it, 1, 1))
                        nc.gpsimd.tensor_tensor(rstd[:], veps[:], G.minus_half[:, 0:NB], ALU.pow).then_inc(rstd_ready, 1)

            @block.tensor
            def _(pe):
                pe.sem_inc(prod_done, NB)
                pe.sem_inc(turn_done, NB)
                pe.sem_inc(y_done, 1)

                def product(i, b):
                    pe.wait_ge(qs_ready, now(i, NB, b + 1))
                    pe.wait_ge(out_ready, before(i, NB, b + 1))
                    for k in range(KC):
                        ins = nc.tensor.matmul(prod[b][:, k, 0:N], qs[:, k, b], W.kv[:, b, k, 0:N], start=True, stop=True)
                    ins.then_inc(prod_done, 1)

                def turn(i, b):
                    pe.wait_ge(out_ready, now(i, NB, b + 1, credit=True))
                    pe.wait_ge(turn_out, before(i, NB, b + 1))
                    for k in range(KC):
                        ins = nc.tensor.transpose(turned[b][:, k], out[:, b, k * P:(k + 1) * P], G.ident[:])
                    ins.then_inc(turn_done, 1)

                def output(i):
                    pe.wait_ge(x_added, before(i, 1, 1))
                    for b in range(NB):
                        pe.wait_ge(turn_out, now(i, NB, b + 1, credit=True))
                        for k in range(KC):
                            ins = nc.tensor.matmul(y[:, b], outT[:, b, k], W["wo"][:, k], start=(k == 0), stop=(k == KC - 1))
                    ins.then_inc(y_done, 1)

                for b in range(NB):
                    product(0, b)
                with pe.Fori(0, TILES - 1) as it:
                    for b in range(NB):
                        product(it + 1, b)
                        turn(it, b)
                    output(it)
                for b in range(NB):
                    turn(TILES - 1, b)
                output(TILES - 1)

            @block.scalar
            def _(act):
                act.sem_inc(turn_out, NB)
                with act.Fori(0, TILES) as it:
                    for b in range(NB):
                        act.wait_ge(turn_done, now(it, NB, b + 1, credit=True))
                        if b == 0:
                            act.wait_ge(y_done, before(it, 1, 1))
                        nc.scalar.copy(outT[:, b], turned[b][:]).then_inc(turn_out, 1)

            @block.vector
            def _(dve):
                dve.sem_inc(out_ready, NB)
                dve.sem_inc(x_added, 1)

                def x_tile(i):
                    return G.x[:, :, bass.ds(i, 1), :].rearrange("p b i d -> p b (i d)")

                def add_output(i):
                    dve.wait_ge(y_done, now(i, 1, 1, credit=True))
                    nc.vector.tensor_tensor(x_tile(i), y[:], x_tile(i), ALU.add).then_inc(x_added, 1)

                def turn(i, first):
                    steps = Steps(dve, dve_steps, i, 3 * NB + 1 if gated else 2 * NB + 1)
                    add_bias = lambda: steps.mark(nc.vector.tensor_tensor(x_tile(i), x_tile(i), spread(W["bo"][:].unsqueeze(1), [P, NB, D]), ALU.add))
                    if gated:
                        for b in range(NB):
                            dve.wait_ge(prod_done, now(i, NB, b + 1, credit=True))
                            n = steps.mark(nc.vector.bn_stats(stats[:, b], prod[b][:, :, 0:P]))
                        hold_apart(dve, dve_steps, now(i, steps.per, n), apart)
                        for b in range(NB):
                            n = steps.mark(nc.vector.bn_aggr(mv[:, b], stats[:, b]))
                        steps.hold(n)
                        nc.vector.tensor_scalar(veps[:], mv[:, :, 1], EPS, None, ALU.add).then_inc(var_ready, 1)
                        add_bias()
                        for b in range(NB):
                            dve.wait_ge(turn_done, before(i, NB, b + 1))
                            o, ug = (t.rearrange("p (k d) -> p k d", k=KC) for t in (out[:, b], W.ug[:, b, bass.ds(i, 1)].rearrange("p a d -> p (a d)")))
                            ub = W.u[:, b, bass.ds(i, 1)].rearrange("p a d -> p (a d)")
                            steps.then(nc.vector.scalar_tensor_tensor(o, prod[b][:, :, 0:P], mv[:, b, 0:1], ug, ALU.subtract, ALU.mult))
                            if b == 0:
                                dve.wait_ge(rstd_ready, now(i, 1, 1))
                            nc.vector.scalar_tensor_tensor(out[:, b], out[:, b], rstd[:, b:b + 1], ub, ALU.mult, ALU.add).then_inc(out_ready, 1)
                            if b == 0 and not first:
                                add_output(i - 1)
                    else:
                        add_bias()
                        for b in range(NB):
                            dve.wait_ge(prod_done, now(i, NB, b + 1, credit=True))
                            steps.then(nc.vector.tensor_scalar(den[:, b], prod[b][:, :, P:P + HPC], 1e-8, None, ALU.add))
                            steps.then(nc.vector.reciprocal(den[:, b], den[:, b]))
                            dve.wait_ge(turn_done, before(i, NB, b + 1))
                            nc.vector.tensor_tensor(out[:, b].rearrange("p (k h d) -> p k h d", k=KC, h=HPC),
                                                    prod[b][:, :, 0:P].rearrange("p k (h d) -> p k h d", h=HPC),
                                                    spread(den[:, b].unsqueeze(3), [P, KC, HPC, LD]), ALU.mult).then_inc(out_ready, 1)
                        if not first:
                            add_output(i - 1)
                    steps.close()

                turn(0, True)
                with dve.Fori(1, TILES) as it:
                    turn(it, False)
                add_output(TILES - 1)


def l2_attn(nc, G):
    linear_attn(nc, G, "l2", False)


def l3_attn(nc, G):
    linear_attn(nc, G, "l3", True)


E2, SH = 8, 256
HC = E2 + SH // P


def l2_ffn(nc, G):
    with Phase(nc, "f2w") as W:
        loads = {"gate": ([P, KC, E2], G.dram["L2_ffn_gate_w"].rearrange("(k p) n -> p k n", p=P)),
                 "w1": ([P, KC, HC * P], G.dram["f2_w1"].rearrange("(k p) n -> p k n", p=P)),
                 "b1": ([P, HC], G.dram["f2_b1"]),
                 "w2": ([P, HC, D], G.dram["f2_w2"].rearrange("(c p) n -> p c n", p=P)),
                 "b2": ([E2, D], G.dram["L2_ffn_b2"]),
                 "sb2": ([P, D], G.dram["L2_ffn_shared_b2"].partition_broadcast(P)),
                 "iota8": ([P, E2], G.dram["iota8"].partition_broadcast(P))}
        for name, (shape, _) in loads.items():
            W.sb(name, shape)
        w_in = W.sem("w_in")

        def load(sp):
            for name, (_, src) in loads.items():
                sp.dma_start(W[name][:], src).then_inc(w_in, 16)
        norm_phase(nc, G, "f2n", load=load)
        l2_ffn_blocks(nc, G, W, w_in, 16 * len(loads))


def l2_ffn_blocks(nc, G, W, w_in, LOADS):
    with Phase(nc, "f2b") as ph:
        xs = ph.sb("xs", [P, KC, BLK])
        logits = ph.sb("logits", [P, TPB, E2])
        top = ph.sb("top", [P, TPB, 8])
        index = ph.sb("index", [P, TPB, 8], U32)
        index_f = ph.sb("index_f", [P, TPB, 2])
        hot = ph.sb("hot", [P, TPB, 2, E2])
        expo = ph.sb("expo", [P, TPB])
        g = ph.sb("g", [P, TPB, 2])
        hot_g = ph.sb("hot_g", [P, TPB, 2, E2])
        gates = ph.sb("gates", [P, TPB, E2])
        gatesT = ph.sb("gatesT", [E2, TPB, P])
        h = ph.sb("h", [P, HC, BLK])
        odd_sum = ph.sb("odd_sum", [P, D])
        OB = 3
        first = ph.ps("first", [P, TPB, E2])
        turned = ph.ps("turned", [E2, TPB, P])
        hid = [ph.ps(f"hid{j}", [P, BLK]) for j in range(2)]
        shared = ph.ps("shared", [P, D])
        out = [ph.ps(f"out{j}", [P, 2, D]) for j in range(OB)]
        xs_ready = ph.sem("xs_ready")
        first_done = ph.sem("first_done")
        gap_ready = ph.sem("gap_ready")
        expo_done = ph.sem("expo_done")
        gates_ready = ph.sem("gates_ready")
        turn_done = ph.sem("turn_done")
        turn_out = ph.sem("turn_out")
        hid_done = ph.sem("hid_done")
        h_done = ph.sem("h_done")
        shared_done = ph.sem("shared_done")
        out_done = ph.sem("out_done")
        shared_read = ph.sem("shared_read")
        out_read = ph.sem("out_read")
        logits_read = ph.sem("logits_read")
        dve_steps, route_steps, gate_steps = ph.sem("dve_steps"), ph.sem("route_steps"), ph.sem("gate_steps")
        apart, apart_pool = ph.sem("apart"), ph.sem("apart_pool")
        OUTS = TPB * E2 // 2
        xnT = G.xnT[:].rearrange("p k b t -> p k (b t)")
        x_flat = G.x[:].rearrange("p b i d -> p (b i) d")
        with ph.block() as block:
            @block.gpsimd
            def _(pool):
                with pool.Fori(0, BLOCKS) as it:
                    hold_apart(pool, first_done, before(it, 1, 1), apart_pool)
                    nc.gpsimd.tensor_copy(xs[:], xnT[:, :, bass.ds(it * BLK, BLK)]).then_inc(xs_ready, 1)

            @block.tensor
            def _(pe):
                pe.sem_inc(first_done, 1)
                pe.sem_inc(hid_done, HC)
                pe.sem_inc(out_done, OUTS)
                pe.wait_ge(w_in, LOADS)

                def router(t):
                    pe.wait_ge(xs_ready, now(t, 1, 1))
                    pe.wait_ge(logits_read, before(t, 1, 1))
                    for j in range(TPB):
                        for k in range(KC):
                            ins = nc.tensor.matmul(first[:, j], xs[:, k, j * P:(j + 1) * P], W["gate"][:, k],
                                                   start=(k == 0), stop=(k == KC - 1))
                    ins.then_inc(first_done, 1)

                def body(t, nxt):
                    if nxt is not None:
                        router(nxt)
                    for c in range(HC):
                        pe.wait_ge(h_done, now(t, HC, c - 1, credit=True) if c >= 2 else before(t, HC, HC - 1 + c))
                        for k in range(KC):
                            ins = nc.tensor.matmul(hid[c % 2][:], W["w1"][:, k, c * P:(c + 1) * P],
                                                   xnT[:, k, bass.ds(t * BLK, BLK)], start=(k == 0), stop=(k == KC - 1))
                        ins.then_inc(hid_done, 1)
                        if c == 1:
                            pe.wait_ge(gates_ready, now(t, 1, 1))
                            for j in range(TPB):
                                ins = nc.tensor.transpose(turned[:, j], gates[:, j], G.ident[:])
                            ins.then_inc(turn_done, 1)
                    pe.wait_ge(turn_out, now(t, 1, 1))
                    pe.wait_ge(h_done, now(t, HC, HC, credit=True))
                    for j in range(TPB):
                        cols = slice(j * P, (j + 1) * P)
                        pe.wait_ge(shared_read, t * TPB + j + 1)
                        nc.tensor.matmul(shared[:], gatesT[:, j], W["b2"][:], start=True, stop=False)
                        for c in range(E2, HC):
                            ins = nc.tensor.matmul(shared[:], h[:, c, cols], W["w2"][:, c], start=False, stop=(c == HC - 1))
                        ins.then_inc(shared_done, 1)
                        for e in range(0, E2, 2):
                            n = j * (E2 // 2) + e // 2
                            pe.wait_ge(out_read, now(t, OUTS, n - OB + 1, credit=True))
                            for d in range(2):
                                ins = nc.tensor.matmul(out[n % OB][:, d], h[:, e + d, cols], W["w2"][:, e + d], start=True, stop=True)
                            ins.then_inc(out_done, 1)

                router(0)
                with pe.Fori(0, BLOCKS - 1) as it:
                    body(it, it + 1)
                body(BLOCKS - 1, None)

            @block.scalar
            def _(act):
                act.sem_inc(h_done, HC)
                act.wait_ge(w_in, LOADS)

                def exponential(t):
                    act.wait_ge(gap_ready, now(t, 1, 1))
                    nc.scalar.activation(expo[:], expo[:], ACT.Exp).then_inc(expo_done, 1)

                def body(t, nxt):
                    act.wait_ge(out_done, before(t, OUTS, OUTS))
                    for c in range(HC):
                        act.wait_ge(hid_done, now(t, HC, c + 1, credit=True))
                        nc.scalar.activation(h[:, c], hid[c % 2][:], ACT.Gelu, bias=W["b1"][:, c:c + 1]).then_inc(h_done, 1)
                        if c == 3:
                            act.wait_ge(turn_done, now(t, 1, 1))
                            nc.scalar.copy(gatesT[:], turned[:]).then_inc(turn_out, 1)
                    if nxt is not None:
                        exponential(nxt)

                exponential(0)
                with act.Fori(0, BLOCKS - 1) as it:
                    body(it, it + 1)
                body(BLOCKS - 1, None)

            @block.vector
            def _(dve):
                dve.sem_inc(logits_read, 1)
                dve.sem_inc(shared_read, 1)
                dve.sem_inc(out_read, OUTS)
                dve.wait_ge(w_in, LOADS)
                GATE_STEPS = 4

                def choose(t):
                    steps = Steps(dve, route_steps, t, ROUTE_STEPS)
                    dve.wait_ge(first_done, now(t, 1, 1, credit=True))
                    nc.vector.tensor_copy(logits[:], first[:]).then_inc(logits_read, 1)
                    hold_apart(dve, logits_read, now(t, 1, 1, credit=True), apart)
                    route(nc, dve, steps, apart, logits, top, index, index_f, hot, W["iota8"])
                    steps.close()
                    nc.vector.tensor_tensor(expo[:], top[:, :, 1], top[:, :, 0], ALU.subtract).then_inc(gap_ready, 1)

                def weigh(t):
                    steps = Steps(dve, gate_steps, t, GATE_STEPS)
                    dve.wait_ge(expo_done, now(t, 1, 1))
                    steps.then(nc.vector.tensor_scalar(g[:, :, 0], expo[:], 1.0, None, ALU.add))
                    steps.then(nc.vector.reciprocal(g[:, :, 0], g[:, :, 0]))
                    steps.then(nc.vector.tensor_tensor(g[:, :, 1], expo[:], g[:, :, 0], ALU.mult))
                    steps.then(nc.vector.tensor_tensor(hot_g[:], hot[:], spread(g[:].unsqueeze(3), [P, TPB, 2, E2]), ALU.mult))
                    nc.vector.tensor_tensor(gates[:], hot_g[:, :, 0], hot_g[:, :, 1], ALU.add).then_inc(gates_ready, 1)
                    steps.close()

                def body(t, nxt):
                    steps = Steps(dve, dve_steps, t, TPB * (1 + E2 // 2))
                    x_tile = lambda j: x_flat[:, bass.ds(t * TPB + j, 1), :].rearrange("p a d -> p (a d)")
                    for j in range(TPB):
                        n = steps.mark(nc.vector.tensor_tensor(x_tile(j), x_tile(j), W["sb2"][:], ALU.add))
                    steps.hold(n)
                    if nxt is not None:
                        choose(nxt)
                    dve.wait_ge(gates_ready, now(t, 1, 1))
                    for j in range(TPB):
                        dve.wait_ge(shared_done, now(t, TPB, j + 1))
                        nc.vector.tensor_tensor(x_tile(j), shared[:], x_tile(j), ALU.add).then_inc(shared_read, 1)
                        for e in range(E2):
                            n_bank = j * (E2 // 2) + e // 2
                            into = odd_sum[:] if e % 2 else x_tile(j)
                            dve.wait_ge(out_done, now(t, OUTS, n_bank + 1, credit=True))
                            if e == 0:
                                dve.wait_ge(shared_read, t * TPB + j + 2)
                            elif e % 2 == 0:
                                steps.hold(n)
                            elif e > 1:
                                dve.wait_ge(out_read, now(t, OUTS, n_bank, credit=True))
                            gate = gates[:, j, e:e + 1]
                            if e == 1:
                                ins = nc.vector.tensor_scalar(into, out[n_bank % OB][:, 1], gate, None, ALU.mult)
                            else:
                                ins = nc.vector.scalar_tensor_tensor(into, out[n_bank % OB][:, e % 2], gate, into, ALU.mult, ALU.add)
                            if e % 2:
                                ins.then_inc(out_read, 1)
                            else:
                                n = steps.mark(ins)
                        steps.hold(n)
                        dve.wait_ge(out_read, now(t, OUTS, n_bank + 1, credit=True))
                        nc.vector.tensor_tensor(x_tile(j), x_tile(j), odd_sum[:], ALU.add)
                    steps.close()
                    if nxt is not None:
                        weigh(nxt)

                choose(0)
                weigh(0)
                with dve.Fori(0, BLOCKS - 1) as it:
                    body(it, it + 1)
                body(BLOCKS - 1, None)



def l3_ffn(nc, G):
    with Phase(nc, "f3w") as W:
        w = W.sb("w", [P, KC, D])
        variation = W.sb("variation", [P, KC, D])
        low = W.sb("low", [P, KC, D])
        wT = W.sb("wT", [P, KC, D])
        w_in, steps_sem = W.sem("w_in"), W.sem("steps")
        TH_X, SC_X, TH_W, SC_W = 0.33, 0.5, 0.2, 0.6

        def load(sp):
            sp.dma_start(w[:], G.dram["f3_w"].rearrange("(k p) n -> p k n", p=P)).then_inc(w_in, 16)
            sp.dma_start(variation[:], G.dram["f3_v"].rearrange("(k p) n -> p k n", p=P)).then_inc(w_in, 16)
        norm_phase(nc, G, "f3n", load=load, ternary=(TH_X, SC_X))
        with nc.Block() as block:
            @block.vector
            def _(dve):
                steps = Steps(dve, steps_sem)
                dve.wait_ge(w_in, 2 * 16)
                nc.vector.tensor_scalar(low[:], w[:], -TH_W, SC_W, ALU.is_lt, ALU.mult)
                steps.then(nc.vector.tensor_scalar(wT[:], w[:], TH_W, SC_W, ALU.is_gt, ALU.mult))
                steps.then(nc.vector.tensor_tensor(wT[:], wT[:], low[:], ALU.subtract))
                nc.vector.tensor_tensor(wT[:], wT[:], variation[:], ALU.add)
        staged_linear(nc, G, "f3l", wT, None, store=True)


BRANCHES = [l0_attn, l0_ffn, l1_attn, l1_ffn, l2_attn, l2_ffn, l3_attn, l3_ffn]


SEMS_OF_A_BRANCH = 80


def program(nc, dram, out):
    RETIRED.clear()
    with Phase(nc, "g") as G:
        G.dram = dram
        G.x = G.sb("x", [P, NB, TILES, D])
        G.xnT = G.sb("xnT", [P, KC, NB, SEQ])
        G.ident = G.sb("ident", [P, P])
        G.minus_half = G.sb("minus_half", [P, TPB])
        G.x_in = [G.sem(f"x_in{n}") for n in range(BLOCKS)]
        G.loading = True
        const = G.sem("const")
        G.out, G.stored = out, G.sem("stored")
        with nc.Block() as block:
            @block.sync
            def _(sp):
                for n in range(BLOCKS):
                    b, at = n // BPB, slice(n % BPB * TPB, (n % BPB + 1) * TPB)
                    sp.dma_start(G.x[:, b, at], dram["L0_attn_x"][b].rearrange("(i p) d -> p i d", p=P)[:, at]).then_inc(G.x_in[n], 16)

            @block.gpsimd
            def _(pool):
                nc.gpsimd.memset(G.minus_half[:], -0.5)
                nc.gpsimd.memset(G.ident[:], 0.0).then_inc(const, 1)
                pool.wait_ge(const, 1)
                nc.gpsimd.affine_select(out=G.ident[:], in_=G.ident[:], compare_op=ALU.not_equal, fill=1.0,
                                        base=0, pattern=[[-1, P]], channel_multiplier=1)
        for n in LAYERS:
            if n == 1 and 2 in LAYERS:
                continue
            if n == 2 and 1 in LAYERS:
                l1_attn(nc, G, before=l0_ffn)
            else:
                BRANCHES[n](nc, G)
            if nc.free_len() < SEMS_OF_A_BRANCH:
                recycle_semaphores(nc)


def rope_tables():
    fraction = np.arange(0, HD, 2, dtype=np.float32) / np.float32(HD)
    inv = (np.float32(1.0) / np.power(np.float32(10000.0), fraction)).astype(np.float32)
    angle = np.outer(np.arange(SEQ, dtype=np.float32), inv).astype(np.float32)
    cos, sin = np.cos(angle).T, np.sin(angle).T
    return np.concatenate([cos, cos]), np.concatenate([sin, -sin])


def l1_layouts(i):
    places = np.concatenate([np.arange(0, DR, 2), np.arange(1, DR, 2)])
    swapped = np.concatenate([np.arange(1, DR, 2), np.arange(0, DR, 2)])
    by_head = lambda w, d: w.reshape(w.shape[0], NH, d).transpose(2, 1, 0)
    qr = i["L1_attn_W_qr"].reshape(QL, PAIRS, 2, DR)
    kr = i["L1_attn_W_kr"]
    inv = 1.0 / 10000.0 ** (np.arange(0, DR, 2)[:DR // 2].astype(np.float32) / DR)
    angle = np.outer(np.arange(SEQ, dtype=np.float32), inv)
    cos, sin = np.cos(angle).T.astype(np.float32), np.sin(angle).T.astype(np.float32)
    rows = np.arange(P)
    order = rows // TOPK
    return {
        "l1_qcT": by_head(i["L1_attn_W_qc"], DK), "l1_kcT": by_head(i["L1_attn_W_kc"], DK),
        "l1_vT": by_head(i["L1_attn_W_v"], DV), "L1_attn_W_o": i["L1_attn_W_o"],
        "l1_qr": qr[..., places].reshape(QL, PAIRS, P),
        "l1_k": np.concatenate([kr[:, places], i["L1_attn_W_c"], kr[:, swapped]], axis=1),
        **{n: i[n] for n in ("L1_attn_W_cp", "L1_attn_W_gate", "L1_attn_W_idx", "L1_attn_W_sq",
                             "L1_attn_W_sk", "L1_attn_W_sv", "L1_attn_W_iout")},
        "l1_cos": np.concatenate([cos] * 4), "l1_sin": np.concatenate([-sin, sin] * 2),
        "l1_iota": (rows[:, None] + P * np.arange(TILES)).astype(np.float32),
        "l1_same": np.where(order[:, None] == order, 0.0, BIG).astype(np.float32),
        "l1_mean": ((order[:, None] == np.arange(NB * IH)) / TOPK).astype(np.float32),
    }


def ffn_layouts(i):
    B1 = i["L1_ffn_B1"].transpose(0, 2, 1).reshape(E1 * R1, F1)
    B2 = i["L1_ffn_B2"].transpose(0, 2, 1).reshape(E1 * R1, D)
    return {
        "f1_ra": np.concatenate([i["L1_ffn_W_r"].T, i["L1_ffn_A1"].reshape(E1 * R1, D).T], axis=1),
        "f1_w1": i["L1_ffn_W1"].T, "f1_b1": i["L1_ffn_b1"].reshape(FM, P).T, "f1_B1": np.concatenate([B1, B1]),
        "f1_A2": i["L1_ffn_A2"].reshape(E1 * R1, F1).T, "f1_w2": i["L1_ffn_W2"].T, "f1_B2": np.concatenate([B2, B2]),
        "L1_ffn_b2": i["L1_ffn_b2"], "L1_ffn_b_r": i["L1_ffn_b_r"],
        "iota8": np.arange(8, dtype=np.float32),
        "L2_ffn_gate_w": i["L2_ffn_gate_w"], "L2_ffn_b2": i["L2_ffn_b2"], "L2_ffn_shared_b2": i["L2_ffn_shared_b2"],
        "f2_w1": np.concatenate([i["L2_ffn_w1"].transpose(1, 0, 2).reshape(D, E2 * P), i["L2_ffn_shared_w1"]], axis=1),
        "f2_b1": np.concatenate([i["L2_ffn_b1"], i["L2_ffn_shared_b1"].reshape(SH // P, P)]).T,
        "f2_w2": np.concatenate([i["L2_ffn_w2"].reshape(E2 * P, D), i["L2_ffn_shared_w2"]]),
        "f3_w": i["L3_ffn_weight"].T, "f3_v": i["L3_ffn_rram_variation"].T,
    }


def linear_layouts(i):
    two, three = (lambda n: i["L2_attn_" + n]), (lambda n: i["L3_attn_" + n])
    head = np.arange(P) // LD
    return {
        "l2_w": np.concatenate([two(n).T for n in ("wq", "wk", "wv")], axis=1),
        "l2_b": np.concatenate([two(n) for n in ("bq", "bk", "bv")]),
        "l2_wo": two("wo").T, "L2_attn_bo": two("bo"),
        "l3_w": np.concatenate([three(n) for n in ("Wqk", "Wv", "Wu")], axis=1),
        "l3_b": np.concatenate([three(n) for n in ("bqk", "bv", "bu")]),
        "l3_wo": three("Wo"), "L3_attn_bo": three("bo"), "L3_attn_ln_g": three("ln_g"), "L3_attn_ln_b": three("ln_b"),
        "same_head": (head[:, None] == head).astype(np.float32),
        "head_of": (head[:, None] == np.arange(HPC)).astype(np.float32),
    }


def layouts(i):
    cos, sin = rope_tables()
    return {
        "L0_attn_x": i["L0_attn_x"],
        "L0_attn_q_kernel": i["L0_attn_q_kernel"], "L0_attn_k_kernel": i["L0_attn_k_kernel"],
        "L0_attn_v_kernel": i["L0_attn_v_kernel"], "L0_attn_out_kernel": i["L0_attn_out_kernel"],
        "l0_cos": cos, "l0_sin": sin,
        "L0_ffn_weight": i["L0_ffn_weight"], "L0_ffn_bias": i["L0_ffn_bias"],
        **l1_layouts(i), **ffn_layouts(i), **linear_layouts(i),
    }


def kernel(**inputs):
    import numpy as _np
    import concourse.bacc as _bacc
    from concourse import mybir as _mybir
    from concourse.bass_utils import run_bass_kernel_spmd as _run

    nc = _bacc.Bacc("TRN2", target_bir_lowering=False, num_devices=1)
    arrays, dram = {}, {}
    for name, a in layouts({k: _np.asarray(v) for k, v in inputs.items()}).items():
        arrays[f"in_{name}"] = a = _np.ascontiguousarray(a)
        dram[name] = nc.dram_tensor(f"in_{name}", a.shape, _mybir.dt.from_np(a.dtype), kind="ExternalInput").ap()
    out = nc.dram_tensor("out_0_dram", (NB, SEQ, D), F32, kind="ExternalOutput").ap()
    program(nc, dram, out)
    r = _run(nc, [arrays], core_ids=[0])
    return r.results[0]["out_0_dram"]
```
